# Optimizing a Trainium2 kernel written in Bass

```python
import numpy as np
import jax
import jax.numpy as jnp

def _softmax(x, axis=-1):
    return jax.nn.softmax(x, axis=axis)

def _gelu(x):
    return jax.nn.gelu(x, approximate=True)

def _silu(x):
    return jax.nn.silu(x)

def _sigmoid(x):
    return jax.nn.sigmoid(x)

def _layernorm(x, axis=-1, eps=1e-05):
    m = jnp.mean(x, axis=axis, keepdims=True)
    v = jnp.var(x, axis=axis, keepdims=True)
    return (x - m) / jnp.sqrt(v + eps)

def _scatter_add(tgt, idx, src, axis=0):
    return tgt.at[idx].add(src)

def _segment_sum(src, seg, n):
    return jax.ops.segment_sum(src, seg, n)
kernel_name = 'mk_gps_d1_gnn_r8_09e7db'

def setup_inputs(seed: int=0):
    np.random.seed(seed)
    _w = jnp.asarray

    def _rec_inputs():
        import jax
        import jax.numpy as jnp
        _gk = jax.random.key(seed)
        x = -0.0002117 + 1 * jax.random.normal(jax.random.fold_in(_gk, 1), (6250, 512), jnp.float32)
        src = jax.random.randint(jax.random.fold_in(_gk, 2), (100000,), 0, 6250, jnp.int32)
        dst = jnp.minimum((6250 * jax.random.uniform(jax.random.fold_in(_gk, 3), (100000,)) ** 2.0).astype(jnp.int32), 49999)
        _o = jnp.argsort(dst, stable=True)
        src = src[_o]
        dst = dst[_o]
        return (x, src, dst)
    x, src, dst = _rec_inputs()

    def _L0_gnn_setup():
        import jax, jax.numpy as jnp
        import numpy as np
        N = 6250
        E = 50000
        IN_FEATS = 512
        HEADS = 8
        OUT_FEATS = 64
        NEG_SLOPE = 0.2
        key = jax.random.key(seed)
        ks = jax.random.split(key, 12)
        HF = HEADS * OUT_FEATS
        s = 1.0 / np.sqrt(IN_FEATS)
        inp = {'feat': jax.random.normal(ks[0], (N, IN_FEATS), dtype=jnp.float32), 'src': jax.random.randint(ks[1], (E,), 0, N, dtype=jnp.int32), 'dst': jax.random.randint(ks[2], (E,), 0, N, dtype=jnp.int32), 'W_src': jax.random.normal(ks[3], (IN_FEATS, HF), dtype=jnp.float32) * s, 'b_src': jax.random.normal(ks[4], (HF,), dtype=jnp.float32) * 0.01, 'W_dst': jax.random.normal(ks[5], (IN_FEATS, HF), dtype=jnp.float32) * s, 'b_dst': jax.random.normal(ks[6], (HF,), dtype=jnp.float32) * 0.01, 'W_val': jax.random.normal(ks[7], (IN_FEATS, HF), dtype=jnp.float32) * s, 'b_val': jax.random.normal(ks[8], (HF,), dtype=jnp.float32) * 0.01, 'attn_l': jax.random.normal(ks[9], (HEADS, OUT_FEATS), dtype=jnp.float32) * 0.1, 'attn_r': jax.random.normal(ks[10], (HEADS, OUT_FEATS), dtype=jnp.float32) * 0.1}
        return inp
    _L0_gnn_all = _L0_gnn_setup()
    _L0_gnn_in = {k: v for k, v in _L0_gnn_all.items() if k in ('W_src', 'b_src', 'W_dst', 'b_dst', 'W_val', 'b_val', 'attn_l', 'attn_r')}
    del _L0_gnn_all

    def _L0_mix_setup():
        import jax, jax.numpy as jnp
        import numpy as np
        import math
        E = 512
        H = 8
        D = E // H
        M = 64
        EPS = 1e-08
        CLAMP_MAX = 50.0

        def _make_omega(key):
            w = jax.random.normal(key, (D, M), dtype=jnp.float32) / np.sqrt(D)
            q, _ = jnp.linalg.qr(w)
            return q

        def _positive_random_feature_map(v, omega):
            f = jnp.minimum(v @ omega, CLAMP_MAX)
            l2 = jnp.maximum(jnp.linalg.norm(v, axis=-1, keepdims=True), EPS)
            norm_term = jnp.maximum(jnp.exp(-0.5 * l2 * l2), EPS)
            return norm_term * jnp.exp(f)
        key = jax.random.key(seed)
        ks = jax.random.split(key, 8)
        B, S = (2, 2048)
        x = jax.random.normal(ks[0], (B, S, E), dtype=jnp.float32)
        sc = 1.0 / np.sqrt(E)
        Wq = jax.random.normal(ks[1], (E, E), dtype=jnp.float32) * sc
        Wk = jax.random.normal(ks[2], (E, E), dtype=jnp.float32) * sc
        Wv = jax.random.normal(ks[3], (E, E), dtype=jnp.float32) * sc
        Wo = jax.random.normal(ks[4], (E, E), dtype=jnp.float32) * sc
        omega_q = _make_omega(ks[5])
        omega_k = _make_omega(ks[6])
        return {'x': x, 'Wq': Wq, 'Wk': Wk, 'Wv': Wv, 'Wo': Wo, 'omega_q': omega_q, 'omega_k': omega_k}
    _L0_mix_all = _L0_mix_setup()
    _L0_mix_in = {k: v for k, v in _L0_mix_all.items() if k in ('Wq', 'Wk', 'Wv', 'Wo', 'omega_q', 'omega_k')}
    del _L0_mix_all

    def _L0_ffn_setup():
        import jax, jax.numpy as jnp
        import numpy as np
        SINKHORN_ITERS = 8
        TEMPERATURE = 1.0
        EPS = 1e-10

        def sinkhorn(gates):
            t = jnp.log(jnp.clip(gates, EPS)) / TEMPERATURE

            def body(t, _):
                t = t - jax.nn.logsumexp(t, axis=-2, keepdims=True)
                t = t - jax.nn.logsumexp(t, axis=-1, keepdims=True)
                return (t, None)
            t, _ = jax.lax.scan(body, t, None, length=SINKHORN_ITERS)
            return jnp.exp(t)
        key = jax.random.key(seed)
        k1, k2, k3 = jax.random.split(key, 3)
        b, n, d, e, h = (4, 1024, 512, 8, 1)
        x = jax.random.normal(k1, (b, n, d), dtype=jnp.float32)
        gate_w = jax.random.normal(k2, (h, d, e), dtype=jnp.float32)
        experts = jax.random.normal(k3, (e, d, d), dtype=jnp.float32) / np.sqrt(d)
        return {'x': x, 'gate_w': gate_w, 'experts': experts}
    _L0_ffn_all = _L0_ffn_setup()
    _L0_ffn_in = {k: v for k, v in _L0_ffn_all.items() if k in ('gate_w', 'experts')}
    del _L0_ffn_all
    return {'x': x, 'src': src, 'dst': dst, 'L0_gnn_W_src': _L0_gnn_in['W_src'], 'L0_gnn_b_src': _L0_gnn_in['b_src'], 'L0_gnn_W_dst': _L0_gnn_in['W_dst'], 'L0_gnn_b_dst': _L0_gnn_in['b_dst'], 'L0_gnn_W_val': _L0_gnn_in['W_val'], 'L0_gnn_b_val': _L0_gnn_in['b_val'], 'L0_gnn_attn_l': _L0_gnn_in['attn_l'], 'L0_gnn_attn_r': _L0_gnn_in['attn_r'], 'L0_mix_Wq': _L0_mix_in['Wq'], 'L0_mix_Wk': _L0_mix_in['Wk'], 'L0_mix_Wv': _L0_mix_in['Wv'], 'L0_mix_Wo': _L0_mix_in['Wo'], 'L0_mix_omega_q': _L0_mix_in['omega_q'], 'L0_mix_omega_k': _L0_mix_in['omega_k'], 'L0_ffn_gate_w': _L0_ffn_in['gate_w'], 'L0_ffn_experts': _L0_ffn_in['experts']}

def reference(x, src, dst, L0_gnn_W_src, L0_gnn_b_src, L0_gnn_W_dst, L0_gnn_b_dst, L0_gnn_W_val, L0_gnn_b_val, L0_gnn_attn_l, L0_gnn_attn_r, L0_mix_Wq, L0_mix_Wk, L0_mix_Wv, L0_mix_Wo, L0_mix_omega_q, L0_mix_omega_k, L0_ffn_gate_w, L0_ffn_experts):
    import jax
    import jax.numpy as jnp

    def _L0_gnn_ref(feat, src, dst, W_src, b_src, W_dst, b_dst, W_val, b_val, attn_l, attn_r):
        import jax, jax.numpy as jnp
        import numpy as np
        N = 6250
        E = 50000
        IN_FEATS = 512
        HEADS = 8
        OUT_FEATS = 64
        NEG_SLOPE = 0.2
        feat_src = (feat @ W_src + b_src).reshape(N, HEADS, OUT_FEATS)
        feat_dst = (feat @ W_dst + b_dst).reshape(N, HEADS, OUT_FEATS)
        feat_v = (feat @ W_val + b_val).reshape(N, HEADS, OUT_FEATS)
        el = jnp.einsum('nhf,hf->nh', feat_src, attn_l)
        er = jnp.einsum('nhf,hf->nh', feat_dst, attn_r)
        e = el[src] + er[dst]
        e = jnp.where(e >= 0, e, NEG_SLOPE * e)
        e_max = jax.ops.segment_max(e, dst, num_segments=N)
        e_max = jnp.where(jnp.isfinite(e_max), e_max, 0.0)
        exp_e = jnp.exp(e - e_max[dst])
        denom = jax.ops.segment_sum(exp_e, dst, num_segments=N)
        a = exp_e / jnp.maximum(denom[dst], 1e-16)
        msg = feat_v[src] * a[:, :, None]
        rst = jax.ops.segment_sum(msg, dst, num_segments=N)
        return rst.reshape(N, HEADS * OUT_FEATS)

    def _L0_mix_ref(x, Wq, Wk, Wv, Wo, omega_q, omega_k):
        import jax, jax.numpy as jnp
        import numpy as np
        import math
        E = 512
        H = 8
        D = E // H
        M = 64
        EPS = 1e-08
        CLAMP_MAX = 50.0

        def _make_omega(key):
            w = jax.random.normal(key, (D, M), dtype=jnp.float32) / np.sqrt(D)
            q, _ = jnp.linalg.qr(w)
            return q

        def _positive_random_feature_map(v, omega):
            f = jnp.minimum(v @ omega, CLAMP_MAX)
            l2 = jnp.maximum(jnp.linalg.norm(v, axis=-1, keepdims=True), EPS)
            norm_term = jnp.maximum(jnp.exp(-0.5 * l2 * l2), EPS)
            return norm_term * jnp.exp(f)
        B, S, _ = x.shape
        scale = 1.0 / np.sqrt(D)

        def heads(y):
            return y.reshape(B, S, H, D).transpose(0, 2, 1, 3)
        Q = heads(x @ Wq) * scale
        K = heads(x @ Wk) * scale
        V = heads(x @ Wv)
        Q_phi = _positive_random_feature_map(Q, omega_q)
        K_phi = _positive_random_feature_map(K, omega_k)
        KV = jnp.einsum('bhsm,bhsd->bhmd', K_phi, V)
        QKV = jnp.einsum('bhsm,bhmd->bhsd', Q_phi, KV)
        K_ones = K_phi.sum(axis=2)
        QK_ones = jnp.einsum('bhsm,bhm->bhs', Q_phi, K_ones)
        attn = QKV / QK_ones[..., None]
        out = attn.transpose(0, 2, 1, 3).reshape(B, S, E)
        return out @ Wo

    def _L0_ffn_ref(x, gate_w, experts):
        import jax, jax.numpy as jnp
        import numpy as np
        SINKHORN_ITERS = 8
        TEMPERATURE = 1.0
        EPS = 1e-10

        def sinkhorn(gates):
            t = jnp.log(jnp.clip(gates, EPS)) / TEMPERATURE

            def body(t, _):
                t = t - jax.nn.logsumexp(t, axis=-2, keepdims=True)
                t = t - jax.nn.logsumexp(t, axis=-1, keepdims=True)
                return (t, None)
            t, _ = jax.lax.scan(body, t, None, length=SINKHORN_ITERS)
            return jnp.exp(t)
        b, n, d = x.shape
        h = gate_w.shape[0]
        e = experts.shape[0]
        N = b * n
        m = n // e
        x4 = x[:, None]
        gates = jnp.einsum('bhnd,hde->bhne', x4, gate_w)
        xf = jnp.transpose(x4, (1, 0, 2, 3)).reshape(h, N, d)
        gf = jnp.transpose(gates, (1, 0, 2, 3)).reshape(h, N, e)
        cg = sinkhorn(gf)
        vals, idx = jax.lax.top_k(jnp.transpose(cg, (0, 2, 1)), m)
        gate_values = (vals > 0.5).astype(x.dtype)
        gate_values = jnp.transpose(gate_values, (0, 2, 1))
        idx = jnp.transpose(idx, (0, 2, 1))
        routed = xf[jnp.arange(h)[:, None, None], idx]
        outputs = jnp.einsum('hmei,eio->hmeo', routed, experts)
        outputs = outputs * gate_values[..., None]
        o_dim = outputs.shape[-1]
        src = outputs.reshape(h, m * e, o_dim)
        idx_flat = idx.reshape(h, m * e)

        def combine(idxf, srcf):
            s = jnp.zeros((N, o_dim), srcf.dtype).at[idxf].add(srcf)
            c = jnp.zeros((N,), srcf.dtype).at[idxf].add(1.0)
            return s / (c + 1.0)[:, None]
        out = jax.vmap(combine)(idx_flat, src)
        out = out.reshape(h, b, n, o_dim)
        out = jnp.transpose(out, (1, 0, 2, 3))[:, 0]
        return out
    xn = _layernorm(x, axis=-1)
    x = x + _L0_gnn_ref(xn, src, dst, L0_gnn_W_src, L0_gnn_b_src, L0_gnn_W_dst, L0_gnn_b_dst, L0_gnn_W_val, L0_gnn_b_val, L0_gnn_attn_l, L0_gnn_attn_r) + _L0_mix_ref(xn[None], L0_mix_Wq, L0_mix_Wk, L0_mix_Wv, L0_mix_Wo, L0_mix_omega_q, L0_mix_omega_k)[0]
    x = x + _L0_ffn_ref(_layernorm(x, axis=-1)[None], L0_ffn_gate_w, L0_ffn_experts)[0]
    return x

_drawn_inputs = setup_inputs


def setup_inputs(seed=0):
    import zlib

    import numpy as np

    out = dict(_drawn_inputs(seed))
    spreads = {}
    factors = {'L0_gnn_b_src': 23.677,
     'L0_gnn_b_dst': 18.95,
     'L0_mix_Wq': 8.0,
     'L0_mix_Wk': 4.925,
     'L0_mix_omega_q': 8.0,
     'L0_mix_omega_k': 8.0}
    for name, (base, spread) in spreads.items():
        noise = np.random.default_rng([zlib.crc32(name.encode()), seed]).standard_normal(out[name].shape)
        drawn = base * np.exp(spread * noise) if base else spread * noise
        out[name] = jnp.asarray(drawn.astype(out[name].dtype))
    for name, factor in factors.items():
        out[name] = (out[name] * factor).astype(out[name].dtype)
    return out
```

```python
import concourse.bass as bass
from concourse import mybir
from contextlib import ExitStack

FP32 = mybir.dt.float32
INT32 = mybir.dt.int32
ALU = mybir.AluOpType
ACT = mybir.ActivationFunctionType
AX = mybir.AxisListType

N, D = 6250, 512
E = 100000
H, F = 8, 64
P = 125
T = N // P
ET = E // P
KC = D // 128
GT = 2 * P
G = N // GT
C = H // 2
NCH = 16
CL = E // NCH
CT = CL // P
X = 8
CAP = N // X
SLOT = 112
XT = 7
XR = SLOT * XT
ROWS = X * XR
RING = 16
HR = 8
EPS_LN = 1e-5
EPS_PHI = 1e-8
FCLAMP = 50.0
FAR = -1.0e30
BITS = 30
SINK = 8
SCALE = F ** -0.5


class Steps:

    def __init__(self, eng, sem, passed=None):
        self.passed = passed
        self.eng, self.sem, self.base, self.n, self.i, self.per = eng, sem, 0, 0, 0, 0

    def loop(self, i, per):
        if self.per == 0:
            self.base += self.n
        self.n, self.i, self.per = 0, i, per

    def end(self, trips):
        assert self.n == self.per, (self.n, self.per)
        self.base, self.n, self.i, self.per = self.base + trips * self.per, 0, 0, 0

    def done(self, ins, apart=False):
        self.n += 1
        ins.then_inc(self.sem, 1)
        self.eng.wait_ge(self.sem, self.i * self.per + self.base + self.n)
        if apart:
            self.eng.sem_inc(self.passed, 1)


def trips(eng, n, trip):
    trip(0)
    with eng.Fori(1, n) as i:
        trip(i)


def rev(a):
    return a[:, ::-1]


def gps_layer(nc, x, srcT, dstT, dst, W_src, b_src, W_dst, b_dst, W_val, b_val, attn_l, attn_r,
              Wq, Wk, Wv, Wo, omega_q, omega_k, gate_w, experts, out):
    ctx = ExitStack()
    with ctx:
        def sb(name, shape, dt=FP32):
            return ctx.enter_context(nc.sbuf_tensor(name, shape, dt))

        def sem(name):
            return ctx.enter_context(nc.semaphore(name))

        def dram(name, shape):
            return nc.dram_tensor(name, shape, FP32, kind="Internal").ap()

        el_tab = dram("el_tab", (N, H))
        er_tab = dram("er_tab", (N, H))
        val_tab = dram("val_tab", (N, D))
        xm_tab = dram("xm_tab", (N, D))
        x1_tab = dram("x1_tab", (N, D))
        ends_tab = dram("ends_tab", (128, 4))
        xs_tab = dram("xs_tab", (ROWS, D))
        y_tab = dram("y_tab", (ROWS + 1, D))

        R1 = sb("R1", [128, 26024])
        R2 = sb("R2", [128, 16384])
        xnT_all = R1[:, 0:KC * N].rearrange("p (k n) -> p k n", k=KC)
        scan_d = R1[:, 0:CL]
        scan_e = R1[:, CL:2 * CL]
        scan_m = R1[:, 2 * CL:3 * CL]
        scan_p = R1[:, 3 * CL:4 * CL + 1]
        acc = R1[0:P, 0:T * D].rearrange("p (t n) -> p t n", t=T)
        accd = R1[0:P, T * D:T * D + T * H].rearrange("p (t h) -> p t h", t=T)
        EW = R2[0:P, 0:ET * H].rearrange("p (t h) -> p t h", h=H)
        WS = [R2[:, 6400 + 2048 * i:8448 + 2048 * i].rearrange("p (k n) -> p k n", k=KC) for i in range(4)]
        w_vg, w_k, w_v, w_q = WS
        w_o = WS[0]
        ring = R2[0:P, 6400:6400 + RING * D].rearrange("p (s n) -> p s n", s=RING)
        EL = R2[0:P, 8448:8448 + ET * H].rearrange("p (g c h) -> p g c h", c=NCH, h=H)
        exp_w = R2[:, 0:X * KC * D].rearrange("p (e k n) -> p e k n", e=X, k=KC)
        s_wsrc = R1[:, 0:2048].rearrange("p (k n) -> p k n", k=KC)
        s_wdst = R1[:, 2048:4096].rearrange("p (k n) -> p k n", k=KC)
        s_prod = R1[:, 4096:6144].rearrange("p (k n) -> p k n", k=KC)
        s_al = R1[:, 6144:6656]
        s_ar = R1[:, 6656:7168]
        s_bs = R1[:, 7168:7680]
        s_bd = R1[:, 7680:8192]

        src_i = sb("src_i", [P, ET], INT32)
        dst_i = sb("dst_i", [P, ET], INT32)
        negdst = sb("negdst", [P, ET])
        pidx = sb("pidx", [P, 2, 2, HR], INT32)
        vidx = sb("vidx", [P, RING], INT32)
        ident = sb("ident", [128, 128])
        ones = sb("ones", [128, 128])
        halves = sb("halves", [128, 128])
        before = sb("before", [128, 128])
        omk = sb("omk", [128, 128])
        omq = sb("omq", [128, 128])
        half2 = sb("half2", [128, 2])
        bval = R2[0:P, 15616:16128]
        welr = R2[:, 16128:16192].rearrange("p (k n) -> p k n", k=KC)
        belr = R2[0:P, 16192:16208]
        gw = sb("gw", [128, KC, X])
        eps = sb("eps", [128, 1])
        kvb = R1[:, 25000:25512].rearrange("p (c n) -> p c n", c=C)
        kob = R1[:, 25512:26024].rearrange("p (c n) -> p c n", c=C)
        kvacc = sb("kvacc", [128, 2, 258])
        hi_tab = sb("hi_tab", [1, T + 1], INT32)
        work = sb("work", [128, 6400])
        pring = work[:, 6072:6328][0:P, :].rearrange("p (a b n) -> p a b n", a=2, b=2)

        def wk(a, n):
            return work[:, a:a + n]

        x_in = wk(0, 1024).rearrange("p (j n) -> p j n", j=2)
        xn = wk(1024, 1024).rearrange("p (j n) -> p j n", j=2)
        elr_sb = wk(2048, 32).rearrange("p (j n) -> p j n", j=2)
        st6 = wk(2080, 12).rearrange("p (j n) -> p j n", j=2)
        mv = wk(2092, 4).rearrange("p (j n) -> p j n", j=2)
        std = wk(2096, 2)
        rstd = wk(2098, 2)
        xT1 = wk(4000, 1000).rearrange("p (k n) -> p k n", k=KC)
        xT = [wk(1000 * b, 1000).rearrange("p (k n) -> p k n", k=KC) for b in range(2)]
        ts = wk(2000, 1000)
        ts3 = ts.rearrange("p (k n) -> p k n", k=KC)
        ts2 = wk(3000, 1000)
        ts23 = ts2.rearrange("p (k n) -> p k n", k=KC)
        phi = wk(4000, 1024).rearrange("p (j n) -> p j n", j=2)
        vext = wk(5024, 1032).rearrange("p (j c n) -> p j c n", j=2, c=C)
        nk = wk(6056, 16).rearrange("p (j n) -> p j n", j=2)
        vout = R2[0:P, 14592:15616].rearrange("p (j n) -> p j n", j=2)
        rq = wk(2000, 1000)
        attnT = wk(3000, 1000)
        attnT3 = attnT.rearrange("p (k n) -> p k n", k=KC)
        xm = wk(0, 1024).rearrange("p (j n) -> p j n", j=2)
        cand = wk(0, 64).rearrange("p (k c) -> p k c", k=NCH)
        candv = wk(64, 32)
        ends = wk(96, 4)
        cfl = wk(100, 2)
        onehot = [wk(2112 + 128 * s, P) for s in range(2)]
        absd = [wk(2368 + 128 * s, P) for s in range(2)]
        iota_f = wk(2624, P)
        one125 = wk(2750, 1)
        zrow = wk(2752, D)
        thr = wk(3266, 1)
        cmp = wk(3272, ET // 2)
        cnt = wk(3674, 2)
        xmb = wk(0, 1024).rearrange("p (j n) -> p j n", j=2)
        xn2b = wk(1024, 1024).rearrange("p (j n) -> p j n", j=2)
        xT6 = wk(4000, 1000).rearrange("p (k j n) -> p k j n", k=KC, j=2)
        den = wk(5000, 16).rearrange("p (j n) -> p j n", j=2)
        gK, gA, gB, sel, win, pre, cnt_t, keep = [work[0:P, a_:a_ + T * X]
                                                  for a_ in (5100, 2600, 2200, 3000, 3400, 4000, 4400, 5500)]
        slot_s = sb("slot_s", [P, T], INT32)
        slot_g = sb("slot_g", [P, T], INT32)
        rcnt = sb("rcnt", [P, T])
        noff = sb("noff", [P, T])
        tb = [sb(f"tb{i}", [P, T]) for i in range(3)]
        sm = sb("sm", [P, 8, X])
        smi = sb("smi", [P, 4, X], INT32)
        xs = [R1[0:SLOT, D * s:D * (s + 1)] for s in range(2)]
        xsT = [R1[:, 1024 + 448 * s:1472 + 448 * s] for s in range(2)]
        ys = [R1[0:SLOT, 2048 + D * s:2560 + D * s] for s in range(2)]
        yg = [R1[0:P, 3072 + D * s:3584 + D * s] for s in range(2)]
        xf = [R1[0:P, 4096 + D * s:4608 + D * s] for s in range(2)]

        ps = ctx.enter_context(nc.psum_tensor("ps", [128, 8, 512], FP32))

        def two(b, rows=128):
            return ps[0:rows, b:b + 2, 0:500]

        def chunk(b, k, lo, n, rows=128):
            return ps[0:rows, b + k // 2, (k % 2) * GT + lo:(k % 2) * GT + lo + n]

        names = """elr_params omega_params xn_ready idx_loaded val_params proj_params consts_ready xnT_ready
            elr_written v_psum vg_read lq_psum wo_loaded xm_ready wo_psum attn_ready dst_loaded ends_ready
            ends_written segmax_ready xn2_ready sp_passed x1_ready block_summed experts_loaded scattered
            xs_transposed y_ready out_ready pool_step pool_passed elr_ready logits_added iota_ready zero_written
            zeros_ready seg_b_read tile_free slots_ready onehot_free acc_free welr_ready xn_transposed elr_psum
            fq_read kt_psum lq_read vg_psum v_copied fk_read fk_psum kt_copied qt_psum phi_ready kv_added
            kv_psum qt_copied fq_psum kvb_ready phiq_ready qkv_psum edge_logits seg_t_copied seg_t_psum
            seg_b_psum negdst_ready f_psum cmp_ready hi_psum hi_ready weights_ready msg_ready onehot_ready
            xT6_ready xn2_transposed gate_read gate_psum col_ready col_psum cnt_ready cnt_psum pre_ready
            pre_psum xsT_copied y_psum act_step var_ready std_ready kexp_done qexp_done xn2_kept dve_step
            dve_passed dve_misc""".split()
        S = {n: sem(n) for n in names}
        x_loaded = [sem(f"x_loaded{j}") for j in range(2)]
        xT_loaded = [sem(f"xT_loaded{b}") for b in range(2)]
        val_written = [sem(f"val_written{j}") for j in range(2)]
        xm_in = [sem(f"xm_in{j}") for j in range(2)]
        xm_out = [sem(f"xm_out{j}") for j in range(2)]
        logits_in = [sem(f"logits_in{h_}") for h_ in range(2)]
        gathered = [sem(f"gathered{s}") for s in range(RING)]
        xmb_loaded = [sem(f"xmb_loaded{j}") for j in range(2)]
        x1_out = [sem(f"x1_out{j}") for j in range(2)]
        xs_loaded = [sem(f"xs_loaded{s}") for s in range(2)]
        y_out = [sem(f"y_out{s}") for s in range(2)]
        yg_loaded = [sem(f"yg_loaded{s}") for s in range(2)]
        xf_loaded = [sem(f"xf_loaded{s}") for s in range(2)]
        out_done = [sem(f"out_done{s}") for s in range(2)]

        def rows(tab, t):
            return tab[bass.ds(t * P, P), :]

        block = ctx.enter_context(nc.Block())

        @block.sync
        def _(sp_):
            eng = sp_
            wv4 = "(k p) n -> p k n"
            eng.dma_start(s_wsrc, W_src.rearrange(wv4, p=128)).then_inc(S["elr_params"], 16)
            eng.dma_start(s_wdst, W_dst.rearrange(wv4, p=128)).then_inc(S["elr_params"], 16)
            for d_, a_ in ((s_al, attn_l.rearrange("h f -> (h f)")), (s_ar, attn_r.rearrange("h f -> (h f)")),
                           (s_bs, b_src), (s_bd, b_dst)):
                eng.dma_start(d_, a_.partition_broadcast(128)).then_inc(S["elr_params"], 16)
            with nc.allow_non_contiguous_dma(reason="small"):
                eng.dma_start(gw[:, :, :], gate_w.rearrange("o (k p) e -> p (o k) e", p=128)).then_inc(S["omega_params"], 16)
            def trip(g):
                eng.wait_ge(S["xn_ready"], 2 * g)
                for j in range(2):
                    eng.dma_start(x_in[0:P, j, :], rows(x, 2 * g + j)).then_inc(x_loaded[j], 16)

            trips(eng, G, trip)
            eng.dma_start(src_i[:, :], srcT).then_inc(S["idx_loaded"], 16)
            eng.dma_start(dst_i[:, :], dstT).then_inc(S["idx_loaded"], 16)
            eng.dma_start(bval[:, :], b_val.partition_broadcast(P)).then_inc(S["val_params"], 16)
            eng.dma_start(w_vg, W_val.rearrange(wv4, p=128)).then_inc(S["val_params"], 16)
            for w_, m_ in ((w_k, Wk), (w_v, Wv), (w_q, Wq)):
                eng.dma_start(w_, m_.rearrange(wv4, p=128)).then_inc(S["proj_params"], 16)
            eng.wait_ge(S["consts_ready"], 1)
            for o_, m_ in ((omk, omega_k), (omq, omega_q)):
                for r in range(2):
                    eng.dma_start(o_[F * r:F * r + F, F * r:F * r + F], m_).then_inc(S["omega_params"], 16)
            eng.wait_ge(S["xnT_ready"], 2 * G)
            eng.wait_ge(S["elr_written"], 32 * G)

            def load_xT(g, b, used):
                if used is not None:
                    eng.wait_ge(S["v_psum"], used)
                eng.dma_start(xT[b], xnT_all[:, :, bass.ds(g * GT, GT)]).then_inc(xT_loaded[b], 16)

            def store_val(g, b):
                for j in range(2):
                    eng.wait_ge(S["vg_read"], 2 * g + j + 1)
                    eng.dma_start(rows(val_tab, 2 * g + j), vout[:, j, :]).then_inc(val_written[j], 16)

            load_xT(0, 0, None)
            def trip(i):
                load_xT(2 * i + 1, 1, 4 * i)
                store_val(2 * i, 0)
                load_xT(2 * i + 2, 0, 4 * i + 2)
                store_val(2 * i + 1, 1)

            trips(eng, G // 2, trip)
            store_val(G - 1, 0)
            eng.wait_ge(S["lq_psum"], G)
            eng.dma_start(w_o, Wo.rearrange(wv4, p=128)).then_inc(S["wo_loaded"], 16)
            def trip(g):
                for j in range(2):
                    eng.wait_ge(xm_out[j], 16 * g)
                    eng.dma_start(xm[0:P, j, :], rows(x, 2 * g + j)).then_inc(xm_in[j], 16)
                for j in range(2):
                    eng.wait_ge(S["xm_ready"], 2 * g + j + 1)
                    eng.dma_start(rows(xm_tab, 2 * g + j), xm[0:P, j, :]).then_inc(xm_out[j], 16)

            trips(eng, G, trip)
            for j in range(2):
                eng.wait_ge(xm_out[j], 16 * G)
            eng.wait_ge(S["wo_psum"], 2 * G)
            eng.wait_ge(S["attn_ready"], G)
            for c in range(NCH):
                eng.dma_start(scan_m[H * c:H * c + H, :].bitcast(INT32), dst[c * CL:(c + 1) * CL].partition_broadcast(H)).then_inc(S["dst_loaded"], 16)
            eng.wait_ge(S["ends_ready"], 1)
            eng.dma_start(ends_tab, ends).then_inc(S["ends_written"], 16)
            eng.wait_ge(S["ends_written"], 16)
            with nc.allow_non_contiguous_dma(reason="ends of chunks"):
                for c in range(NCH):
                    eng.dma_start(cand[H * c:H * c + H, :, :], ends_tab.rearrange("(k h) c -> h k c", h=H)).then_inc(S["ends_written"], 16)
            eng.wait_ge(S["segmax_ready"], 1)
            def trip(i):
                eng.wait_ge(S["xn2_ready"], 2 * i)
                eng.sem_inc(S["sp_passed"], 1)
                for j in range(2):
                    eng.wait_ge(x1_out[j], 16 * i)
                    eng.dma_start(xmb[0:P, j, :], rows(xm_tab, 2 * i + j)).then_inc(xmb_loaded[j], 16)
                for j in range(2):
                    eng.wait_ge(S["x1_ready"], 2 * i + j + 1)
                    eng.dma_start(rows(x1_tab, 2 * i + j), xmb[0:P, j, :]).then_inc(x1_out[j], 16)

            trips(eng, T // 2, trip)
            eng.wait_ge(S["block_summed"], T)
            for e_ in range(X):
                eng.dma_start(exp_w[:, e_, :, :], experts[e_].rearrange(wv4, p=128)).then_inc(S["experts_loaded"], 16)
            eng.wait_ge(S["scattered"], 16 * T)

            def load_xs(n, s, used):
                if used is not None:
                    eng.wait_ge(S["xs_transposed"], used)
                eng.dma_start(xs[s], xs_tab[bass.ds(n * SLOT, SLOT), :]).then_inc(xs_loaded[s], 16)

            def store_y(n, s):
                eng.wait_ge(S["y_ready"], n + 1)
                eng.dma_start(y_tab[bass.ds(n * SLOT, SLOT), :], ys[s]).then_inc(y_out[s], 16)

            NT = X * XT
            load_xs(0, 0, None)
            def trip(i):
                load_xs(2 * i + 1, 1, 2 * i)
                store_y(2 * i, 0)
                load_xs(2 * i + 2, 0, 2 * i + 1)
                store_y(2 * i + 1, 1)

            trips(eng, NT // 2 - 1, trip)
            load_xs(NT - 1, 1, NT - 2)
            store_y(NT - 2, 0)
            store_y(NT - 1, 1)
            for j in range(2):
                eng.wait_ge(x1_out[j], 16 * (T // 2))
            def trip(i):
                for s in range(2):
                    eng.wait_ge(out_done[s], 16 * i)
                    eng.dma_start(xf[s], rows(x1_tab, 2 * i + s)).then_inc(xf_loaded[s], 16)
                for s in range(2):
                    eng.wait_ge(S["out_ready"], 2 * i + s + 1)
                    eng.dma_start(rows(out, 2 * i + s), xf[s]).then_inc(out_done[s], 16)

            trips(eng, T // 2, trip)
            for s in range(2):
                eng.wait_ge(out_done[s], 16 * (T // 2))

        @block.gpsimd
        def _(eng):
            st = Steps(eng, S["pool_step"], S["pool_passed"])
            for t_ in (omk, omq):
                st.done(eng.memset(t_[:, :], 0.0))
            eng.sem_inc(S["consts_ready"], 1)
            for t_ in (ident, halves, half2, before):
                st.done(eng.memset(t_[:, :], 0.0))
            for t_ in (kvb, kob, kvacc):
                st.done(eng.memset(t_[:, :, :], 0.0))
            st.done(eng.memset(eps[:, :], EPS_LN))
            st.done(eng.memset(ones[:, :], 1.0))
            st.done(eng.affine_select(out=ident[:, :], in_=ident[:, :], compare_op=ALU.not_equal, fill=1.0, base=0,
                                      pattern=[[-1, 128]], channel_multiplier=1))
            st.done(eng.affine_select(out=before[:, :], in_=before[:, :], compare_op=ALU.is_ge, fill=1.0, base=0,
                                      pattern=[[-1, 128]], channel_multiplier=1))
            for r in range(2):
                st.done(eng.memset(halves[F * r:F * r + F, F * r:F * r + F], 1.0))
                st.done(eng.memset(half2[F * r:F * r + F, r:r + 1], 1.0))
            eng.sem_inc(S["consts_ready"], 1)
            el_v = el_tab.rearrange("(t p) h -> p t h", p=P)
            er_v = er_tab.rearrange("(t p) h -> p t h", p=P)
            with nc.allow_non_contiguous_dma(reason="32-byte rows"):
                def trip(g):
                    eng.wait_ge(S["elr_ready"], g + 1)
                    eng.dma_start(el_v[:, bass.ds(2 * g, 2), :], elr_sb[0:P, :, 0:H]).then_inc(S["elr_written"], 16)
                    eng.dma_start(er_v[:, bass.ds(2 * g, 2), :], elr_sb[0:P, :, H:2 * H]).then_inc(S["elr_written"], 16)

                trips(eng, G, trip)
            eng.wait_ge(S["elr_written"], 32 * G)
            eng.wait_ge(S["idx_loaded"], 32)
            def gather_logits(first, h_):
                for tab_i, ix in ((src_i, 0), (dst_i, 1)):
                    st.done(eng.tensor_copy(pidx[:, h_, ix, :], tab_i[:, bass.ds(first, HR)]), apart=True)
                for q in range(HR):
                    for tab_, ix in ((el_tab, 0), (er_tab, 1)):
                        eng.indirect_dma_start(out=pring[:, h_, ix, q * H:q * H + H], out_offset=None, in_=tab_[:, :],
                                               in_offset=bass.IndirectOffsetOnAxis(ap=pidx[:, h_, ix, q:q + 1], axis=0))\
                            .then_inc(logits_in[h_], 16)

            def add_logits(first, h_):
                st.done(eng.tensor_tensor(out=EW[:, bass.ds(first, HR), :].rearrange("p t h -> p (t h)"), in0=pring[:, h_, 0, :],
                                          in1=pring[:, h_, 1, :], op=ALU.add))

            for h_ in range(2):
                gather_logits(h_ * HR, h_)
            st.n -= 6
            with eng.Fori(1, ET // (2 * HR)) as i:
                st.loop(i, 6)
                for h_ in range(2):
                    eng.wait_ge(logits_in[h_], 32 * HR * i)
                    add_logits(2 * HR * (i - 1) + h_ * HR, h_)
                    gather_logits(2 * HR * i + h_ * HR, h_)
            st.end(ET // (2 * HR))
            for h_ in range(2):
                eng.wait_ge(logits_in[h_], 32 * HR * (ET // (2 * HR)))
                add_logits(ET - 2 * HR + h_ * HR, h_)
            eng.sem_inc(S["logits_added"], 1)
            eng.wait_ge(S["xm_ready"], 2 * G)
            eng.wait_ge(S["wo_psum"], 2 * G)
            st.done(eng.iota(iota_f[0:P, :], pattern=[[1, P]], base=0, channel_multiplier=0, allow_small_or_imprecise_dtypes=True))
            st.done(eng.memset(one125[:, :], float(P)))
            st.done(eng.memset(zrow[:, :], 0.0))
            st.done(eng.iota(thr[:, :], pattern=[[0, 1]], base=P, channel_multiplier=P, allow_small_or_imprecise_dtypes=True))
            st.done(eng.iota(sm[:, 4, :], pattern=[[XR, X]], base=0, channel_multiplier=0, allow_small_or_imprecise_dtypes=True))
            st.done(eng.iota(noff[:, :], pattern=[[P, T]], base=ROWS, channel_multiplier=1, allow_small_or_imprecise_dtypes=True))
            eng.sem_inc(S["iota_ready"], 1)
            zb = zrow[0:P, :]
            def trip(t):
                eng.dma_start(rows(xs_tab, t), zb).then_inc(S["zero_written"], 16)

            trips(eng, T, trip)
            eng.dma_start(xs_tab[N:ROWS, :], zb[0:ROWS - N, :]).then_inc(S["zero_written"], 16)
            eng.dma_start(y_tab[ROWS:ROWS + 1, :], zb[0:1, :]).then_inc(S["zero_written"], 16)
            eng.wait_ge(S["zero_written"], 16 * (T + 2))
            eng.sem_inc(S["zeros_ready"], 1)
            for j in range(2):
                eng.wait_ge(val_written[j], 16 * G)
            eng.wait_ge(S["seg_b_read"], CT)
            with eng.Fori(0, ET // RING) as i:
                st.loop(i, RING // 4)
                for q in range(0, RING, 4):
                    eng.wait_ge(S["tile_free"], RING * i + q + 4)
                    st.done(eng.tensor_copy(vidx[:, q:q + 4], src_i[:, bass.ds(RING * i + q, 4)]), apart=True)
                    for s in range(q, q + 4):
                        eng.indirect_dma_start(out=ring[:, s, :], out_offset=None, in_=val_tab[:, :],
                                               in_offset=bass.IndirectOffsetOnAxis(ap=vidx[:, s:s + 1], axis=0))\
                            .then_inc(gathered[s], 16)
            st.end(ET // RING)
            eng.wait_ge(S["slots_ready"], 1)
            eng.wait_ge(S["xn2_kept"], T)
            for t in range(T):
                eng.indirect_dma_start(out=xs_tab[:, :], out_offset=bass.IndirectOffsetOnAxis(ap=slot_s[:, t:t + 1], axis=0),
                                       in_=acc[:, t, :], in_offset=None,
                                       bounds_check=ROWS - 1, oob_is_err=False).then_inc(S["scattered"], 16)
            NT = X * XT
            for s in range(2):
                eng.wait_ge(y_out[s], 16 * (NT // 2))
            for t in range(T):
                if t >= 2:
                    eng.wait_ge(S["out_ready"], t - 1)
                eng.indirect_dma_start(out=yg[t % 2], out_offset=None, in_=y_tab[:, :],
                                       in_offset=bass.IndirectOffsetOnAxis(ap=slot_g[:, t:t + 1], axis=0))\
                    .then_inc(yg_loaded[t % 2], 16)

        @block.tensor
        def _(pe):
            pe.sem_inc(S["tile_free"], RING)
            pe.sem_inc(S["onehot_free"], 2)
            pe.sem_inc(S["acc_free"], 2)

            def mm(o, l, r, start=True, stop=True):
                return pe.matmul(o, l, r, start=start, stop=stop)

            pe.wait_ge(S["consts_ready"], 2)
            pe.wait_ge(S["welr_ready"], 1)
            def trip(g):
                pe.wait_ge(S["xnT_ready"], 2 * g)
                for j in range(2):
                    pe.wait_ge(S["xn_ready"], 2 * g + j + 1)
                    for k in range(KC):
                        last = pe.transpose(chunk(0, k, j * P, P), xn[0:P, j, 128 * k:128 * k + 128], ident[0:P, 0:P])
                    last.then_inc(S["xn_transposed"], 1)
                pe.wait_ge(S["elr_ready"], g)
                pe.wait_ge(S["xnT_ready"], 2 * g + 2)
                for j in range(2):
                    for k in range(KC):
                        last = mm(ps[0:P, 2, 16 * j:16 * j + 16], xT1[:, k, j * P:j * P + P],
                                  welr[:, k, :], k == 0, k == KC - 1)
                last.then_inc(S["elr_psum"], 1)

            trips(pe, G, trip)
            pe.wait_ge(S["val_params"], 32)
            pe.wait_ge(S["proj_params"], 48)
            pe.wait_ge(S["omega_params"], 80)
            pe.wait_ge(S["elr_ready"], G)

            def group(g, b, u):
                pe.wait_ge(xT_loaded[b], 16 * (u + 1))
                pe.wait_ge(S["fq_read"], g)
                for c in range(C):
                    for k in range(KC):
                        last = mm(chunk(0, c, 0, GT), w_k[:, k, 128 * c:128 * c + 128], xT[b][:, k, :], k == 0, k == KC - 1)
                last.then_inc(S["kt_psum"], 1)
                pe.wait_ge(S["lq_read"], g)

                def values(j):
                    pe.wait_ge(S["vg_read"], 2 * g + j)
                    for k in range(KC):
                        last = mm(ps[0:P, 2, :], xT[b][:, k, j * P:j * P + P], w_vg[:, k, :], k == 0, k == KC - 1)
                    last.then_inc(S["vg_psum"], 1)
                    pe.wait_ge(S["v_copied"], 2 * g + j)
                    for k in range(KC):
                        last = mm(ps[0:P, 3, :], xT[b][:, k, j * P:j * P + P], w_v[:, k, :], k == 0, k == KC - 1)
                    last.then_inc(S["v_psum"], 1)

                def scores_k(j):
                    pe.wait_ge(S["fk_read"], 4 * g + 2 * j)
                    for c in range(C):
                        mm(ps[0:P, 4, 128 * c:128 * c + 128], ts3[:, c, j * P:j * P + P], omk[:, :])
                        last = mm(ps[0:P, 7, 2 * c:2 * c + 2], ts23[:, c, j * P:j * P + P], half2[:, :])
                    last.then_inc(S["fk_psum"], 1)

                values(0)
                pe.wait_ge(S["kt_copied"], 2 * g + 2)
                scores_k(0)
                scores_k(1)
                for c in range(C):
                    for k in range(KC):
                        last = mm(chunk(0, c, 0, GT), w_q[:, k, 128 * c:128 * c + 128], xT[b][:, k, :], k == 0, k == KC - 1)
                last.then_inc(S["qt_psum"], 1)
                values(1)
                pe.wait_ge(S["phi_ready"], 2 * g + 2)
                pe.wait_ge(S["v_copied"], 2 * g + 2)
                pe.wait_ge(S["kv_added"], g)
                for c in range(C):
                    for j in range(2):
                        last = mm(ps[:, 5 + c // 2, 129 * (c % 2):129 * (c % 2) + 129], phi[0:P, j, 128 * c:128 * c + 128],
                                  vext[0:P, j, c, :], j == 0, j == 1)
                last.then_inc(S["kv_psum"], 1)
                pe.wait_ge(S["qt_copied"], 2 * g + 2)
                for c in range(C):
                    last = mm(chunk(0, c, 0, GT), omq[:, :], ts3[:, c, :])
                last.then_inc(S["fq_psum"], 1)
                pe.wait_ge(S["vg_read"], 2 * g + 2)
                for c in range(C):
                    last = mm(chunk(2, c, 0, GT), halves[:, :], ts23[:, c, :])
                last.then_inc(S["lq_psum"], 1)
                

            def trip(i):
                group(2 * i, 0, i)
                group(2 * i + 1, 1, i)

            trips(pe, G // 2, trip)
            group(G - 1, 0, G // 2)
            pe.wait_ge(S["kvb_ready"], 8)
            pe.wait_ge(S["phiq_ready"], G)
            pe.wait_ge(S["wo_loaded"], 16)
            def trip(g):
                pe.wait_ge(S["attn_ready"], g)
                for c in range(C):
                    mm(chunk(0, c, 0, GT), kvb[:, c, :], xnT_all[:, c, bass.ds(g * GT, GT)])
                for c in range(C):
                    last = mm(chunk(2, c, 0, GT), kob[:, c, :], xnT_all[:, c, bass.ds(g * GT, GT)])
                last.then_inc(S["qkv_psum"], 1)
                pe.wait_ge(S["attn_ready"], g + 1)
                for j in range(2):
                    pe.wait_ge(S["xm_ready"], 2 * g)
                    for c in range(C):
                        last = mm(ps[0:P, 4 + j, :], attnT3[:, c, j * P:j * P + P], w_o[:, c, :], c == 0, c == C - 1)
                    last.then_inc(S["wo_psum"], 1)

            trips(pe, G, trip)
            pe.wait_ge(S["edge_logits"], NCH)
            for g in range(CT):
                if g >= 2:
                    pe.wait_ge(S["seg_t_copied"], g - 1)
                pe.transpose(ps[:, g % 2, 0:P], EL[:, g, :, :].rearrange("p c h -> p (c h)"), ident[0:P, 0:P]).then_inc(S["seg_t_psum"], 1)
            pe.wait_ge(S["segmax_ready"], 1)
            for g in range(CT):
                if g >= 2:
                    pe.wait_ge(S["seg_b_read"], g - 1)
                pe.transpose(ps[0:P, 2 + g % 2, 0:128], scan_e[:, g * P:g * P + P], ident[:, :]).then_inc(S["seg_b_psum"], 1)
            pe.wait_ge(S["negdst_ready"], 1)
            pe.wait_ge(S["iota_ready"], 1)
            mm(ps[0:T, 4, 0:ET // 2], ones[0:1, 0:T], negdst[0:1, :].rearrange("p (u s) -> p u s", s=2)[:, :, 0]).then_inc(S["f_psum"], 1)
            pe.wait_ge(S["cmp_ready"], 1)
            mm(ps[0:1, 5, 0:T], cnt[0:T, 1:2], ident[0:T, 0:T]).then_inc(S["hi_psum"], 1)
            pe.wait_ge(S["hi_ready"], 1)
            pe.wait_ge(S["weights_ready"], 1)
            with pe.Fori(0, T) as c:
                lo = pe.value_load(hi_tab[0:1, bass.ds(c, 1)], min_val=0, max_val=ET // 2 - 1)
                hi = pe.value_load(hi_tab[0:1, bass.ds(c + 1, 1)], min_val=0, max_val=ET // 2 - 1)
                a = c % 2
                pe.wait_ge(S["acc_free"], c + 1)
                o512 = ps[0:P, bass.ds(2 * a, 1), :].rearrange("p a n -> p (a n)")
                o8 = ps[0:P, bass.ds(2 * a + 1, 1), 0:H].rearrange("p a n -> p (a n)")
                mm(o512, zrow[0:1, 0:P], zrow[0:1, :], True, False)
                mm(o8, zrow[0:1, 0:P], zrow[0:1, 0:H], True, False)

                def tiles(u, lastone):
                    for s in range(2):
                        pe.wait_ge(S["msg_ready"], 2 * u + s + 1)
                        pe.wait_ge(S["onehot_ready"], 2 * (u + c) + s + 1)
                        stop = lastone and s == 1
                        m = mm(o512, onehot[s][0:P, :], ring[:, bass.ds((2 * u + s) % RING, 1), :].rearrange("p a n -> p (a n)"), False, stop)
                        if not lastone:
                            m.then_inc(S["tile_free"], 1)
                        mm(o8, onehot[s][0:P, :], EW[:, bass.ds(2 * u + s, 1), :].rearrange("p a n -> p (a n)"), False, stop)\
                            .then_inc(S["onehot_free"], 1)

                with pe.If(lo < hi):
                    with pe.Fori(lo, hi) as u:
                        tiles(u, False)
                tiles(hi, True)
            def trip(i):
                for j in range(2):
                    t = 2 * i + j
                    pe.wait_ge(S["xn2_ready"], t + 1)
                    pe.wait_ge(S["xT6_ready"], t)
                    for k in range(KC):
                        last = pe.transpose(ps[:, 4 + j, k * P:k * P + P], xn2b[0:P, j, 128 * k:128 * k + 128], ident[0:P, 0:P])
                    last.then_inc(S["xn2_transposed"], 1)
                    pe.wait_ge(S["xT6_ready"], t + 1)
                    pe.wait_ge(S["gate_read"], t)
                    for k in range(KC):
                        last = mm(ps[0:P, 6 + j, 0:X], xT6[:, k, j, :], gw[:, k, :], k == 0, k == KC - 1)
                    last.then_inc(S["gate_psum"], 1)

            trips(pe, T // 2, trip)
            def trip(i):
                pe.wait_ge(S["col_ready"], i + 1)
                mm(ps[0:P, 0, 0:X], ones[0:P, 0:P], sm[:, 0, :]).then_inc(S["col_psum"], 1)

            trips(pe, SINK, trip)
            def trip(i):
                pe.wait_ge(S["cnt_ready"], i + 1)
                mm(ps[0:P, 1, 0:X], ones[0:P, 0:P], sm[:, 1, :]).then_inc(S["cnt_psum"], 1)

            trips(pe, BITS + 1, trip)
            for r in range(2):
                pe.wait_ge(S["pre_ready"], r + 1)
                mm(ps[0:P, 2, 0:T * X], before[0:P, 0:P], win)
                mm(ps[0:P, 3, 0:T * X], ones[0:P, 0:P], win).then_inc(S["pre_psum"], 1)
            pe.wait_ge(S["experts_loaded"], 16 * X)

            def routed(n, s, e_):
                pe.wait_ge(xs_loaded[s], 16 * (n // 2 + 1))
                pe.wait_ge(S["xsT_copied"], n)
                for k in range(KC):
                    last = pe.transpose(ps[:, 4 + s, k * SLOT:k * SLOT + SLOT], xs[s][:, 128 * k:128 * k + 128], ident[0:SLOT, 0:SLOT])
                last.then_inc(S["xs_transposed"], 1)
                pe.wait_ge(S["xsT_copied"], n + 1)
                pe.wait_ge(S["y_ready"], n)
                for k in range(KC):
                    last = mm(ps[0:SLOT, 6 + s, :], xsT[s][:, k * SLOT:k * SLOT + SLOT],
                              exp_w[:, bass.ds(e_, 1), k, :].rearrange("p a n -> p (a n)"), k == 0, k == KC - 1)
                last.then_inc(S["y_psum"], 1)

            def trip(i):
                for m in range(2 * XT):
                    routed(i * 2 * XT + m, m % 2, 2 * i + m // XT)

            trips(pe, X // 2, trip)

        @block.scalar
        def _(act):
            st = Steps(act, S["act_step"])
            fn = act.activation
            act.wait_ge(S["consts_ready"], 2)
            def trip(g):
                for j in range(2):
                    act.wait_ge(S["var_ready"], 2 * g + j + 1)
                    fn(std[0:P, j:j + 1], mv[0:P, j, 1:2], ACT.Sqrt, bias=eps[0:P, :]).then_inc(S["std_ready"], 1)
                act.wait_ge(S["xn_transposed"], 2 * g + 2)
                act.wait_ge(S["elr_psum"], g)
                fn(xT1, two(0), ACT.Copy).then_inc(S["xnT_ready"], 1)
                fn(xnT_all[:, :, bass.ds(g * GT, GT)], ps[:, 0:2, 0:500].rearrange("p b (k n) -> p b k n", k=2), ACT.Copy)\
                    .then_inc(S["xnT_ready"], 1)

            trips(act, G, trip)
            act.wait_ge(S["elr_written"], 32 * G)

            def group(g):
                act.wait_ge(S["kt_psum"], g + 1)
                act.wait_ge(S["phiq_ready"], g)
                fn(ts, two(0), ACT.Copy, scale=SCALE).then_inc(S["kt_copied"], 1)
                fn(ts2, two(0), ACT.Square, scale=SCALE).then_inc(S["kt_copied"], 1)

                def v_copy(j):
                    act.wait_ge(S["v_psum"], 2 * g + j + 1)
                    act.wait_ge(S["kv_psum"], g)
                    fn(vext[0:P, j, :, 0:128], ps[0:P, 3, :].rearrange("p (c n) -> p c n", c=C), ACT.Copy).then_inc(S["v_copied"], 1)

                v_copy(0)
                for j in range(2):
                    act.wait_ge(S["fk_read"], 4 * g + 2 * j + 2)
                    fn(phi[0:P, j, :], phi[0:P, j, :], ACT.Exp).then_inc(S["kexp_done"], 1)
                    fn(nk[0:P, j, :], nk[0:P, j, :], ACT.Exp, scale=-0.5).then_inc(S["kexp_done"], 1)
                act.wait_ge(S["qt_psum"], g + 1)
                act.wait_ge(S["fk_psum"], 2 * g + 2)
                fn(ts, two(0), ACT.Copy, scale=SCALE).then_inc(S["qt_copied"], 1)
                fn(ts2, two(0), ACT.Square, scale=SCALE).then_inc(S["qt_copied"], 1)
                v_copy(1)
                act.wait_ge(S["fq_read"], g + 1)
                fn(ts, ts, ACT.Exp).then_inc(S["qexp_done"], 1)
                act.wait_ge(S["lq_read"], g + 1)
                fn(ts2, ts2, ACT.Exp, scale=-0.5).then_inc(S["qexp_done"], 1)

            def trip(g):
                group(g)

            trips(act, G, trip)
            for g in range(CT):
                act.wait_ge(S["seg_t_psum"], g + 1)
                fn(scan_e[:, g * P:g * P + P], ps[:, g % 2, 0:P], ACT.Copy).then_inc(S["seg_t_copied"], 1)
            act.wait_ge(S["seg_b_read"], CT)
            fn(EW, EW, ACT.Exp).then_inc(S["weights_ready"], 1)
            act.wait_ge(S["iota_ready"], 1)
            act.wait_ge(S["hi_ready"], 1)
            act.wait_ge(S["weights_ready"], 1)
            with act.Fori(0, T) as c:
                lo = act.value_load(hi_tab[0:1, bass.ds(c, 1)], min_val=0, max_val=ET // 2 - 1)
                hi = act.value_load(hi_tab[0:1, bass.ds(c + 1, 1)], min_val=0, max_val=ET // 2 - 1)
                with act.Fori(lo, hi + 1) as u:
                    for s in range(2):
                        k2 = 2 * (u + c) + s
                        fn(absd[s][0:P, :], iota_f[0:P, :], ACT.Abs, bias=negdst[:, bass.ds(2 * u + s, 1)]).then_inc(S["act_step"], 1)
                        act.wait_ge(S["act_step"], k2 + c + 1)
                        act.wait_ge(S["onehot_free"], k2 + 1)
                        fn(onehot[s][0:P, :], absd[s][0:P, :], ACT.Relu, scale=-1.0, bias=1.0).then_inc(S["onehot_ready"], 1)
                fn(iota_f[0:P, :], iota_f[0:P, :], ACT.Identity, bias=one125[0:P, :]).then_inc(S["act_step"], 1)
                act.wait_ge(S["act_step"], 2 * (hi + c) + 2 + c + 1)
                act.wait_ge(S["onehot_free"], 2 * (hi + c) + 2 + 2)
                a = c % 2
                fn(acc[:, bass.ds(c, 1), :].rearrange("p a n -> p (a n)"), ps[0:P, bass.ds(2 * a, 1), :].rearrange("p a n -> p (a n)"), ACT.Copy)\
                    .then_inc(S["block_summed"], 1)
                fn(accd[:, bass.ds(c, 1), :].rearrange("p a n -> p (a n)"), ps[0:P, bass.ds(2 * a + 1, 1), 0:H].rearrange("p a n -> p (a n)"), ACT.Copy)\
                    .then_inc(S["acc_free"], 1)
            def trip(i):
                for j in range(2):
                    t = 2 * i + j
                    act.wait_ge(S["var_ready"], T + t + 1)
                    fn(std[0:P, j:j + 1], mv[0:P, j, 1:2], ACT.Sqrt, bias=eps[0:P, :]).then_inc(S["std_ready"], 1)
                    act.wait_ge(S["xn2_transposed"], t + 1)
                    act.wait_ge(S["gate_psum"], t)
                    fn(xT6[:, :, j, :], ps[:, 4 + j, 0:500].rearrange("p (k n) -> p k n", k=KC), ACT.Copy).then_inc(S["xT6_ready"], 1)
                    act.wait_ge(S["xn2_ready"], t + 1)
                    fn(acc[:, bass.ds(t, 1), :].rearrange("p a n -> p (a n)"), xn2b[0:P, j, :], ACT.Copy).then_inc(S["xn2_kept"], 1)

            trips(act, T // 2, trip)
            def trip(i):
                for s in range(2):
                    n = 2 * i + s
                    act.wait_ge(S["xs_transposed"], n + 1)
                    act.wait_ge(S["y_psum"], n)
                    fn(xsT[s], ps[:, 4 + s, 0:KC * SLOT], ACT.Copy).then_inc(S["xsT_copied"], 1)

            trips(act, X * XT // 2, trip)

        @block.vector
        def _(v):
            st = Steps(v, S["dve_step"], S["dve_passed"])
            st.done(v.memset(vext[:, :, :, 128:129], 1.0))
            v.wait_ge(S["elr_params"], 96)
            for w_, a_, o_ in ((s_wsrc, s_al, 0), (s_wdst, s_ar, H)):
                st.done(v.tensor_tensor(out=s_prod, in0=w_, in1=a_.unsqueeze(1).to_broadcast([128, KC, D]), op=ALU.mult))
                st.done(v.tensor_reduce(out=welr[:, :, o_:o_ + H], in_=s_prod.rearrange("p k (h f) -> p k h f", h=H), axis=AX.X, op=ALU.add))
            for b_, a_, o_ in ((s_bs, s_al, 0), (s_bd, s_ar, H)):
                st.done(v.tensor_tensor(out=b_, in0=b_, in1=a_, op=ALU.mult))
                st.done(v.tensor_reduce(out=belr[:, o_:o_ + H], in_=b_[0:P, :].rearrange("p (h f) -> p h f", h=H), axis=AX.X, op=ALU.add))
            v.sem_inc(S["welr_ready"], 1)
            def trip(g):
                st.loop(g, 4)
                for j in range(2):
                    v.wait_ge(x_loaded[j], 16 * (g + 1))
                    st.done(v.bn_stats(out=st6[0:P, j, :], in_=x_in[0:P, j, :]), apart=True)
                    v.bn_aggr(out=mv[0:P, j, :], in_=st6[0:P, j, :]).then_inc(S["var_ready"], 1)
                for j in range(2):
                    v.wait_ge(S["std_ready"], 2 * g + j + 1)
                    st.done(v.reciprocal(rstd[0:P, j:j + 1], std[0:P, j:j + 1]))
                    v.wait_ge(S["xn_transposed"], 2 * g)
                    v.tensor_scalar(xn[0:P, j, :], x_in[0:P, j, :], mv[0:P, j, 0:1], rstd[0:P, j:j + 1], ALU.subtract, ALU.mult)\
                        .then_inc(S["xn_ready"], 1)
                v.wait_ge(S["elr_psum"], g + 1)
                v.wait_ge(S["elr_written"], 32 * g)
                v.tensor_tensor(out=elr_sb[0:P, :, :], in0=ps[0:P, 2, 0:32].rearrange("p (j n) -> p j n", j=2),
                                in1=belr[:, :].unsqueeze(1).to_broadcast([P, 2, 2 * H]), op=ALU.add).then_inc(S["elr_ready"], 1)

            trips(v, G, trip)
            st.end(G)
            v.wait_ge(S["elr_written"], 32 * G)
            v.wait_ge(S["val_params"], 32)
            v.wait_ge(S["consts_ready"], 2)

            def trip(g):
                st.loop(g, 3)

                def values(j):
                    v.wait_ge(S["vg_psum"], 2 * g + j + 1)
                    v.wait_ge(val_written[j], 16 * g)
                    v.tensor_tensor(out=vout[:, j, :], in0=ps[0:P, 2, :], in1=bval[:, :], op=ALU.add).then_inc(S["vg_read"], 1)

                values(0)
                for j in range(2):
                    v.wait_ge(S["fk_psum"], 2 * g + j + 1)
                    v.wait_ge(S["kv_psum"], g)
                    v.tensor_scalar(phi[0:P, j, :], ps[0:P, 4, :], FCLAMP, None, ALU.min).then_inc(S["fk_read"], 1)
                    v.tensor_scalar(nk[0:P, j, :], ps[0:P, 7, 0:H], EPS_PHI * EPS_PHI, None, ALU.max).then_inc(S["fk_read"], 1)
                for j in range(2):
                    v.wait_ge(S["kexp_done"], 4 * g + 2 * j + 2)
                    st.done(v.tensor_scalar(nk[0:P, j, :], nk[0:P, j, :], EPS_PHI, None, ALU.max))
                    p3 = phi[0:P, j, :].rearrange("p (h m) -> p h m", h=H)
                    v.tensor_tensor(out=p3, in0=p3, in1=nk[0:P, j, :].unsqueeze(2).to_broadcast([P, H, F]), op=ALU.mult)\
                        .then_inc(S["phi_ready"], 1)
                values(1)
                v.wait_ge(S["kv_psum"], g + 1)
                v.wait_ge(S["kv_added"], g)
                v.tensor_tensor(out=kvacc[:, :, :], in0=kvacc[:, :, :], in1=ps[:, 5:7, 0:258], op=ALU.add).then_inc(S["kv_added"], 1)
                v.wait_ge(S["fq_psum"], g + 1)
                v.tensor_scalar(ts, two(0), FCLAMP, None, ALU.min).then_inc(S["fq_read"], 1)
                v.wait_ge(S["lq_psum"], g + 1)
                v.tensor_scalar(ts2, two(2), EPS_PHI * EPS_PHI, None, ALU.max).then_inc(S["lq_read"], 1)
                v.wait_ge(S["qexp_done"], 2 * g + 2)
                st.done(v.tensor_scalar(ts2, ts2, EPS_PHI, None, ALU.max))
                v.tensor_tensor(out=xnT_all[:, :, bass.ds(g * GT, GT)], in0=ts3, in1=ts23, op=ALU.mult).then_inc(S["phiq_ready"], 1)

            trips(v, G, trip)
            st.end(G)
            v.wait_ge(S["kv_added"], G)
            kv4 = kvacc[:, :, :].rearrange("p b (q n) -> p (b q) n", n=129)
            for r in range(2):
                h_ = slice(F * r, F * r + F)
                for c in range(C):
                    v.tensor_copy(kob[h_, c, h_], kv4[h_, c, 128:129].to_broadcast([F, F])).then_inc(S["dve_misc"], 1)
                v.tensor_copy(kvb[h_, :, h_], kv4[h_, :, h_]).then_inc(S["kvb_ready"], 4)
            v.wait_ge(S["dve_misc"], 2 * C)
            def trip(g):
                st.loop(g, 1)
                v.wait_ge(S["qkv_psum"], g + 1)
                st.done(v.reciprocal(rq.rearrange("p (b n) -> p b n", b=2), two(2)))
                v.wait_ge(S["wo_psum"], 2 * g)
                v.tensor_tensor(out=attnT.rearrange("p (b n) -> p b n", b=2), in0=two(0), in1=rq.rearrange("p (b n) -> p b n", b=2), op=ALU.mult)\
                    .then_inc(S["attn_ready"], 1)
                for j in range(2):
                    v.wait_ge(S["wo_psum"], 2 * g + j + 1)
                    v.wait_ge(xm_in[j], 16 * (g + 1))
                    v.tensor_tensor(out=xm[0:P, j, :], in0=xm[0:P, j, :], in1=ps[0:P, 4 + j, :], op=ALU.add).then_inc(S["xm_ready"], 1)

            trips(v, G, trip)
            st.end(G)
            v.wait_ge(S["idx_loaded"], 32)
            st.done(v.tensor_scalar(negdst[:, :], dst_i[:, :], -1.0, None, ALU.mult))
            v.sem_inc(S["negdst_ready"], 1)
            v.wait_ge(S["dst_loaded"], 16 * NCH)
            st.done(v.tensor_copy(scan_d, scan_m.bitcast(INT32)))
            st.done(v.memset(scan_p[:, 0:1], FAR))
            st.done(v.memset(scan_p[:, CL:CL + 1], FAR))
            st.done(v.tensor_tensor(out=scan_p[:, 1:CL], in0=scan_d[:, 1:CL], in1=scan_d[:, 0:CL - 1], op=ALU.not_equal))
            st.done(v.tensor_scalar(scan_p[:, 1:CL], scan_p[:, 1:CL], FAR, None, ALU.mult))
            v.wait_ge(S["logits_added"], 1)
            for c in range(NCH):
                e_ = EW[:, c * CT:(c + 1) * CT, :]
                v.scalar_tensor_tensor(out=EL[:, :, c, :], in0=e_, scalar=0.2, in1=e_, op0=ALU.mult, op1=ALU.max)\
                    .then_inc(S["edge_logits"], 1)
            v.wait_ge(S["seg_t_copied"], CT)
            st.done(v.tensor_tensor_scan(out=scan_m, data0=scan_p[:, 0:CL], data1=scan_e, initial=FAR, op0=ALU.add, op1=ALU.max))
            st.done(v.tensor_tensor_scan(out=rev(scan_e), data0=rev(scan_p[:, 1:CL + 1]), data1=rev(scan_m), initial=FAR, op0=ALU.add, op1=ALU.max))
            for c_, s_ in ((0, scan_d[:, 0:1]), (1, scan_e[:, 0:1]), (2, scan_d[:, CL - 1:CL]), (3, scan_m[:, CL - 1:CL])):
                st.done(v.tensor_copy(ends[:, c_:c_ + 1], s_))
            v.sem_inc(S["ends_ready"], 1)
            v.wait_ge(S["ends_written"], 16 * (NCH + 1))
            cd = cand.rearrange("p k (a b) -> p (k a) b", b=2)
            for side, edge in ((0, scan_d[:, 0:1]), (1, scan_d[:, CL - 1:CL])):
                st.done(v.tensor_scalar(candv, cd[:, :, 0], edge, FAR, ALU.not_equal, ALU.mult))
                st.done(v.tensor_tensor(out=candv, in0=candv, in1=cd[:, :, 1], op=ALU.add))
                st.done(v.tensor_reduce(out=cfl[:, side:side + 1], in_=candv, axis=AX.X, op=ALU.max))
                st.done(v.tensor_scalar(scan_m, scan_d, edge, FAR, ALU.not_equal, ALU.mult))
                st.done(v.scalar_tensor_tensor(out=scan_e, in0=scan_m, scalar=cfl[:, side:side + 1], in1=scan_e, op0=ALU.add, op1=ALU.max))
            v.sem_inc(S["segmax_ready"], 1)
            v.wait_ge(S["edge_logits"], NCH)
            ew_v = EW.rearrange("p (c g) h -> p g c h", c=NCH)
            for g in range(CT):
                v.wait_ge(S["seg_b_psum"], g + 1)
                v.tensor_tensor(out=ew_v[:, g, :, :], in0=EL[:, g, :, :], in1=ps[0:P, 2 + g % 2, 0:128].rearrange("p (c h) -> p c h", h=H),
                                op=ALU.subtract).then_inc(S["seg_b_read"], 1)
            v.wait_ge(S["f_psum"], 1)
            v.wait_ge(S["iota_ready"], 1)
            st.done(v.tensor_scalar(cmp[0:T, :], ps[0:T, 4, 0:ET // 2], thr[0:T, :], 0.0, ALU.add, ALU.is_gt))
            st.done(v.tensor_reduce(out=cnt[0:T, 0:1], in_=cmp[0:T, :], axis=AX.X, op=ALU.add))
            st.done(v.tensor_scalar(cnt[0:T, 1:2], cnt[0:T, 0:1], -1.0, 0.0, ALU.add, ALU.max))
            v.sem_inc(S["cmp_ready"], 1)
            v.wait_ge(S["hi_psum"], 1)
            st.done(v.memset(hi_tab[0:1, 0:1], 0))
            st.done(v.tensor_copy(hi_tab[0:1, 1:T + 1], ps[0:1, 5, 0:T]))
            v.sem_inc(S["hi_ready"], 1)
            v.wait_ge(S["weights_ready"], 1)
            with v.Fori(0, ET // RING) as i:
                for s in range(RING):
                    v.wait_ge(gathered[s], 16 * (i + 1))
                    r3 = ring[:, s, :].rearrange("p (h f) -> p h f", h=H)
                    w_ = EW[:, bass.ds(RING * i + s, 1), :].rearrange("p a h -> p (a h)").unsqueeze(2).to_broadcast([P, H, F])
                    v.tensor_tensor(out=r3, in0=r3, in1=w_, op=ALU.mult).then_inc(S["msg_ready"], 1)
            v.wait_ge(S["zeros_ready"], 1)
            def trip(i):
                st.loop(i, 10)
                for j in range(2):
                    t = 2 * i + j
                    v.wait_ge(S["acc_free"], t + 3)
                    v.wait_ge(S["block_summed"], t + 1)
                    v.wait_ge(xmb_loaded[j], 16 * (i + 1))
                    a1 = acc[:, bass.ds(t, 1), :].rearrange("p a n -> p (a n)")
                    st.done(v.tensor_scalar(den[0:P, j, :], accd[:, bass.ds(t, 1), :].rearrange("p a n -> p (a n)"), 1e-16, None, ALU.max))
                    st.done(v.reciprocal(den[0:P, j, :], den[0:P, j, :]))
                    a3 = a1.rearrange("p (h f) -> p h f", h=H)
                    st.done(v.tensor_tensor(out=a3, in0=a3, in1=den[0:P, j, :].unsqueeze(2).to_broadcast([P, H, F]), op=ALU.mult))
                    v.tensor_tensor(out=xmb[0:P, j, :], in0=xmb[0:P, j, :], in1=a1, op=ALU.add).then_inc(S["x1_ready"], 1)
                    v.wait_ge(S["x1_ready"], t + 1)
                    st.done(v.bn_stats(out=st6[0:P, j, :], in_=xmb[0:P, j, :]), apart=True)
                    v.bn_aggr(out=mv[0:P, j, :], in_=st6[0:P, j, :]).then_inc(S["var_ready"], 1)
                for j in range(2):
                    t = 2 * i + j
                    v.wait_ge(S["std_ready"], N // P + t + 1)
                    st.done(v.reciprocal(rstd[0:P, j:j + 1], std[0:P, j:j + 1]))
                    v.wait_ge(S["xn2_transposed"], 2 * i)
                    v.wait_ge(S["xn2_kept"], 2 * i)
                    v.tensor_scalar(xn2b[0:P, j, :], xmb[0:P, j, :], mv[0:P, j, 0:1], rstd[0:P, j:j + 1], ALU.subtract, ALU.mult)\
                        .then_inc(S["xn2_ready"], 1)
                for j in range(2):
                    t = 2 * i + j
                    v.wait_ge(S["gate_psum"], t + 1)
                    v.tensor_scalar(gK[:, bass.ds(t * X, X)], ps[0:P, 6 + j, 0:X], 1e-10, None, ALU.max).then_inc(S["gate_read"], 1)

            trips(v, T // 2, trip)
            st.end(T // 2)
            def te(a_):
                return a_.rearrange("p (t e) -> p t e", e=X)

            def et(a_):
                return a_.rearrange("p (t e) -> p e t", e=X)

            def over_t(a_):
                return a_.unsqueeze(1).to_broadcast([P, T, X])

            def over_e(a_):
                return a_.unsqueeze(2).to_broadcast([P, T, X])

            sa, sr, lose = tb[0], tb[1], tb[2]
            v.wait_ge(S["gate_read"], T)
            st.done(v.memset(sa[:, :], 1.0))
            def trip(i):
                st.loop(i, 6)
                st.done(v.tensor_tensor(out=te(gB), in0=te(gK), in1=over_e(sa[:, :]), op=ALU.mult))
                st.done(v.tensor_reduce(out=sm[:, 0, :], in_=et(gB), axis=AX.X, op=ALU.add))
                v.sem_inc(S["col_ready"], 1)
                v.wait_ge(S["col_psum"], i + 1)
                st.done(v.reciprocal(sm[:, 2, :], ps[0:P, 0, 0:X]))
                st.done(v.tensor_tensor(out=te(gB), in0=te(gK), in1=over_t(sm[:, 2, :]), op=ALU.mult))
                st.done(v.tensor_reduce(out=sr[:, :], in_=te(gB), axis=AX.X, op=ALU.add))
                st.done(v.reciprocal(sa[:, :], sr[:, :]))

            trips(v, SINK, trip)
            st.end(SINK)
            st.done(v.tensor_tensor(out=te(gA), in0=te(gB), in1=over_e(sa[:, :]), op=ALU.mult))
            cur, bit, trial, hit = [smi[:, q, :] for q in range(4)]
            st.done(v.memset(cur, 0))
            st.done(v.memset(bit, 1 << (BITS - 1)))
            def trip(i):
                st.loop(i, 6)
                st.done(v.tensor_tensor(out=trial, in0=cur, in1=bit, op=ALU.bitwise_or))
                st.done(v.tensor_tensor(out=te(sel), in0=te(gA), in1=over_t(trial.bitcast(FP32)), op=ALU.is_ge))
                st.done(v.tensor_reduce(out=sm[:, 1, :], in_=et(sel), axis=AX.X, op=ALU.add))
                v.sem_inc(S["cnt_ready"], 1)
                v.wait_ge(S["cnt_psum"], i + 1)
                st.done(v.scalar_tensor_tensor(out=hit, in0=ps[0:P, 1, 0:X], scalar=float(CAP), in1=bit, op0=ALU.is_ge, op1=ALU.mult))
                st.done(v.tensor_tensor(out=cur, in0=cur, in1=hit, op=ALU.bitwise_or))
                st.done(v.tensor_scalar(bit, bit, 0.5, None, ALU.mult))

            trips(v, BITS, trip)
            st.end(BITS)
            cf = over_t(cur.bitcast(FP32))
            st.done(v.tensor_tensor(out=te(sel), in0=te(gA), in1=cf, op=ALU.is_gt))
            st.done(v.tensor_tensor(out=te(win), in0=te(gA), in1=cf, op=ALU.is_equal))
            st.done(v.tensor_reduce(out=sm[:, 1, :], in_=et(sel), axis=AX.X, op=ALU.add))
            v.sem_inc(S["cnt_ready"], 1)
            v.wait_ge(S["cnt_psum"], BITS + 1)
            st.done(v.tensor_scalar(sm[:, 3, :], ps[0:P, 1, 0:X], -1.0, float(CAP), ALU.mult, ALU.add))
            keep3 = keep.rearrange("p (e t) -> p e t", e=X)
            st.done(v.memset(keep, 1.0))
            st.done(v.memset(keep3[:, :, 0:1], 0.0))

            def rank(r):
                v.sem_inc(S["pre_ready"], 1)
                v.wait_ge(S["pre_psum"], r + 1)
                ct3 = cnt_t.rearrange("p (e t) -> p e t", e=X)
                st.done(v.tensor_copy(ct3, et(ps[0:P, 3, 0:T * X])))
                st.done(v.tensor_tensor_scan(out=gB, data0=keep, data1=cnt_t, initial=0.0, op0=ALU.mult, op1=ALU.add))
                st.done(v.tensor_tensor(out=gB, in0=gB, in1=cnt_t, op=ALU.subtract))
                st.done(v.tensor_tensor(out=te(pre), in0=te(ps[0:P, 2, 0:T * X]), in1=gB.rearrange("p (e t) -> p t e", e=X), op=ALU.add))

            rank(0)
            st.done(v.tensor_tensor(out=te(pre), in0=te(pre), in1=over_t(sm[:, 3, :]), op=ALU.is_lt))
            st.done(v.tensor_tensor(out=pre, in0=pre, in1=win, op=ALU.mult))
            st.done(v.tensor_tensor(out=sel, in0=sel, in1=pre, op=ALU.add))
            st.done(v.tensor_reduce(out=rcnt[:, :], in_=te(sel), axis=AX.X, op=ALU.add))
            st.done(v.tensor_scalar(rcnt[:, :], rcnt[:, :], 1.0, None, ALU.add))
            st.done(v.reciprocal(rcnt[:, :], rcnt[:, :]))
            st.done(v.scalar_tensor_tensor(out=win, in0=gA, scalar=0.5, in1=sel, op0=ALU.is_gt, op1=ALU.mult))
            st.done(v.tensor_reduce(out=sr[:, :], in_=te(win), axis=AX.X, op=ALU.add))
            st.done(v.tensor_scalar(sa[:, :], sr[:, :], 1.5, None, ALU.is_lt))
            st.done(v.tensor_tensor(out=te(win), in0=te(win), in1=over_e(sa[:, :]), op=ALU.mult))
            st.done(v.tensor_tensor(out=sr[:, :], in0=sr[:, :], in1=sa[:, :], op=ALU.mult))
            st.done(v.tensor_scalar(lose[:, :], sr[:, :], -1.0, 1.0, ALU.mult, ALU.add))
            rank(1)
            st.done(v.tensor_tensor(out=te(pre), in0=te(pre), in1=over_t(sm[:, 4, :]), op=ALU.add))
            st.done(v.tensor_tensor(out=pre, in0=pre, in1=win, op=ALU.mult))
            st.done(v.tensor_reduce(out=sr[:, :], in_=te(pre), axis=AX.X, op=ALU.add))
            st.done(v.tensor_tensor(out=noff[:, :], in0=noff[:, :], in1=lose[:, :], op=ALU.mult))
            st.done(v.tensor_tensor(out=slot_s[:, :], in0=noff[:, :], in1=sr[:, :], op=ALU.add))
            st.done(v.scalar_tensor_tensor(out=slot_g[:, :], in0=lose[:, :], scalar=float(ROWS), in1=sr[:, :], op0=ALU.mult, op1=ALU.add))
            v.sem_inc(S["slots_ready"], 1)
            def trip(i):
                for s in range(2):
                    n = 2 * i + s
                    v.wait_ge(S["y_psum"], n + 1)
                    v.wait_ge(y_out[s], 16 * i)
                    v.tensor_copy(ys[s], ps[0:SLOT, 6 + s, :]).then_inc(S["y_ready"], 1)

            trips(v, X * XT // 2, trip)
            def trip(i):
                for s in range(2):
                    v.wait_ge(yg_loaded[s], 16 * (i + 1))
                    v.wait_ge(xf_loaded[s], 16 * (i + 1))
                    v.scalar_tensor_tensor(out=xf[s], in0=yg[s], scalar=rcnt[:, bass.ds(2 * i + s, 1)], in1=xf[s], op0=ALU.mult, op1=ALU.add)\
                        .then_inc(S["out_ready"], 1)

            trips(v, T // 2, trip)


_INS = ["x", "srcT", "dstT", "dst", "L0_gnn_W_src", "L0_gnn_b_src", "L0_gnn_W_dst", "L0_gnn_b_dst", "L0_gnn_W_val", "L0_gnn_b_val",
        "L0_gnn_attn_l", "L0_gnn_attn_r", "L0_mix_Wq", "L0_mix_Wk", "L0_mix_Wv", "L0_mix_Wo", "L0_mix_omega_q", "L0_mix_omega_k",
        "L0_ffn_gate_w", "L0_ffn_experts"]


def kernel(**inputs):
    import numpy as _np
    import concourse.bacc as _bacc
    from concourse import mybir as _mybir
    from concourse.bass_utils import run_bass_kernel_spmd as _run

    nc = _bacc.Bacc("TRN2", target_bir_lowering=False, num_devices=1)
    arrays, args = {}, []
    laid = dict(inputs)
    for name in ("src", "dst"):
        laid[name + "T"] = _np.ascontiguousarray(_np.asarray(inputs[name]).reshape(ET, P).T)
    for name in _INS:
        a = _np.ascontiguousarray(laid[name])
        arrays[f"in_{name}_dram"] = a
        args.append(nc.dram_tensor(f"in_{name}_dram", a.shape, _mybir.dt.from_np(a.dtype), kind="ExternalInput").ap())
    args.append(nc.dram_tensor("out_0_dram", (N, D), _mybir.dt.float32, kind="ExternalOutput").ap())
    gps_layer(nc, *args)
    r = _run(nc, [arrays], core_ids=[0])
    return r.results[0]["out_0_dram"]
```

```python
import concourse.bass as bass
from concourse import mybir
from contextlib import ExitStack

FP32 = mybir.dt.float32
INT32 = mybir.dt.int32
BF16 = mybir.dt.bfloat16
ALU = mybir.AluOpType
ACT = mybir.ActivationFunctionType
AX = mybir.AxisListType

N, D = 6250, 512
E = 100000
H, F = 8, 64
P = 125
T = N // P
ET = E // P
KC = D // 128
GT = 2 * P
G = N // GT
C = H // 2
NCH = 16
CL = E // NCH
CT = CL // P
X = 8
CAP = N // X
SLOT = 112
XT = 7
XR = SLOT * XT
ROWS = X * XR
RING = 16
NF = 5
HR = 10
TOPS = 25
MIDS = ET // TOPS
TB = 4
NB = -(-CT // TB)
EPS_LN = 1e-5
EPS_PHI = 1e-8
FCLAMP = 50.0
FAR = -1.0e30
BITS = 30
SINK = 8
SCALE = F ** -0.5


class Steps:

    def __init__(self, eng, sem, passed=None):
        self.passed = passed
        self.eng, self.sem, self.base, self.n, self.i, self.per = eng, sem, 0, 0, 0, 0

    def loop(self, i, per):
        if self.per == 0:
            self.base += self.n
        self.n, self.i, self.per = 0, i, per

    def end(self, trips):
        assert self.n == self.per, (self.n, self.per)
        self.base, self.n, self.i, self.per = self.base + trips * self.per, 0, 0, 0

    def done(self, ins, apart=False):
        self.n += 1
        ins.then_inc(self.sem, 1)
        self.eng.wait_ge(self.sem, self.i * self.per + self.base + self.n)
        if apart:
            self.eng.sem_inc(self.passed, 1)


def trips(eng, n, trip):
    trip(0)
    with eng.Fori(1, n) as i:
        trip(i)


def staggered(eng, step, steps=None):
    for c in range(3):
        step(c, True)
    if steps:
        steps.n -= 15
    with eng.Fori(3, T) as c:
        step(c, True)
    if steps:
        steps.end(T)
    for c in range(T, T + 3):
        step(c, False)


def rev(a):
    return a[:, ::-1]


def gps_layer(nc, x, srcT, dstT, dst, W_src, b_src, W_dst, b_dst, W_val, b_val, attn_l, attn_r,
              Wq, Wk, Wv, Wo, omega_q, omega_k, gate_w, experts, out):
    ctx = ExitStack()
    with ctx:
        def sb(name, shape, dt=FP32):
            return ctx.enter_context(nc.sbuf_tensor(name, shape, dt))

        def sem(name):
            return ctx.enter_context(nc.semaphore(name))

        def dram(name, shape):
            return nc.dram_tensor(name, shape, FP32, kind="Internal").ap()

        el_tab = dram("el_tab", (N, H))
        er_tab = dram("er_tab", (N, H))
        val_tab = dram("val_tab", (N, D))
        xm_tab = dram("xm_tab", (N, D))
        x1_tab = dram("x1_tab", (N, D))
        er_starts = dram("er_starts", (E, H))
        start_tab = dram("start_tab", (P, T))
        ends_tab = dram("ends_tab", (128, 4))
        xs_tab = dram("xs_tab", (ROWS, D))
        y_tab = dram("y_tab", (ROWS + 1, D))

        R1 = sb("R1", [128, 26024])
        R2 = sb("R2", [128, 16384])
        xnT_all = R1[:, 0:KC * N].rearrange("p (k n) -> p k n", k=KC)
        scan_d = R1[:, 0:CL]
        scan_e = R1[:, CL:2 * CL]
        scan_m = R1[:, 2 * CL:3 * CL]
        scan_p = R1[:, 3 * CL:4 * CL + 1]
        acc = R1[0:P, 0:T * D].rearrange("p (t n) -> p t n", t=T)
        accd = R1[0:P, T * D:T * D + T * H].rearrange("p (t h) -> p t h", t=T)
        EW = R2[0:P, 0:ET * H].rearrange("p (t h) -> p t h", h=H)
        WS = [R2[:, 6400 + 2048 * i:8448 + 2048 * i].rearrange("p (k n) -> p k n", k=KC) for i in range(4)]
        w_vg, w_k, w_v, w_q = WS
        w_o = WS[0]
        ring = R2[0:P, 6400:6400 + RING * D].rearrange("p (s n) -> p s n", s=RING)
        ELP = R2[0:P, 0:ET * H].rearrange("p (g c h) -> p g c h", c=NCH, h=H)
        ert = R2[0:P, 8448:8448 + ET * H].rearrange("p (g c h) -> p g c h", c=NCH, h=H)
        scan_x = R2[:, 8448:8448 + CL]
        tops = R2[0:P, 14592:14592 + ET].bitcast(INT32)
        cthr = R2[0:P, 15400:15415]
        look = R2[0:P, 0:ET * H]
        exp_w = R2[:, 0:X * KC * D].rearrange("p (e k n) -> p e k n", e=X, k=KC)
        s_wsrc = R1[:, 0:2048].rearrange("p (k n) -> p k n", k=KC)
        s_wdst = R1[:, 2048:4096].rearrange("p (k n) -> p k n", k=KC)
        s_prod = R1[:, 4096:6144].rearrange("p (k n) -> p k n", k=KC)
        s_al = R1[:, 6144:6656]
        s_ar = R1[:, 6656:7168]
        s_bs = R1[:, 7168:7680]
        s_bd = R1[:, 7680:8192]

        src_i = sb("src_i", [P, ET], INT32)
        dst_i = sb("dst_i", [P, ET], INT32)
        negdst = sb("negdst", [P, ET])
        pidx = sb("pidx", [P, 2, HR], INT32)
        vidx = sb("vidx", [P, RING], INT32)
        ident = sb("ident", [128, 128])
        ones = sb("ones", [128, 128])
        halves = sb("halves", [128, 128])
        before = sb("before", [128, 128])
        omk = sb("omk", [128, 128])
        omq = sb("omq", [128, 128])
        half2 = sb("half2", [128, 2])
        bval = R2[0:P, 15616:16128]
        welr = R2[:, 16128:16192].rearrange("p (k n) -> p k n", k=KC)
        belr = R2[0:P, 16192:16208]
        gw = sb("gw", [128, KC, X])
        eps = sb("eps", [128, 1])
        kvb = R1[:, 25000:25512].rearrange("p (c n) -> p c n", c=C)
        kob = R1[:, 25512:26024].rearrange("p (c n) -> p c n", c=C)
        kvacc = sb("kvacc", [128, 2, 258])
        hi_tab = sb("hi_tab", [1, T + 1], INT32)
        work = sb("work", [128, 6400])
        pring = work[0:P, 6072:6072 + 2 * HR * H].rearrange("p (a n) -> p a n", a=2)

        def wk(a, n):
            return work[:, a:a + n]

        x_in = [wk(1024 * b, 1024).rearrange("p (j n) -> p j n", j=2) for b in range(2)]
        xn = [wk(2048 + 1024 * b, 1024).rearrange("p (j n) -> p j n", j=2) for b in range(2)]
        elr_sb = wk(4096, 32).rearrange("p (j n) -> p j n", j=2)
        st6 = wk(4128, 12).rearrange("p (j n) -> p j n", j=2)
        mv = wk(4140, 4).rearrange("p (j n) -> p j n", j=2)
        std = wk(4144, 2)
        rstd = wk(4146, 2)
        xT1 = [wk(4200 + 1000 * b, 1000) for b in range(2)]
        xT13 = [a_.rearrange("p (k n) -> p k n", k=KC) for a_ in xT1]
        xT = [wk(1000 * b, 1000).rearrange("p (k n) -> p k n", k=KC) for b in range(2)]
        ts = wk(2000, 1000)
        ts3 = ts.rearrange("p (k n) -> p k n", k=KC)
        ts2 = wk(3000, 1000)
        ts23 = ts2.rearrange("p (k n) -> p k n", k=KC)
        phi = wk(4000, 1024).rearrange("p (j n) -> p j n", j=2)
        vext = wk(5024, 1032).rearrange("p (j c n) -> p j c n", j=2, c=C)
        nk = wk(6056, 16).rearrange("p (j n) -> p j n", j=2)
        vout = R2[0:P, 14592:15616].rearrange("p (j n) -> p j n", j=2)
        rq = wk(2000, 1000)
        attnT = wk(3000, 1000)
        attnT3 = attnT.rearrange("p (k n) -> p k n", k=KC)
        xm = wk(0, 1024).rearrange("p (j n) -> p j n", j=2)
        cand = wk(0, 64).rearrange("p (k c) -> p k c", k=NCH)
        candv = wk(64, 32)
        ends = wk(96, 4)
        cfl = wk(100, 2)
        onehot = [wk(2112 + 128 * s, P) for s in range(2)]
        absd = [wk(2368 + 128 * s, P) for s in range(2)]
        iota_f = wk(2624, P)
        one125 = wk(2750, 1)
        zrow = wk(2752, D)
        thr = wk(3266, 1)
        cmp = wk(3272, ET // 2)
        cnt = wk(3674, 2)
        xmb = wk(0, 1024).rearrange("p (j n) -> p j n", j=2)
        xn2b = wk(1024, D)
        den = wk(4150, H)
        xT6 = wk(4200, 500)
        xT63 = xT6.rearrange("p (k n) -> p k n", k=KC)
        gK, gA, gB, sel, win, pre, cnt_t, keep = [work[0:P, a_:a_ + T * X]
                                                  for a_ in (5100, 2600, 2200, 3000, 3400, 4000, 4400, 5500)]
        slot_s = sb("slot_s", [P, T], INT32)
        slot_g = sb("slot_g", [P, T], INT32)
        rcnt = sb("rcnt", [P, T])
        noff = sb("noff", [P, T])
        tb = [sb(f"tb{i}", [P, T]) for i in range(3)]
        sm = sb("sm", [P, 8, X])
        smi = sb("smi", [P, 4, X], INT32)
        xs = [R1[0:SLOT, D * s:D * (s + 1)] for s in range(2)]
        xsT = [R1[:, 1024 + 448 * s:1472 + 448 * s] for s in range(2)]
        ys = [R1[0:SLOT, 2048 + D * s:2560 + D * s] for s in range(2)]
        yg = [R1[0:P, 3072 + D * s:3584 + D * s] for s in range(NF)]
        xf = [R1[0:P, 3072 + D * (NF + s):3584 + D * (NF + s)] for s in range(NF)]

        ps = ctx.enter_context(nc.psum_tensor("ps", [128, 8, 512], FP32))

        def two(b, rows=128):
            return ps[0:rows, b:b + 2, 0:500]

        def chunk(b, k, lo, n, rows=128):
            return ps[0:rows, b + k // 2, (k % 2) * GT + lo:(k % 2) * GT + lo + n]

        names = """elr_params omega_params xn_ready xnT_ready elr_ready elr_written idx_loaded val_params proj_params
            consts_ready row_ready er_back elr_psum v_psum vg_read lq_psum wo_loaded er_started ert_loaded
            xm_ready wo_psum attn_ready dst_loaded ends_ready ends_written segmax_ready sp_passed xm_back
            x1_ready x1_kept xn2_ready block_summed experts_loaded scattered xs_transposed y_ready out_ready
            pool_step pool_passed tops_loaded node_ready looked_up starts_moved chunk_er logits_kept iota_ready
            zero_written weights_kept tile_free vals_ready slots_ready xn2_kept onehot_free acc_free welr_ready
            xn_transposed v_ones fq_read kt_psum lq_read vg_psum v_copied fk_read fk_psum kt_copied qt_psum
            phi_ready kv_added kv_psum qt_copied fq_psum kvb_ready phiq_ready qkv_psum seg_t_psum negdst_ready
            f_psum cmp_ready hi_psum weights_ready weights_psum hi_ready msg_ready onehot_ready xT6_ready
            gate_read gate_psum xn2_transposed col_ready col_psum cnt_ready cnt_psum pre_ready pre_psum
            xsT_copied y_psum act_step var_ready std_ready kexp_done qexp_done el_t_copied dst_read er_t_copied
            shifted dve_step dve_passed dve_misc""".split()
        S = {n: sem(n) for n in names}
        x_loaded = [sem(f"x_loaded{b}") for b in range(2)]
        xT_kept = [sem(f"xT_kept{b}") for b in range(2)]
        xT_loaded = [sem(f"xT_loaded{b}") for b in range(2)]
        val_written = [sem(f"val_written{j}") for j in range(2)]
        xm_in = [sem(f"xm_in{j}") for j in range(2)]
        xm_out = [sem(f"xm_out{j}") for j in range(2)]
        logits_in = [sem(f"logits_in{h_}") for h_ in range(2)]
        gathered = [sem(f"gathered{q}") for q in range(4)]
        xs_loaded = [sem(f"xs_loaded{s}") for s in range(2)]
        y_out = [sem(f"y_out{s}") for s in range(2)]
        yg_loaded = [sem(f"yg_loaded{s}") for s in range(NF)]
        xf_loaded = [sem(f"xf_loaded{s}") for s in range(NF)]
        out_done = [sem(f"out_done{s}") for s in range(NF)]

        def rows(tab, t):
            return tab[bass.ds(t * P, P), :]

        block = ctx.enter_context(nc.Block())

        @block.sync
        def _(sp_):
            eng = sp_
            wv4 = "(k p) n -> p k n"
            eng.dma_start(s_wsrc, W_src.rearrange(wv4, p=128)).then_inc(S["elr_params"], 16)
            eng.dma_start(s_wdst, W_dst.rearrange(wv4, p=128)).then_inc(S["elr_params"], 16)
            for d_, a_ in ((s_al, attn_l.rearrange("h f -> (h f)")), (s_ar, attn_r.rearrange("h f -> (h f)")),
                           (s_bs, b_src), (s_bd, b_dst)):
                eng.dma_start(d_, a_.partition_broadcast(128)).then_inc(S["elr_params"], 16)
            with nc.allow_non_contiguous_dma(reason="small"):
                eng.dma_start(gw[:, :, :], gate_w.rearrange("o (k p) e -> p (o k) e", p=128)).then_inc(S["omega_params"], 16)
            def load_x(g, b, used):
                if used is not None:
                    eng.wait_ge(S["xn_ready"], used)
                for j in range(2):
                    eng.dma_start(x_in[b][0:P, j, :], rows(x, 2 * g + j)).then_inc(x_loaded[b], 16)

            def keep_xT(g, b):
                eng.wait_ge(S["xnT_ready"], g + 1)
                eng.dma_start(xnT_all[:, :, bass.ds(g * GT, GT)], xT13[b]).then_inc(xT_kept[b], 16)

            el_v = el_tab.rearrange("(t p) h -> p t h", p=P)
            er_v = er_tab.rearrange("(t p) h -> p t h", p=P)

            def store_logits(g):
                eng.wait_ge(S["elr_ready"], g + 1)
                eng.dma_start(el_v[:, bass.ds(2 * g, 2), :], elr_sb[0:P, :, 0:H]).then_inc(S["elr_written"], 16)
                eng.dma_start(er_v[:, bass.ds(2 * g, 2), :], elr_sb[0:P, :, H:2 * H]).then_inc(S["elr_written"], 16)

            load_x(0, 0, None)

            def trip(i):
                load_x(2 * i + 1, 1, 4 * i)
                keep_xT(2 * i, 0)
                if not isinstance(i, int):
                    store_logits(2 * i - 1)
                load_x(2 * i + 2, 0, 4 * i + 2)
                keep_xT(2 * i + 1, 1)
                store_logits(2 * i)

            trip(0)
            eng.dma_start(src_i[:, :], srcT).then_inc(S["idx_loaded"], 16)
            eng.dma_start(dst_i[:, :], dstT).then_inc(S["idx_loaded"], 16)
            eng.dma_start(bval[:, :], b_val.partition_broadcast(P)).then_inc(S["val_params"], 16)
            eng.dma_start(w_vg, W_val.rearrange(wv4, p=128)).then_inc(S["val_params"], 16)
            for w_, m_ in ((w_k, Wk), (w_v, Wv), (w_q, Wq)):
                eng.dma_start(w_, m_.rearrange(wv4, p=128)).then_inc(S["proj_params"], 16)
            eng.wait_ge(S["consts_ready"], 1)
            for o_, m_ in ((omk, omega_k), (omq, omega_q)):
                for r in range(2):
                    eng.dma_start(o_[F * r:F * r + F, F * r:F * r + F], m_).then_inc(S["omega_params"], 16)
            with nc.allow_non_contiguous_dma(reason="32-byte rows"):
                with eng.Fori(1, G // 2) as i:
                    trip(i)
                keep_xT(G - 1, 0)
                store_logits(G - 2)
                store_logits(G - 1)
                eng.wait_ge(S["elr_written"], 32 * G)
                eng.wait_ge(S["row_ready"], 4)
                eng.dma_start(look[:, 0:T * H].rearrange("p (t h) -> p t h", h=H), er_v).then_inc(S["er_back"], 16)
                eng.dma_start(smi[0:NCH, 0, 0:1], dst.rearrange("(c r) -> c r", c=NCH)[:, 0:1]).then_inc(S["er_back"], 16)
            for b in range(2):
                eng.wait_ge(xT_kept[b], 16 * (G // 2 + 1 - b))
            eng.wait_ge(S["elr_psum"], G)
            eng.wait_ge(S["elr_written"], 32 * G)

            def load_xT(g, b, used):
                if used is not None:
                    eng.wait_ge(S["v_psum"], used)
                eng.dma_start(xT[b], xnT_all[:, :, bass.ds(g * GT, GT)]).then_inc(xT_loaded[b], 16)

            def store_val(g, b):
                for j in range(2):
                    eng.wait_ge(S["vg_read"], 2 * g + j + 1)
                    eng.dma_start(rows(val_tab, 2 * g + j), vout[:, j, :]).then_inc(val_written[j], 16)

            load_xT(0, 0, None)
            def trip(i):
                load_xT(2 * i + 1, 1, 4 * i)
                store_val(2 * i, 0)
                load_xT(2 * i + 2, 0, 4 * i + 2)
                store_val(2 * i + 1, 1)

            trips(eng, G // 2, trip)
            store_val(G - 1, 0)
            eng.wait_ge(S["lq_psum"], G)
            eng.dma_start(w_o, Wo.rearrange(wv4, p=128)).then_inc(S["wo_loaded"], 16)
            for j in range(2):
                eng.wait_ge(val_written[j], 16 * G)
            eng.wait_ge(S["er_started"], 16 * (T + 1))
            eng.dma_start(R2[0:P, 8448:8448 + ET * H], er_starts.rearrange("(p r) h -> p (r h)", p=P)).then_inc(S["ert_loaded"], 16)
            def trip(g):
                for j in range(2):
                    eng.wait_ge(xm_out[j], 16 * g)
                    eng.dma_start(xm[0:P, j, :], rows(x, 2 * g + j)).then_inc(xm_in[j], 16)
                for j in range(2):
                    eng.wait_ge(S["xm_ready"], 2 * g + j + 1)
                    eng.dma_start(rows(xm_tab, 2 * g + j), xm[0:P, j, :]).then_inc(xm_out[j], 16)

            trips(eng, G, trip)
            for j in range(2):
                eng.wait_ge(xm_out[j], 16 * G)
            eng.wait_ge(S["wo_psum"], 2 * G)
            eng.wait_ge(S["attn_ready"], G)
            for c in range(NCH):
                eng.dma_start(scan_m[H * c:H * c + H, :].bitcast(INT32), dst[c * CL:(c + 1) * CL].partition_broadcast(H)).then_inc(S["dst_loaded"], 16)
            eng.wait_ge(S["ends_ready"], 1)
            eng.dma_start(ends_tab, ends).then_inc(S["ends_written"], 16)
            eng.wait_ge(S["ends_written"], 16)
            with nc.allow_non_contiguous_dma(reason="ends of chunks"):
                for c in range(NCH):
                    eng.dma_start(cand[H * c:H * c + H, :, :], ends_tab.rearrange("(k h) c -> h k c", h=H)).then_inc(S["ends_written"], 16)
            eng.wait_ge(S["segmax_ready"], 1)

            def hold(sem_, value):
                eng.wait_ge(sem_, value)
                eng.sem_inc(S["sp_passed"], 1)

            def load_xm(t):
                hold(S["xm_back"], 16 * t)
                eng.dma_start(xmb[0:P, bass.ds(t % 2, 1), :].rearrange("p a n -> p (a n)"), rows(xm_tab, t)).then_inc(S["xm_back"], 16)

            def store_x1(t):
                hold(S["x1_ready"], t + 1)
                hold(S["x1_kept"], 16 * t)
                eng.dma_start(rows(x1_tab, t), xmb[0:P, bass.ds(t % 2, 1), :].rearrange("p a n -> p (a n)")).then_inc(S["x1_kept"], 16)

            load_xm(0)
            load_xm(1)
            store_x1(0)
            with eng.Fori(2, T) as t:
                hold(S["x1_kept"], 16 * (t - 1))
                hold(S["xn2_ready"], t - 1)
                load_xm(t)
                store_x1(t - 1)
            store_x1(T - 1)
            eng.wait_ge(S["block_summed"], T)
            for e_ in range(X):
                eng.dma_start(exp_w[:, e_, :, :], experts[e_].rearrange(wv4, p=128)).then_inc(S["experts_loaded"], 16)
            eng.wait_ge(S["scattered"], 16 * T)

            def load_xs(n, s, used):
                if used is not None:
                    eng.wait_ge(S["xs_transposed"], used)
                eng.dma_start(xs[s], xs_tab[bass.ds(n * SLOT, SLOT), :]).then_inc(xs_loaded[s], 16)

            def store_y(n, s):
                eng.wait_ge(S["y_ready"], n + 1)
                eng.dma_start(y_tab[bass.ds(n * SLOT, SLOT), :], ys[s]).then_inc(y_out[s], 16)

            NT = X * XT
            load_xs(0, 0, None)
            def trip(i):
                load_xs(2 * i + 1, 1, 2 * i)
                store_y(2 * i, 0)
                load_xs(2 * i + 2, 0, 2 * i + 1)
                store_y(2 * i + 1, 1)

            trips(eng, NT // 2 - 1, trip)
            load_xs(NT - 1, 1, NT - 2)
            store_y(NT - 2, 0)
            store_y(NT - 1, 1)
            eng.wait_ge(S["x1_kept"], 16 * T)
            def trip(i):
                for s in range(NF):
                    eng.wait_ge(out_done[s], 16 * i)
                    eng.dma_start(xf[s], rows(x1_tab, NF * i + s)).then_inc(xf_loaded[s], 16)
                for s in range(NF):
                    eng.wait_ge(S["out_ready"], NF * i + s + 1)
                    eng.dma_start(rows(out, NF * i + s), xf[s]).then_inc(out_done[s], 16)

            trips(eng, T // NF, trip)
            for s in range(NF):
                eng.wait_ge(out_done[s], 16 * (T // NF))

        @block.gpsimd
        def _(eng):
            st = Steps(eng, S["pool_step"], S["pool_passed"])
            for t_ in (omk, omq):
                st.done(eng.memset(t_[:, :], 0.0))
            eng.sem_inc(S["consts_ready"], 1)
            for t_ in (ident, halves, half2, before):
                st.done(eng.memset(t_[:, :], 0.0))
            for t_ in (kvb, kob, kvacc):
                st.done(eng.memset(t_[:, :, :], 0.0))
            st.done(eng.memset(eps[:, :], EPS_LN))
            st.done(eng.memset(ones[:, :], 1.0))
            st.done(eng.affine_select(out=ident[:, :], in_=ident[:, :], compare_op=ALU.not_equal, fill=1.0, base=0,
                                      pattern=[[-1, 128]], channel_multiplier=1))
            st.done(eng.affine_select(out=before[:, :], in_=before[:, :], compare_op=ALU.is_ge, fill=1.0, base=0,
                                      pattern=[[-1, 128]], channel_multiplier=1))
            for r in range(2):
                st.done(eng.memset(halves[F * r:F * r + F, F * r:F * r + F], 1.0))
                st.done(eng.memset(half2[F * r:F * r + F, r:r + 1], 1.0))
            eng.sem_inc(S["consts_ready"], 1)
            node, start, nxt = noff[:, :], tb[0][:, :], tb[1][:, :]
            eng.dma_start(tops, dstT[0, :].partition_broadcast(P)).then_inc(S["tops_loaded"], 16)
            st.done(eng.memset(look, 0.0))
            eng.dma_start(er_starts.rearrange("(p r) h -> p (r h)", p=P), look).then_inc(S["tops_loaded"], 16)
            st.done(eng.iota(node, pattern=[[P, T]], base=0, channel_multiplier=1, allow_small_or_imprecise_dtypes=True))
            st.done(eng.memset(nxt, float(E)))
            st.done(eng.iota(cthr, pattern=[[CL, NCH - 1]], base=CL, channel_multiplier=0, allow_small_or_imprecise_dtypes=True))
            eng.sem_inc(S["node_ready"], 1)
            for n, tab_ in enumerate((dstT[0:1, :].rearrange("o (a b) -> (o a) b", b=MIDS), dst.rearrange("(a b) -> a b", b=P))):
                w_ = tab_.shape[1]
                eng.wait_ge(S["row_ready"], n + 1)
                for t in range(T):
                    eng.indirect_dma_start(out=look[:, w_ * t:w_ * t + w_].bitcast(INT32), out_offset=None, in_=tab_,
                                           in_offset=bass.IndirectOffsetOnAxis(ap=slot_g[:, t:t + 1], axis=0)).then_inc(S["looked_up"], 16)
            eng.wait_ge(S["row_ready"], 3)
            eng.dma_start(start_tab, start).then_inc(S["starts_moved"], 16)
            eng.wait_ge(S["starts_moved"], 16)
            eng.dma_start(nxt[0:P - 1, :], start_tab[1:P, :]).then_inc(S["starts_moved"], 16)
            eng.dma_start(nxt[P - 1:P, 0:T - 1], start_tab[0:1, 1:T]).then_inc(S["starts_moved"], 16)
            eng.wait_ge(S["row_ready"], 4)
            eng.wait_ge(S["er_back"], 32)
            eng.indirect_dma_start(out=sm[0:NCH, 0, :], out_offset=None, in_=er_tab[:, :],
                                   in_offset=bass.IndirectOffsetOnAxis(ap=smi[0:NCH, 0, 0:1], axis=0)).then_inc(S["chunk_er"], 16)
            for t in range(T):
                eng.indirect_dma_start(out=er_starts[:, :], out_offset=bass.IndirectOffsetOnAxis(ap=slot_s[:, t:t + 1], axis=0),
                                       in_=look[:, t * H:t * H + H], in_offset=None,
                                       bounds_check=E - 1, oob_is_err=False).then_inc(S["er_started"], 16)
            eng.wait_ge(S["chunk_er"], 16)
            eng.wait_ge(S["er_started"], 16 * T)
            eng.dma_start(er_starts[0:NCH, :], sm[0:NCH, 0, :]).then_inc(S["er_started"], 16)
            eng.wait_ge(S["idx_loaded"], 32)
            for b in range(2):
                eng.wait_ge(xT_kept[b], 16 * (G // 2 + 1 - b))
            BC = CT // HR

            def gather_logits(i, b):
                h_ = b % 2
                st.done(eng.tensor_copy(pidx[:, h_, :], src_i[:, bass.ds((2 * BC * i + b) * HR, HR)]), apart=True)
                for q in range(HR):
                    eng.indirect_dma_start(out=pring[:, h_, q * H:q * H + H], out_offset=None, in_=el_tab[:, :],
                                           in_offset=bass.IndirectOffsetOnAxis(ap=pidx[:, h_, q:q + 1], axis=0))\
                        .then_inc(logits_in[h_], 16)

            def keep_logits(i, b):
                g0 = (b % BC) * HR
                st.done(eng.tensor_copy(ELP[:, g0:g0 + HR, bass.ds(2 * i + b // BC, 1), :].rearrange("p g c h -> p g (c h)"),
                                        pring[:, b % 2, :].rearrange("p (g h) -> p g h", h=H)))

            def trip(i):
                for b in range(2 * BC):
                    if b >= 2 or not isinstance(i, int):
                        eng.wait_ge(logits_in[b % 2], 16 * HR * (BC * i + b // 2))
                        keep_logits(i, b - 2)
                    gather_logits(i, b)

            trip(0)
            st.n -= 4 * BC
            with eng.Fori(1, NCH // 2) as i:
                st.loop(i, 4 * BC)
                trip(i)
            st.end(NCH // 2)
            for b in range(2):
                eng.wait_ge(logits_in[b], 16 * HR * BC * NCH // 2)
                keep_logits(NCH // 2, b - 2)
            eng.sem_inc(S["logits_kept"], 1)
            eng.wait_ge(S["xm_ready"], 2 * G)
            eng.wait_ge(S["wo_psum"], 2 * G)
            st.done(eng.iota(iota_f[0:P, :], pattern=[[1, P]], base=0, channel_multiplier=0, allow_small_or_imprecise_dtypes=True))
            st.done(eng.memset(one125[:, :], float(P)))
            st.done(eng.memset(zrow[:, :], 0.0))
            st.done(eng.iota(thr[:, :], pattern=[[0, 1]], base=P, channel_multiplier=P, allow_small_or_imprecise_dtypes=True))
            st.done(eng.iota(sm[:, 4, :], pattern=[[XR, X]], base=0, channel_multiplier=0, allow_small_or_imprecise_dtypes=True))
            st.done(eng.iota(noff[:, :], pattern=[[P, T]], base=ROWS, channel_multiplier=1, allow_small_or_imprecise_dtypes=True))
            eng.sem_inc(S["iota_ready"], 1)
            zb = zrow[0:P, :]
            eng.dma_start(xs_tab[N:ROWS, :], zb[0:ROWS - N, :]).then_inc(S["zero_written"], 16)
            eng.dma_start(y_tab[ROWS:ROWS + 1, :], zb[0:1, :]).then_inc(S["zero_written"], 16)
            for j in range(2):
                eng.wait_ge(val_written[j], 16 * G)
            eng.wait_ge(S["weights_kept"], NB)
            def quarter(i, q):
                eng.wait_ge(S["tile_free"], RING * i + 4 * q + 4)
                st.done(eng.tensor_copy(vidx[:, 4 * q:4 * q + 4], src_i[:, bass.ds(RING * i + 4 * q, 4)]), apart=True)
                for s in range(4 * q, 4 * q + 4):
                    eng.indirect_dma_start(out=ring[:, s, :], out_offset=None, in_=val_tab[:, :],
                                           in_offset=bass.IndirectOffsetOnAxis(ap=vidx[:, s:s + 1], axis=0))\
                        .then_inc(gathered[q], 16)

            def report(q, n):
                eng.wait_ge(gathered[q], 64 * n)
                eng.sem_inc(S["vals_ready"], 4)

            def trip(i):
                eng.dma_start(rows(xs_tab, i), zb).then_inc(S["zero_written"], 16)
                st.loop(i, 4)
                for q in range(4):
                    quarter(i, q)
                    if q >= 2:
                        report(q - 2, i + 1)
                    elif not isinstance(i, int):
                        report(q + 2, i)

            assert ET // RING == T
            trips(eng, T, trip)
            st.end(T)
            for q in range(2, 4):
                report(q, ET // RING)
            eng.wait_ge(S["zero_written"], 16 * (T + 2))
            eng.wait_ge(S["slots_ready"], 1)
            eng.wait_ge(S["xn2_kept"], T)
            for t in range(T):
                eng.indirect_dma_start(out=xs_tab[:, :], out_offset=bass.IndirectOffsetOnAxis(ap=slot_s[:, t:t + 1], axis=0),
                                       in_=acc[:, t, :], in_offset=None,
                                       bounds_check=ROWS - 1, oob_is_err=False).then_inc(S["scattered"], 16)
            NT = X * XT
            for s in range(2):
                eng.wait_ge(y_out[s], 16 * (NT // 2))
            for t in range(T):
                if t >= NF:
                    eng.wait_ge(S["out_ready"], t - NF + 1)
                eng.indirect_dma_start(out=yg[t % NF], out_offset=None, in_=y_tab[:, :],
                                       in_offset=bass.IndirectOffsetOnAxis(ap=slot_g[:, t:t + 1], axis=0))\
                    .then_inc(yg_loaded[t % NF], 16)

        @block.tensor
        def _(pe):
            pe.sem_inc(S["tile_free"], RING)
            pe.sem_inc(S["onehot_free"], 2)
            pe.sem_inc(S["acc_free"], 2)

            def mm(o, l, r, start=True, stop=True):
                return pe.matmul(o, l, r, start=start, stop=stop)

            pe.wait_ge(S["consts_ready"], 2)
            pe.wait_ge(S["welr_ready"], 1)
            def logits(g, b):
                pe.wait_ge(S["xnT_ready"], g + 1)
                pe.wait_ge(S["elr_ready"], g)
                for j in range(2):
                    for k in range(KC):
                        last = mm(ps[0:P, 4, 16 * j:16 * j + 16], xT13[b][:, k, j * P:j * P + P], welr[:, k, :], k == 0, k == KC - 1)
                last.then_inc(S["elr_psum"], 1)

            def turn(g, b, copied):
                if copied is not None:
                    pe.wait_ge(S["xnT_ready"], copied)
                for j in range(2):
                    pe.wait_ge(S["xn_ready"], 2 * g + j + 1)
                    for k in range(KC):
                        last = pe.transpose(chunk(2 * b, k, j * P, P), xn[b][0:P, j, 128 * k:128 * k + 128], ident[0:P, 0:P])
                    last.then_inc(S["xn_transposed"], 1)

            turn(0, 0, None)
            turn(1, 1, None)
            logits(0, 0)

            def trip(i):
                turn(2 * i, 0, 2 * i - 1)
                logits(2 * i - 1, 1)
                turn(2 * i + 1, 1, 2 * i)
                logits(2 * i, 0)

            with pe.Fori(1, G // 2) as i:
                trip(i)
            turn(G - 1, 0, G - 2)
            logits(G - 2, 1)
            logits(G - 1, 0)
            pe.wait_ge(S["val_params"], 32)
            pe.wait_ge(S["proj_params"], 48)
            pe.wait_ge(S["omega_params"], 80)
            pe.wait_ge(S["elr_ready"], G)
            pe.wait_ge(S["v_ones"], 1)

            def group(g, b, u):
                pe.wait_ge(xT_loaded[b], 16 * (u + 1))
                pe.wait_ge(S["fq_read"], g)
                for c in range(C):
                    for k in range(KC):
                        last = mm(chunk(0, c, 0, GT), w_k[:, k, 128 * c:128 * c + 128], xT[b][:, k, :], k == 0, k == KC - 1)
                last.then_inc(S["kt_psum"], 1)
                pe.wait_ge(S["lq_read"], g)

                def values(j):
                    pe.wait_ge(S["vg_read"], 2 * g + j)
                    for k in range(KC):
                        last = mm(ps[0:P, 2, :], xT[b][:, k, j * P:j * P + P], w_vg[:, k, :], k == 0, k == KC - 1)
                    last.then_inc(S["vg_psum"], 1)
                    pe.wait_ge(S["v_copied"], 2 * g + j)
                    for k in range(KC):
                        last = mm(ps[0:P, 3, :], xT[b][:, k, j * P:j * P + P], w_v[:, k, :], k == 0, k == KC - 1)
                    last.then_inc(S["v_psum"], 1)

                def scores_k(j):
                    pe.wait_ge(S["fk_read"], 4 * g + 2 * j)
                    for c in range(C):
                        mm(ps[0:P, 4, 128 * c:128 * c + 128], ts3[:, c, j * P:j * P + P], omk[:, :])
                        last = mm(ps[0:P, 7, 2 * c:2 * c + 2], ts23[:, c, j * P:j * P + P], half2[:, :])
                    last.then_inc(S["fk_psum"], 1)

                values(0)
                pe.wait_ge(S["kt_copied"], 2 * g + 2)
                scores_k(0)
                scores_k(1)
                for c in range(C):
                    for k in range(KC):
                        last = mm(chunk(0, c, 0, GT), w_q[:, k, 128 * c:128 * c + 128], xT[b][:, k, :], k == 0, k == KC - 1)
                last.then_inc(S["qt_psum"], 1)
                values(1)
                pe.wait_ge(S["phi_ready"], 2 * g + 2)
                pe.wait_ge(S["v_copied"], 2 * g + 2)
                pe.wait_ge(S["kv_added"], g)
                for c in range(C):
                    for j in range(2):
                        last = mm(ps[:, 5 + c // 2, 129 * (c % 2):129 * (c % 2) + 129], phi[0:P, j, 128 * c:128 * c + 128],
                                  vext[0:P, j, c, :], j == 0, j == 1)
                last.then_inc(S["kv_psum"], 1)
                pe.wait_ge(S["qt_copied"], 2 * g + 2)
                for c in range(C):
                    last = mm(chunk(0, c, 0, GT), omq[:, :], ts3[:, c, :])
                last.then_inc(S["fq_psum"], 1)
                pe.wait_ge(S["vg_read"], 2 * g + 2)
                for c in range(C):
                    last = mm(chunk(2, c, 0, GT), halves[:, :], ts23[:, c, :])
                last.then_inc(S["lq_psum"], 1)
                

            def trip(i):
                group(2 * i, 0, i)
                group(2 * i + 1, 1, i)

            trips(pe, G // 2, trip)
            group(G - 1, 0, G // 2)
            pe.wait_ge(S["kvb_ready"], 8)
            pe.wait_ge(S["phiq_ready"], G)
            pe.wait_ge(S["wo_loaded"], 16)
            def attention(g):
                pe.wait_ge(S["attn_ready"], g)
                for c in range(C):
                    mm(chunk(0, c, 0, GT), kvb[:, c, :], xnT_all[:, c, bass.ds(g * GT, GT)])
                for c in range(C):
                    last = mm(chunk(2, c, 0, GT), kob[:, c, :], xnT_all[:, c, bass.ds(g * GT, GT)])
                last.then_inc(S["qkv_psum"], 1)

            def output(g):
                pe.wait_ge(S["attn_ready"], g + 1)
                pe.wait_ge(S["xm_ready"], 2 * g)
                for j in range(2):
                    for c in range(C):
                        last = mm(ps[0:P, 4 + j, :], attnT3[:, c, j * P:j * P + P], w_o[:, c, :], c == 0, c == C - 1)
                    last.then_inc(S["wo_psum"], 1)

            attention(0)
            attention(1)
            output(0)
            with pe.Fori(2, G) as g:
                attention(g)
                output(g - 1)
            output(G - 1)
            pe.wait_ge(S["logits_kept"], 1)
            pe.wait_ge(S["ert_loaded"], 16)
            for first, tab_, b0, copied in ((0, ELP, 0, "el_t_copied"), (NB, ert, 2, "er_t_copied")):
                for k in range(NB):
                    if k >= 2:
                        pe.wait_ge(S[copied], k - 1)
                    for g in range(TB * k, min(TB * k + TB, CT)):
                        last = pe.transpose(ps[:, b0 + k % 2, (g % TB) * P:(g % TB) * P + P], tab_[:, g, :, :].rearrange("p c h -> p (c h)"),
                                            ident[0:P, 0:P])
                    last.then_inc(S["seg_t_psum"], 1)
            pe.wait_ge(S["negdst_ready"], 1)
            pe.wait_ge(S["iota_ready"], 1)
            mm(ps[0:T, 4, 0:ET // 2], ones[0:1, 0:T], negdst[0:1, :].rearrange("p (u s) -> p u s", s=2)[:, :, 0]).then_inc(S["f_psum"], 1)
            pe.wait_ge(S["cmp_ready"], 1)
            mm(ps[0:1, 5, 0:T], cnt[0:T, 1:2], ident[0:T, 0:T]).then_inc(S["hi_psum"], 1)
            for k in range(NB):
                pe.wait_ge(S["weights_ready"], k + 1)
                if k >= 2:
                    pe.wait_ge(S["weights_kept"], k - 1)
                for g in range(TB * k, min(TB * k + TB, CT)):
                    last = pe.transpose(ps[0:P, 6 + k % 2, (g % TB) * 128:(g % TB) * 128 + 128], scan_x[:, g * P:g * P + P], ident[:, :])
                last.then_inc(S["weights_psum"], 1)
            pe.wait_ge(S["hi_ready"], 1)
            pe.wait_ge(S["weights_kept"], NB)
            zb16 = zrow.bitcast(BF16)

            def block_sums(c):
                lo = pe.value_load(hi_tab[0:1, bass.ds(c, 1)], min_val=0, max_val=ET // 2 - 1)
                hi = pe.value_load(hi_tab[0:1, bass.ds(c + 1, 1)], min_val=0, max_val=ET // 2 - 1)
                a = c % 2
                pe.wait_ge(S["acc_free"], c + 1)
                o512 = ps[0:P, bass.ds(2 * a, 1), :].rearrange("p a n -> p (a n)")
                o8 = ps[0:P, bass.ds(2 * a + 1, 1), 0:H].rearrange("p a n -> p (a n)")
                mm(o512, zb16[0:1, 0:P], zb16[0:1, 0:D], True, False)
                mm(o8, zb16[0:1, 0:P], zb16[0:1, 0:H], True, False)

                def tiles(u, lastone):
                    for s in range(2):
                        pe.wait_ge(S["msg_ready"], 2 * u + s + 1)
                        pe.wait_ge(S["onehot_ready"], 2 * (u + c) + s + 1)
                        stop = lastone and s == 1
                        m = mm(o512, onehot[s][0:P, :], ring[:, bass.ds((2 * u + s) % RING, 1), :].rearrange("p a n -> p (a n)"), False, stop)
                        if not lastone:
                            m.then_inc(S["tile_free"], 1)
                        mm(o8, onehot[s][0:P, :], EW[:, bass.ds(2 * u + s, 1), :].rearrange("p a n -> p (a n)"), False, stop)\
                            .then_inc(S["onehot_free"], 1)

                with pe.If(lo < hi):
                    with pe.Fori(lo, hi) as u:
                        tiles(u, False)
                tiles(hi, True)

            def gates(t):
                pe.wait_ge(S["xT6_ready"], t + 1)
                pe.wait_ge(S["gate_read"], t)
                for k in range(KC):
                    last = mm(ps[0:P, 6, 0:X], xT63[:, k, :], gw[:, k, :], k == 0, k == KC - 1)
                last.then_inc(S["gate_psum"], 1)

            def turn_xn2(t):
                pe.wait_ge(S["xn2_ready"], t + 1)
                pe.wait_ge(S["xT6_ready"], t)
                for k in range(KC):
                    last = pe.transpose(ps[:, 4, k * P:k * P + P], xn2b[0:P, 128 * k:128 * k + 128], ident[0:P, 0:P])
                last.then_inc(S["xn2_transposed"], 1)

            def step(c, sums):
                if sums:
                    block_sums(c)
                if not isinstance(c, int) or c >= 3:
                    gates(c - 3)
                if not isinstance(c, int) or 2 <= c < T + 2:
                    turn_xn2(c - 2)

            staggered(pe, step)
            def trip(i):
                pe.wait_ge(S["col_ready"], i + 1)
                mm(ps[0:P, 0, 0:X], ones[0:P, 0:P], sm[:, 0, :]).then_inc(S["col_psum"], 1)

            trips(pe, SINK, trip)
            def trip(i):
                pe.wait_ge(S["cnt_ready"], i + 1)
                mm(ps[0:P, 1, 0:X], ones[0:P, 0:P], sm[:, 1, :]).then_inc(S["cnt_psum"], 1)

            trips(pe, BITS + 1, trip)
            for r in range(2):
                pe.wait_ge(S["pre_ready"], r + 1)
                mm(ps[0:P, 2, 0:T * X], before[0:P, 0:P], win)
                mm(ps[0:P, 3, 0:T * X], ones[0:P, 0:P], win).then_inc(S["pre_psum"], 1)
            pe.wait_ge(S["experts_loaded"], 16 * X)

            def routed(n, s, e_):
                pe.wait_ge(xs_loaded[s], 16 * (n // 2 + 1))
                pe.wait_ge(S["xsT_copied"], n)
                for k in range(KC):
                    last = pe.transpose(ps[:, 4 + s, k * SLOT:k * SLOT + SLOT], xs[s][:, 128 * k:128 * k + 128], ident[0:SLOT, 0:SLOT])
                last.then_inc(S["xs_transposed"], 1)
                pe.wait_ge(S["xsT_copied"], n + 1)
                pe.wait_ge(S["y_ready"], n)
                for k in range(KC):
                    last = mm(ps[0:SLOT, 6 + s, :], xsT[s][:, k * SLOT:k * SLOT + SLOT],
                              exp_w[:, bass.ds(e_, 1), k, :].rearrange("p a n -> p (a n)"), k == 0, k == KC - 1)
                last.then_inc(S["y_psum"], 1)

            def trip(i):
                for m in range(2 * XT):
                    routed(i * 2 * XT + m, m % 2, 2 * i + m // XT)

            trips(pe, X // 2, trip)

        @block.scalar
        def _(act):
            st = Steps(act, S["act_step"])
            fn = act.activation
            act.wait_ge(S["consts_ready"], 2)

            def deviation(g):
                for j in range(2):
                    act.wait_ge(S["var_ready"], 2 * g + j + 1)
                    fn(std[0:P, j:j + 1], mv[0:P, j, 1:2], ACT.Sqrt, bias=eps[0:P, :]).then_inc(S["std_ready"], 1)

            def copy_xT(g, b, kept):
                act.wait_ge(S["xn_transposed"], 2 * g + 2)
                if kept is not None:
                    act.wait_ge(xT_kept[b], 16 * kept)
                    act.wait_ge(S["elr_psum"], 2 * kept - 1 + b)
                fn(xT1[b], two(2 * b), ACT.Copy).then_inc(S["xnT_ready"], 1)

            deviation(0)
            deviation(1)
            copy_xT(0, 0, None)
            deviation(2)
            copy_xT(1, 1, None)
            with act.Fori(1, G // 2) as i:
                deviation(2 * i + 1)
                copy_xT(2 * i, 0, i)
                deviation(2 * i + 2)
                copy_xT(2 * i + 1, 1, i)
            copy_xT(G - 1, 0, G // 2)
            act.wait_ge(S["elr_written"], 32 * G)
            for b in range(2):
                act.wait_ge(xT_kept[b], 16 * (G // 2 + 1 - b))

            def group(g):
                act.wait_ge(S["kt_psum"], g + 1)
                act.wait_ge(S["phiq_ready"], g)
                fn(ts, two(0), ACT.Copy, scale=SCALE).then_inc(S["kt_copied"], 1)
                fn(ts2, two(0), ACT.Square, scale=SCALE).then_inc(S["kt_copied"], 1)

                def v_copy(j):
                    act.wait_ge(S["v_psum"], 2 * g + j + 1)
                    act.wait_ge(S["kv_psum"], g)
                    fn(vext[0:P, j, :, 0:128], ps[0:P, 3, :].rearrange("p (c n) -> p c n", c=C), ACT.Copy).then_inc(S["v_copied"], 1)

                v_copy(0)
                for j in range(2):
                    act.wait_ge(S["fk_read"], 4 * g + 2 * j + 2)
                    fn(phi[0:P, j, :], phi[0:P, j, :], ACT.Exp).then_inc(S["kexp_done"], 1)
                    fn(nk[0:P, j, :], nk[0:P, j, :], ACT.Exp, scale=-0.5).then_inc(S["kexp_done"], 1)
                act.wait_ge(S["qt_psum"], g + 1)
                act.wait_ge(S["fk_psum"], 2 * g + 2)
                fn(ts, two(0), ACT.Copy, scale=SCALE).then_inc(S["qt_copied"], 1)
                fn(ts2, two(0), ACT.Square, scale=SCALE).then_inc(S["qt_copied"], 1)
                v_copy(1)
                act.wait_ge(S["fq_read"], g + 1)
                fn(ts, ts, ACT.Exp).then_inc(S["qexp_done"], 1)
                act.wait_ge(S["lq_read"], g + 1)
                fn(ts2, ts2, ACT.Exp, scale=-0.5).then_inc(S["qexp_done"], 1)

            def trip(g):
                group(g)

            trips(act, G, trip)
            for k in range(NB):
                act.wait_ge(S["seg_t_psum"], k + 1)
                n = min(TB, CT - TB * k) * P
                fn(scan_e[:, TB * k * P:TB * k * P + n], ps[:, k % 2, 0:n], ACT.Copy).then_inc(S["el_t_copied"], 1)
            act.wait_ge(S["dst_read"], 1)
            m3 = scan_m.rearrange("q (p g) -> q g p", g=CT)
            for k in range(NB):
                act.wait_ge(S["seg_t_psum"], NB + k + 1)
                n = min(TB, CT - TB * k)
                fn(m3[:, TB * k:TB * k + n, :], ps[:, 2 + k % 2, 0:n * P].rearrange("q (g p) -> q g p", g=n), ACT.Copy).then_inc(S["er_t_copied"], 1)
            for k in range(NB):
                act.wait_ge(S["shifted"], k + 1)
                x_ = scan_x[:, TB * k * P:min(TB * k * P + TB * P, CL)]
                fn(x_, x_, ACT.Exp).then_inc(S["weights_ready"], 1)
            act.wait_ge(S["iota_ready"], 1)
            act.wait_ge(S["hi_ready"], 1)

            def onehots(u, c):
                for s in range(2):
                    k2 = 2 * (u + c) + s
                    fn(absd[s][0:P, :], iota_f[0:P, :], ACT.Abs, bias=negdst[:, bass.ds(2 * u + s, 1)]).then_inc(S["act_step"], 1)
                    act.wait_ge(S["act_step"], k2 + c + 1)
                    act.wait_ge(S["onehot_free"], k2 + 1)
                    fn(onehot[s][0:P, :], absd[s][0:P, :], ACT.Relu, scale=-1.0, bias=1.0).then_inc(S["onehot_ready"], 1)

            def block_onehots(c):
                lo = act.value_load(hi_tab[0:1, bass.ds(c, 1)], min_val=0, max_val=ET // 2 - 1)
                hi = act.value_load(hi_tab[0:1, bass.ds(c + 1, 1)], min_val=0, max_val=ET // 2 - 1)
                with act.If(lo < hi):
                    with act.Fori(lo, hi) as u:
                        onehots(u + 1, c)
                fn(iota_f[0:P, :], iota_f[0:P, :], ACT.Identity, bias=one125[0:P, :]).then_inc(S["act_step"], 1)
                act.wait_ge(S["act_step"], 2 * (hi + c) + 2 + c + 1)
                if not isinstance(c, int) or c < T - 1:
                    onehots(hi, c + 1)
                return hi

            def copy_sums(c, hi):
                act.wait_ge(S["onehot_free"], 2 * (hi + c) + 2 + 2)
                a = c % 2
                fn(acc[:, bass.ds(c, 1), :].rearrange("p a n -> p (a n)"), ps[0:P, bass.ds(2 * a, 1), :].rearrange("p a n -> p (a n)"), ACT.Copy)\
                    .then_inc(S["block_summed"], 1)
                fn(accd[:, bass.ds(c, 1), :].rearrange("p a n -> p (a n)"), ps[0:P, bass.ds(2 * a + 1, 1), 0:H].rearrange("p a n -> p (a n)"), ACT.Copy)\
                    .then_inc(S["acc_free"], 1)

            def deviation2(t):
                act.wait_ge(S["var_ready"], T + t + 1)
                fn(std[0:P, 0:1], mv[0:P, 0, 1:2], ACT.Sqrt, bias=eps[0:P, :]).then_inc(S["std_ready"], 1)

            def copy_xn2(t):
                act.wait_ge(S["xn2_transposed"], t + 1)
                act.wait_ge(S["gate_psum"], t)
                fn(xT6, ps[:, 4, 0:500], ACT.Copy).then_inc(S["xT6_ready"], 1)
                fn(acc[:, bass.ds(t, 1), :].rearrange("p a n -> p (a n)"), xn2b[0:P, :], ACT.Copy).then_inc(S["xn2_kept"], 1)

            def step(c, sums):
                if sums:
                    hi = block_onehots(c)
                    copy_sums(c, hi)
                if not isinstance(c, int) or 1 <= c < T + 1:
                    deviation2(c - 1)
                if not isinstance(c, int) or 2 <= c < T + 2:
                    copy_xn2(c - 2)

            onehots(0, 0)
            staggered(act, step)
            def trip(i):
                for s in range(2):
                    n = 2 * i + s
                    act.wait_ge(S["xs_transposed"], n + 1)
                    act.wait_ge(S["y_psum"], n)
                    fn(xsT[s], ps[:, 4 + s, 0:KC * SLOT], ACT.Copy).then_inc(S["xsT_copied"], 1)

            trips(act, X * XT // 2, trip)

        @block.vector
        def _(v):
            st = Steps(v, S["dve_step"], S["dve_passed"])
            v.wait_ge(S["elr_params"], 96)
            for w_, a_, o_ in ((s_wsrc, s_al, 0), (s_wdst, s_ar, H)):
                st.done(v.tensor_tensor(out=s_prod, in0=w_, in1=a_.unsqueeze(1).to_broadcast([128, KC, D]), op=ALU.mult))
                st.done(v.tensor_reduce(out=welr[:, :, o_:o_ + H], in_=s_prod.rearrange("p k (h f) -> p k h f", h=H), axis=AX.X, op=ALU.add))
            for b_, a_, o_ in ((s_bs, s_al, 0), (s_bd, s_ar, H)):
                st.done(v.tensor_tensor(out=b_, in0=b_, in1=a_, op=ALU.mult))
                st.done(v.tensor_reduce(out=belr[:, o_:o_ + H], in_=b_[0:P, :].rearrange("p (h f) -> p h f", h=H), axis=AX.X, op=ALU.add))
            v.sem_inc(S["welr_ready"], 1)
            def norm(g, b, u):
                v.wait_ge(x_loaded[b], 32 * (u + 1))
                for j in range(2):
                    st.done(v.bn_stats(out=st6[0:P, j, :], in_=x_in[b][0:P, j, :]), apart=True)
                    v.bn_aggr(out=mv[0:P, j, :], in_=st6[0:P, j, :]).then_inc(S["var_ready"], 1)
                for j in range(2):
                    v.wait_ge(S["std_ready"], 2 * g + j + 1)
                    st.done(v.reciprocal(rstd[0:P, j:j + 1], std[0:P, j:j + 1]))
                    v.tensor_scalar(xn[b][0:P, j, :], x_in[b][0:P, j, :], mv[0:P, j, 0:1], rstd[0:P, j:j + 1], ALU.subtract, ALU.mult)\
                        .then_inc(S["xn_ready"], 1)

            def add_bias(g):
                v.wait_ge(S["elr_psum"], g + 1)
                v.wait_ge(S["elr_written"], 32 * g)
                v.tensor_tensor(out=elr_sb[0:P, :, :], in0=ps[0:P, 4, 0:32].rearrange("p (j n) -> p j n", j=2),
                                in1=belr[:, :].unsqueeze(1).to_broadcast([P, 2, 2 * H]), op=ALU.add).then_inc(S["elr_ready"], 1)

            def trip(i):
                st.loop(i, 8)
                for b in range(2):
                    v.wait_ge(S["xn_transposed"], 4 * i)
                    norm(2 * i + b, b, i)
                    if b == 1 or not isinstance(i, int):
                        add_bias(2 * i + b - 1)

            node, start, nxt, tmp = noff[:, :], tb[0][:, :], tb[1][:, :], tb[2][:, :]

            def below(row, n, out_):
                l3 = look[:, 0:T * n].rearrange("p (t n) -> p t n", n=n)
                st.done(v.tensor_tensor(out=l3, in0=row, in1=node.unsqueeze(2).to_broadcast([P, T, n]), op=ALU.is_lt))
                st.done(v.tensor_reduce(out=out_, in_=l3, axis=AX.X, op=ALU.add))

            def look_at(n):
                return look[:, 0:T * n].bitcast(INT32).rearrange("p (t n) -> p t n", n=n)

            def first_top():
                v.wait_ge(S["node_ready"], 1)
                v.wait_ge(S["tops_loaded"], 32)
                top_row = tops.rearrange("p (a b) -> p a b", b=MIDS)[:, :, 0]
                below(top_row.unsqueeze(1).to_broadcast([P, T, TOPS]), TOPS, start)
                st.done(v.tensor_scalar(start, start, -1.0, 0.0, ALU.add, ALU.max))
                st.done(v.tensor_copy(slot_g[:, :], start))
                v.sem_inc(S["row_ready"], 1)

            def first_tile():
                v.wait_ge(S["looked_up"], 16 * T)
                below(look_at(MIDS), MIDS, tmp)
                st.done(v.scalar_tensor_tensor(out=start, in0=start, scalar=float(MIDS), in1=tmp, op0=ALU.mult, op1=ALU.add))
                st.done(v.tensor_scalar(start, start, -1.0, 0.0, ALU.add, ALU.max))
                st.done(v.tensor_copy(slot_g[:, :], start))
                v.sem_inc(S["row_ready"], 1)

            def first_edge():
                v.wait_ge(S["looked_up"], 32 * T)
                below(look_at(P), P, tmp)
                st.done(v.scalar_tensor_tensor(out=start, in0=start, scalar=float(P), in1=tmp, op0=ALU.mult, op1=ALU.add))
                v.sem_inc(S["row_ready"], 1)

            def first_row():
                c3 = look[:, 0:T * (NCH - 1)].rearrange("p (t n) -> p t n", n=NCH - 1)
                st.done(v.tensor_tensor(out=c3, in0=start.unsqueeze(2).to_broadcast([P, T, NCH - 1]),
                                        in1=cthr.unsqueeze(1).to_broadcast([P, T, NCH - 1]), op=ALU.is_ge))
                st.done(v.tensor_reduce(out=tmp, in_=c3, axis=AX.X, op=ALU.add))
                v.wait_ge(S["starts_moved"], 48)
                st.done(v.tensor_tensor(out=nxt, in0=start, in1=nxt, op=ALU.is_lt))
                st.done(v.tensor_scalar(start, start, float(NCH), float(-E), ALU.mult, ALU.add))
                st.done(v.scalar_tensor_tensor(out=start, in0=tmp, scalar=float(1 - NCH * CL), in1=start, op0=ALU.mult, op1=ALU.add))
                st.done(v.tensor_tensor(out=start, in0=start, in1=nxt, op=ALU.mult))
                st.done(v.tensor_scalar(slot_s[:, :], start, float(E), None, ALU.add))
                v.sem_inc(S["row_ready"], 1)

            trip(0)
            st.end(1)
            first_top()
            for step_, lo_, hi_ in ((first_tile, 1, 5), (first_edge, 5, 9), (first_row, 9, G // 2)):
                st.n -= 8 * lo_
                with v.Fori(lo_, hi_) as i:
                    trip(i)
                st.end(hi_)
                step_()
            v.wait_ge(S["xn_transposed"], 2 * G - 2)
            norm(G - 1, 0, G // 2)
            add_bias(G - 2)
            add_bias(G - 1)
            v.wait_ge(S["elr_written"], 32 * G)
            v.wait_ge(S["elr_psum"], G)
            for b in range(2):
                v.wait_ge(xT_kept[b], 16 * (G // 2 + 1 - b))
            v.memset(vext[:, :, :, 128:129], 1.0).then_inc(S["v_ones"], 1)
            v.wait_ge(S["val_params"], 32)
            v.wait_ge(S["consts_ready"], 2)

            def trip(g):
                st.loop(g, 3)

                def values(j):
                    v.wait_ge(S["vg_psum"], 2 * g + j + 1)
                    v.wait_ge(val_written[j], 16 * g)
                    v.tensor_tensor(out=vout[:, j, :], in0=ps[0:P, 2, :], in1=bval[:, :], op=ALU.add).then_inc(S["vg_read"], 1)

                values(0)
                for j in range(2):
                    v.wait_ge(S["fk_psum"], 2 * g + j + 1)
                    v.wait_ge(S["kv_psum"], g)
                    v.tensor_scalar(phi[0:P, j, :], ps[0:P, 4, :], FCLAMP, None, ALU.min).then_inc(S["fk_read"], 1)
                    v.tensor_scalar(nk[0:P, j, :], ps[0:P, 7, 0:H], EPS_PHI * EPS_PHI, None, ALU.max).then_inc(S["fk_read"], 1)
                for j in range(2):
                    v.wait_ge(S["kexp_done"], 4 * g + 2 * j + 2)
                    st.done(v.tensor_scalar(nk[0:P, j, :], nk[0:P, j, :], EPS_PHI, None, ALU.max))
                    p3 = phi[0:P, j, :].rearrange("p (h m) -> p h m", h=H)
                    v.tensor_tensor(out=p3, in0=p3, in1=nk[0:P, j, :].unsqueeze(2).to_broadcast([P, H, F]), op=ALU.mult)\
                        .then_inc(S["phi_ready"], 1)
                values(1)
                v.wait_ge(S["kv_psum"], g + 1)
                v.wait_ge(S["kv_added"], g)
                v.tensor_tensor(out=kvacc[:, :, :], in0=kvacc[:, :, :], in1=ps[:, 5:7, 0:258], op=ALU.add).then_inc(S["kv_added"], 1)
                v.wait_ge(S["fq_psum"], g + 1)
                v.tensor_scalar(ts, two(0), FCLAMP, None, ALU.min).then_inc(S["fq_read"], 1)
                v.wait_ge(S["lq_psum"], g + 1)
                v.tensor_scalar(ts2, two(2), EPS_PHI * EPS_PHI, None, ALU.max).then_inc(S["lq_read"], 1)
                v.wait_ge(S["qexp_done"], 2 * g + 2)
                st.done(v.tensor_scalar(ts2, ts2, EPS_PHI, None, ALU.max))
                v.tensor_tensor(out=xnT_all[:, :, bass.ds(g * GT, GT)], in0=ts3, in1=ts23, op=ALU.mult).then_inc(S["phiq_ready"], 1)

            trips(v, G, trip)
            st.end(G)
            v.wait_ge(S["kv_added"], G)
            kv4 = kvacc[:, :, :].rearrange("p b (q n) -> p (b q) n", n=129)
            for r in range(2):
                h_ = slice(F * r, F * r + F)
                for c in range(C):
                    v.tensor_copy(kob[h_, c, h_], kv4[h_, c, 128:129].to_broadcast([F, F])).then_inc(S["dve_misc"], 1)
                v.tensor_copy(kvb[h_, :, h_], kv4[h_, :, h_]).then_inc(S["kvb_ready"], 4)
            v.wait_ge(S["dve_misc"], 2 * C)
            def divide(g):
                v.wait_ge(S["qkv_psum"], g + 1)
                st.done(v.reciprocal(rq.rearrange("p (b n) -> p b n", b=2), two(2)))
                v.wait_ge(S["wo_psum"], 2 * g)
                v.tensor_tensor(out=attnT.rearrange("p (b n) -> p b n", b=2), in0=two(0), in1=rq.rearrange("p (b n) -> p b n", b=2), op=ALU.mult)\
                    .then_inc(S["attn_ready"], 1)

            def add_x(g):
                for j in range(2):
                    v.wait_ge(S["wo_psum"], 2 * g + j + 1)
                    v.wait_ge(xm_in[j], 16 * (g + 1))
                    v.tensor_tensor(out=xm[0:P, j, :], in0=xm[0:P, j, :], in1=ps[0:P, 4 + j, :], op=ALU.add).then_inc(S["xm_ready"], 1)

            divide(0)
            st.n -= 1
            with v.Fori(1, G) as g:
                st.loop(g, 1)
                divide(g)
                add_x(g - 1)
            st.end(G)
            add_x(G - 1)
            v.wait_ge(S["idx_loaded"], 32)
            st.done(v.tensor_scalar(negdst[:, :], dst_i[:, :], -1.0, None, ALU.mult))
            v.sem_inc(S["negdst_ready"], 1)
            v.wait_ge(S["dst_loaded"], 16 * NCH)
            st.done(v.tensor_copy(scan_d, scan_m.bitcast(INT32)))
            v.sem_inc(S["dst_read"], 1)
            st.done(v.tensor_tensor(out=scan_p[:, 1:CL], in0=scan_d[:, 1:CL], in1=scan_d[:, 0:CL - 1], op=ALU.is_equal))
            st.done(v.memset(scan_p[:, 0:1], 0.0))
            v.wait_ge(S["er_t_copied"], NB)
            st.done(v.tensor_tensor_scan(out=scan_x, data0=scan_p[:, 0:CL], data1=scan_m, initial=0.0, op0=ALU.mult, op1=ALU.add))
            v.wait_ge(S["el_t_copied"], NB)
            st.done(v.tensor_tensor(out=scan_x, in0=scan_x, in1=scan_e, op=ALU.add))
            st.done(v.scalar_tensor_tensor(out=scan_x, in0=scan_x, scalar=0.2, in1=scan_x, op0=ALU.mult, op1=ALU.max))
            st.done(v.tensor_scalar(scan_p[:, 0:CL], scan_p[:, 0:CL], -1.0, -FAR, ALU.add, ALU.mult))
            st.done(v.memset(scan_p[:, CL:CL + 1], FAR))
            st.done(v.tensor_tensor_scan(out=scan_m, data0=scan_p[:, 0:CL], data1=scan_x, initial=FAR, op0=ALU.add, op1=ALU.max))
            st.done(v.tensor_tensor_scan(out=rev(scan_e), data0=rev(scan_p[:, 1:CL + 1]), data1=rev(scan_m), initial=FAR, op0=ALU.add, op1=ALU.max))
            for c_, s_ in ((0, scan_d[:, 0:1]), (1, scan_e[:, 0:1]), (2, scan_d[:, CL - 1:CL]), (3, scan_m[:, CL - 1:CL])):
                st.done(v.tensor_copy(ends[:, c_:c_ + 1], s_))
            v.sem_inc(S["ends_ready"], 1)
            v.wait_ge(S["f_psum"], 1)
            v.wait_ge(S["iota_ready"], 1)
            st.done(v.tensor_scalar(cmp[0:T, :], ps[0:T, 4, 0:ET // 2], thr[0:T, :], 0.0, ALU.add, ALU.is_gt))
            st.done(v.tensor_reduce(out=cnt[0:T, 0:1], in_=cmp[0:T, :], axis=AX.X, op=ALU.add))
            st.done(v.tensor_scalar(cnt[0:T, 1:2], cnt[0:T, 0:1], -1.0, 0.0, ALU.add, ALU.max))
            v.sem_inc(S["cmp_ready"], 1)
            v.wait_ge(S["hi_psum"], 1)
            st.done(v.memset(hi_tab[0:1, 0:1], 0))
            st.done(v.tensor_copy(hi_tab[0:1, 1:T + 1], ps[0:1, 5, 0:T]))
            v.sem_inc(S["hi_ready"], 1)
            v.wait_ge(S["ends_written"], 16 * (NCH + 1))
            cd = cand.rearrange("p k (a b) -> p (k a) b", b=2)
            for side, edge in ((0, scan_d[:, 0:1]), (1, scan_d[:, CL - 1:CL])):
                st.done(v.tensor_scalar(candv, cd[:, :, 0], edge, FAR, ALU.not_equal, ALU.mult))
                st.done(v.tensor_tensor(out=candv, in0=candv, in1=cd[:, :, 1], op=ALU.add))
                st.done(v.tensor_reduce(out=cfl[:, side:side + 1], in_=candv, axis=AX.X, op=ALU.max))
                st.done(v.tensor_scalar(scan_m, scan_d, edge, FAR, ALU.not_equal, ALU.mult))
                st.done(v.scalar_tensor_tensor(out=scan_e, in0=scan_m, scalar=cfl[:, side:side + 1], in1=scan_e, op0=ALU.add, op1=ALU.max))
            v.sem_inc(S["segmax_ready"], 1)
            for k in range(NB):
                lo_, hi_ = TB * k * P, min(TB * k * P + TB * P, CL)
                v.tensor_tensor(out=scan_x[:, lo_:hi_], in0=scan_x[:, lo_:hi_], in1=scan_e[:, lo_:hi_], op=ALU.subtract)\
                    .then_inc(S["shifted"], 1)
            ew_v = EW.rearrange("p (c g) h -> p g c h", c=NCH)
            for k in range(NB):
                v.wait_ge(S["weights_psum"], k + 1)
                n = min(TB, CT - TB * k)
                v.tensor_copy(ew_v[:, TB * k:TB * k + n, :, :], ps[0:P, 6 + k % 2, 0:n * 128].rearrange("p (g c h) -> p g c h", g=n, c=NCH))\
                    .then_inc(S["weights_kept"], 1)
            v.wait_ge(S["weights_kept"], NB)

            def messages(u):
                for s in range(2):
                    v.wait_ge(S["vals_ready"], 2 * u + s + 1)
                    r3 = ring[:, bass.ds((2 * u + s) % RING, 1), :].rearrange("p a (h f) -> p (a h) f", h=H)
                    w_ = EW[:, bass.ds(2 * u + s, 1), :].rearrange("p a h -> p (a h)").unsqueeze(2).to_broadcast([P, H, F])
                    v.tensor_tensor(out=r3, in0=r3, in1=w_, op=ALU.mult).then_inc(S["msg_ready"], 1)

            def block_messages(c):
                lo = v.value_load(hi_tab[0:1, bass.ds(c, 1)], min_val=0, max_val=ET // 2 - 1)
                hi = v.value_load(hi_tab[0:1, bass.ds(c + 1, 1)], min_val=0, max_val=ET // 2 - 1)
                with v.If(lo < hi):
                    with v.Fori(lo, hi) as u:
                        messages(u + 1)

            def read_gates(t):
                v.wait_ge(S["gate_psum"], t + 1)
                v.tensor_scalar(gK[:, bass.ds(t * X, X)], ps[0:P, 6, 0:X], 1e-10, None, ALU.max).then_inc(S["gate_read"], 1)

            def slot_of(t):
                return xmb[0:P, bass.ds(t % 2, 1), :].rearrange("p a n -> p (a n)")

            def norm_x1(t):
                v.wait_ge(S["std_ready"], T + t + 1)
                st.done(v.reciprocal(rstd[0:P, 0:1], std[0:P, 0:1]))
                v.wait_ge(S["xn2_transposed"], t)
                v.wait_ge(S["xn2_kept"], t)
                v.tensor_scalar(xn2b[0:P, :], slot_of(t), mv[0:P, 0, 0:1], rstd[0:P, 0:1], ALU.subtract, ALU.mult)\
                    .then_inc(S["xn2_ready"], 1)

            def make_x1(t):
                v.wait_ge(S["acc_free"], t + 3)
                a1 = acc[:, bass.ds(t, 1), :].rearrange("p a n -> p (a n)")
                st.done(v.tensor_scalar(den[0:P, :], accd[:, bass.ds(t, 1), :].rearrange("p a n -> p (a n)"), 1e-16, None, ALU.max))
                st.done(v.reciprocal(den[0:P, :], den[0:P, :]))
                v.wait_ge(S["block_summed"], t + 1)
                a3 = a1.rearrange("p (h f) -> p h f", h=H)
                st.done(v.tensor_tensor(out=a3, in0=a3, in1=den[0:P, :].unsqueeze(2).to_broadcast([P, H, F]), op=ALU.mult))
                v.wait_ge(S["xm_back"], 16 * (t + 1))
                v.tensor_tensor(out=slot_of(t), in0=slot_of(t), in1=a1, op=ALU.add).then_inc(S["x1_ready"], 1)
                v.wait_ge(S["x1_ready"], t + 1)
                v.sem_inc(S["dve_passed"], 1)
                st.done(v.bn_stats(out=st6[0:P, 0, :], in_=slot_of(t)), apart=True)
                v.bn_aggr(out=mv[0:P, 0, :], in_=st6[0:P, 0, :]).then_inc(S["var_ready"], 1)

            def step(c, sums):
                if sums:
                    block_messages(c)
                if not isinstance(c, int) or c >= 3:
                    read_gates(c - 3)
                if not isinstance(c, int):
                    st.loop(c, 5)
                if not isinstance(c, int) or 2 <= c < T + 2:
                    norm_x1(c - 2)
                if not isinstance(c, int) or 1 <= c < T + 1:
                    make_x1(c - 1)

            messages(0)
            staggered(v, step, st)
            def te(a_):
                return a_.rearrange("p (t e) -> p t e", e=X)

            def et(a_):
                return a_.rearrange("p (t e) -> p e t", e=X)

            def over_t(a_):
                return a_.unsqueeze(1).to_broadcast([P, T, X])

            def over_e(a_):
                return a_.unsqueeze(2).to_broadcast([P, T, X])

            sa, sr, lose = tb[0], tb[1], tb[2]
            v.wait_ge(S["gate_read"], T)
            st.done(v.memset(sa[:, :], 1.0))
            def trip(i):
                st.loop(i, 6)
                st.done(v.tensor_tensor(out=te(gB), in0=te(gK), in1=over_e(sa[:, :]), op=ALU.mult))
                st.done(v.tensor_reduce(out=sm[:, 0, :], in_=et(gB), axis=AX.X, op=ALU.add))
                v.sem_inc(S["col_ready"], 1)
                v.wait_ge(S["col_psum"], i + 1)
                st.done(v.reciprocal(sm[:, 2, :], ps[0:P, 0, 0:X]))
                st.done(v.tensor_tensor(out=te(gB), in0=te(gK), in1=over_t(sm[:, 2, :]), op=ALU.mult))
                st.done(v.tensor_reduce(out=sr[:, :], in_=te(gB), axis=AX.X, op=ALU.add))
                st.done(v.reciprocal(sa[:, :], sr[:, :]))

            trips(v, SINK, trip)
            st.end(SINK)
            st.done(v.tensor_tensor(out=te(gA), in0=te(gB), in1=over_e(sa[:, :]), op=ALU.mult))
            cur, bit, trial, hit = [smi[:, q, :] for q in range(4)]
            st.done(v.memset(cur, 0))
            st.done(v.memset(bit, 1 << (BITS - 1)))
            def trip(i):
                st.loop(i, 6)
                st.done(v.tensor_tensor(out=trial, in0=cur, in1=bit, op=ALU.bitwise_or))
                st.done(v.tensor_tensor(out=te(sel), in0=te(gA), in1=over_t(trial.bitcast(FP32)), op=ALU.is_ge))
                st.done(v.tensor_reduce(out=sm[:, 1, :], in_=et(sel), axis=AX.X, op=ALU.add))
                v.sem_inc(S["cnt_ready"], 1)
                v.wait_ge(S["cnt_psum"], i + 1)
                st.done(v.scalar_tensor_tensor(out=hit, in0=ps[0:P, 1, 0:X], scalar=float(CAP), in1=bit, op0=ALU.is_ge, op1=ALU.mult))
                st.done(v.tensor_tensor(out=cur, in0=cur, in1=hit, op=ALU.bitwise_or))
                st.done(v.tensor_scalar(bit, bit, 0.5, None, ALU.mult))

            trips(v, BITS, trip)
            st.end(BITS)
            cf = over_t(cur.bitcast(FP32))
            st.done(v.tensor_tensor(out=te(sel), in0=te(gA), in1=cf, op=ALU.is_gt))
            st.done(v.tensor_tensor(out=te(win), in0=te(gA), in1=cf, op=ALU.is_equal))
            st.done(v.tensor_reduce(out=sm[:, 1, :], in_=et(sel), axis=AX.X, op=ALU.add))
            v.sem_inc(S["cnt_ready"], 1)
            v.wait_ge(S["cnt_psum"], BITS + 1)
            st.done(v.tensor_scalar(sm[:, 3, :], ps[0:P, 1, 0:X], -1.0, float(CAP), ALU.mult, ALU.add))
            keep3 = keep.rearrange("p (e t) -> p e t", e=X)
            st.done(v.memset(keep, 1.0))
            st.done(v.memset(keep3[:, :, 0:1], 0.0))

            def rank(r):
                v.sem_inc(S["pre_ready"], 1)
                v.wait_ge(S["pre_psum"], r + 1)
                ct3 = cnt_t.rearrange("p (e t) -> p e t", e=X)
                st.done(v.tensor_copy(ct3, et(ps[0:P, 3, 0:T * X])))
                st.done(v.tensor_tensor_scan(out=gB, data0=keep, data1=cnt_t, initial=0.0, op0=ALU.mult, op1=ALU.add))
                st.done(v.tensor_tensor(out=gB, in0=gB, in1=cnt_t, op=ALU.subtract))
                st.done(v.tensor_tensor(out=te(pre), in0=te(ps[0:P, 2, 0:T * X]), in1=gB.rearrange("p (e t) -> p t e", e=X), op=ALU.add))

            rank(0)
            st.done(v.tensor_tensor(out=te(pre), in0=te(pre), in1=over_t(sm[:, 3, :]), op=ALU.is_lt))
            st.done(v.tensor_tensor(out=pre, in0=pre, in1=win, op=ALU.mult))
            st.done(v.tensor_tensor(out=sel, in0=sel, in1=pre, op=ALU.add))
            st.done(v.tensor_reduce(out=rcnt[:, :], in_=te(sel), axis=AX.X, op=ALU.add))
            st.done(v.tensor_scalar(rcnt[:, :], rcnt[:, :], 1.0, None, ALU.add))
            st.done(v.reciprocal(rcnt[:, :], rcnt[:, :]))
            st.done(v.scalar_tensor_tensor(out=win, in0=gA, scalar=0.5, in1=sel, op0=ALU.is_gt, op1=ALU.mult))
            st.done(v.tensor_reduce(out=sr[:, :], in_=te(win), axis=AX.X, op=ALU.add))
            st.done(v.tensor_scalar(sa[:, :], sr[:, :], 1.5, None, ALU.is_lt))
            st.done(v.tensor_tensor(out=te(win), in0=te(win), in1=over_e(sa[:, :]), op=ALU.mult))
            st.done(v.tensor_tensor(out=sr[:, :], in0=sr[:, :], in1=sa[:, :], op=ALU.mult))
            st.done(v.tensor_scalar(lose[:, :], sr[:, :], -1.0, 1.0, ALU.mult, ALU.add))
            rank(1)
            st.done(v.tensor_tensor(out=te(pre), in0=te(pre), in1=over_t(sm[:, 4, :]), op=ALU.add))
            st.done(v.tensor_tensor(out=pre, in0=pre, in1=win, op=ALU.mult))
            st.done(v.tensor_reduce(out=sr[:, :], in_=te(pre), axis=AX.X, op=ALU.add))
            st.done(v.tensor_tensor(out=noff[:, :], in0=noff[:, :], in1=lose[:, :], op=ALU.mult))
            st.done(v.tensor_tensor(out=slot_s[:, :], in0=noff[:, :], in1=sr[:, :], op=ALU.add))
            st.done(v.scalar_tensor_tensor(out=slot_g[:, :], in0=lose[:, :], scalar=float(ROWS), in1=sr[:, :], op0=ALU.mult, op1=ALU.add))
            v.sem_inc(S["slots_ready"], 1)
            def trip(i):
                for s in range(2):
                    n = 2 * i + s
                    v.wait_ge(S["y_psum"], n + 1)
                    v.wait_ge(y_out[s], 16 * i)
                    v.tensor_copy(ys[s], ps[0:SLOT, 6 + s, :]).then_inc(S["y_ready"], 1)

            trips(v, X * XT // 2, trip)
            def trip(i):
                for s in range(NF):
                    v.wait_ge(yg_loaded[s], 16 * (i + 1))
                    v.wait_ge(xf_loaded[s], 16 * (i + 1))
                    v.scalar_tensor_tensor(out=xf[s], in0=yg[s], scalar=rcnt[:, bass.ds(NF * i + s, 1)], in1=xf[s], op0=ALU.mult, op1=ALU.add)\
                        .then_inc(S["out_ready"], 1)

            trips(v, T // NF, trip)


_INS = ["x", "srcT", "dstT", "dst", "L0_gnn_W_src", "L0_gnn_b_src", "L0_gnn_W_dst", "L0_gnn_b_dst", "L0_gnn_W_val", "L0_gnn_b_val",
        "L0_gnn_attn_l", "L0_gnn_attn_r", "L0_mix_Wq", "L0_mix_Wk", "L0_mix_Wv", "L0_mix_Wo", "L0_mix_omega_q", "L0_mix_omega_k",
        "L0_ffn_gate_w", "L0_ffn_experts"]


def kernel(**inputs):
    import numpy as _np
    import concourse.bacc as _bacc
    from concourse import mybir as _mybir
    from concourse.bass_utils import run_bass_kernel_spmd as _run

    nc = _bacc.Bacc("TRN2", target_bir_lowering=False, num_devices=1)
    arrays, args = {}, []
    laid = dict(inputs)
    for name in ("src", "dst"):
        laid[name + "T"] = _np.ascontiguousarray(_np.asarray(inputs[name]).reshape(ET, P).T)
    for name in _INS:
        a = _np.ascontiguousarray(laid[name])
        arrays[f"in_{name}_dram"] = a
        args.append(nc.dram_tensor(f"in_{name}_dram", a.shape, _mybir.dt.from_np(a.dtype), kind="ExternalInput").ap())
    args.append(nc.dram_tensor("out_0_dram", (N, D), _mybir.dt.float32, kind="ExternalOutput").ap())
    gps_layer(nc, *args)
    r = _run(nc, [arrays], core_ids=[0])
    return r.results[0]["out_0_dram"]
```

```python
import concourse.bass as bass
from concourse import mybir
from contextlib import ExitStack

FP32 = mybir.dt.float32
INT32 = mybir.dt.int32
BF16 = mybir.dt.bfloat16
ALU = mybir.AluOpType
ACT = mybir.ActivationFunctionType
AX = mybir.AxisListType

N, D = 6250, 512
E = 100000
H, F = 8, 64
P = 125
T = N // P
ET = E // P
KC = D // 128
GT = 2 * P
G = N // GT
C = H // 2
NCH = 16
CL = E // NCH
CT = CL // P
X = 8
CAP = N // X
SLOT = 112
XT = 7
XR = SLOT * XT
ROWS = X * XR
RING = 16
LAG = 5
NF = 10
HR = 10
TOPS = 25
MIDS = ET // TOPS
TB = 4
NB = -(-CT // TB)
EPS_LN = 1e-5
EPS_PHI = 1e-8
FCLAMP = 50.0
FAR = -1.0e30
BITS = 30
SINK = 8
SCALE = F ** -0.5


class Steps:

    def __init__(self, eng, sem, passed=None):
        self.passed = passed
        self.eng, self.sem, self.base, self.n, self.i, self.per = eng, sem, 0, 0, 0, 0

    def loop(self, i, per):
        if self.per == 0:
            self.base += self.n
        self.n, self.i, self.per = 0, i, per

    def end(self, trips):
        assert self.n == self.per, (self.n, self.per)
        self.base, self.n, self.i, self.per = self.base + trips * self.per, 0, 0, 0

    def done(self, ins, apart=False):
        self.n += 1
        ins.then_inc(self.sem, 1)
        self.eng.wait_ge(self.sem, self.i * self.per + self.base + self.n)
        if apart:
            self.eng.sem_inc(self.passed, 1)


def trips(eng, n, trip):
    trip(0)
    with eng.Fori(1, n) as i:
        trip(i)


def staggered(eng, stages, steps=None, per=0):
    def step(c):
        for n, f in stages:
            if n <= c < T + n:
                f(c - n)

    for c in range(LAG):
        step(c)
    if steps:
        steps.n -= per * LAG
    with eng.Fori(LAG, T) as c:
        if steps:
            steps.loop(c, per)
        for n, f in stages:
            f(c - n)
    if steps:
        steps.end(T)
    for c in range(T, T + LAG):
        step(c)


def rev(a):
    return a[:, ::-1]


def gps_layer(nc, x, srcT, dstT, dst, W_src, b_src, W_dst, b_dst, W_val, b_val, attn_l, attn_r,
              Wq, Wk, Wv, Wo, omega_q, omega_k, gate_w, experts, out):
    ctx = ExitStack()
    with ctx:
        def sb(name, shape, dt=FP32):
            return ctx.enter_context(nc.sbuf_tensor(name, shape, dt))

        def sem(name):
            return ctx.enter_context(nc.semaphore(name))

        def dram(name, shape):
            return nc.dram_tensor(name, shape, FP32, kind="Internal").ap()

        el_tab = dram("el_tab", (N, H))
        er_tab = dram("er_tab", (N, H))
        val_tab = dram("val_tab", (N, D))
        xm_tab = dram("xm_tab", (N, D))
        x1_tab = dram("x1_tab", (N, D))
        er_starts = dram("er_starts", (E, H))
        start_tab = dram("start_tab", (P, T))
        ends_tab = dram("ends_tab", (128, 4))
        xs_tab = dram("xs_tab", (ROWS, D))
        y_tab = dram("y_tab", (ROWS + 1, D))

        R1 = sb("R1", [128, 26024])
        R2 = sb("R2", [128, 16384])
        xnT_all = R1[:, 0:KC * N].rearrange("p (k n) -> p k n", k=KC)
        scan_d = R1[:, 0:CL]
        scan_e = R1[:, CL:2 * CL]
        scan_m = R1[:, 2 * CL:3 * CL]
        scan_p = R1[:, 3 * CL:4 * CL + 1]
        acc = R1[0:P, 0:T * D].rearrange("p (t n) -> p t n", t=T)
        accd = R1[0:P, T * D:T * D + T * H].rearrange("p (t h) -> p t h", t=T)
        EW = R2[0:P, 0:ET * H].rearrange("p (t h) -> p t h", h=H)
        WS = [R2[:, 6400 + 2048 * i:8448 + 2048 * i].rearrange("p (k n) -> p k n", k=KC) for i in range(4)]
        w_vg, w_k, w_v, w_q = WS
        w_o = WS[0]
        ring = R2[0:P, 6400:6400 + RING * D].rearrange("p (s n) -> p s n", s=RING)
        ELP = R2[0:P, 0:ET * H].rearrange("p (g c h) -> p g c h", c=NCH, h=H)
        ert = R2[0:P, 8448:8448 + ET * H].rearrange("p (g c h) -> p g c h", c=NCH, h=H)
        scan_x = R2[:, 8448:8448 + CL]
        tops = R2[0:P, 14592:14592 + ET].bitcast(INT32)
        cthr = R2[0:P, 15400:15415]
        look = R2[0:P, 0:ET * H]
        exp_w = R2[:, 0:X * KC * D].rearrange("p (e k n) -> p e k n", e=X, k=KC)
        s_wsrc = R1[:, 0:2048].rearrange("p (k n) -> p k n", k=KC)
        s_wdst = R1[:, 2048:4096].rearrange("p (k n) -> p k n", k=KC)
        s_prod = R1[:, 4096:6144].rearrange("p (k n) -> p k n", k=KC)
        s_al = R1[:, 6144:6656]
        s_ar = R1[:, 6656:7168]
        s_bs = R1[:, 7168:7680]
        s_bd = R1[:, 7680:8192]

        src_i = sb("src_i", [P, ET], INT32)
        dst_i = sb("dst_i", [P, ET], INT32)
        negdst = sb("negdst", [P, ET])
        pidx = sb("pidx", [P, 2, HR], INT32)
        vidx = sb("vidx", [P, RING], INT32)
        ident = sb("ident", [128, 128])
        ones = sb("ones", [128, 128])
        halves = sb("halves", [128, 128])
        before = sb("before", [128, 128])
        omk = sb("omk", [128, 128])
        omq = sb("omq", [128, 128])
        half2 = sb("half2", [128, 2])
        bval = R2[0:P, 15616:16128]
        welr = R2[:, 16128:16192].rearrange("p (k n) -> p k n", k=KC)
        belr = R2[0:P, 16192:16208]
        gw = sb("gw", [128, KC, X])
        eps = sb("eps", [128, 1])
        kvb = R1[:, 25000:25512].rearrange("p (c n) -> p c n", c=C)
        kob = R1[:, 25512:26024].rearrange("p (c n) -> p c n", c=C)
        kvacc = sb("kvacc", [128, 2, 258])
        hi_tab = sb("hi_tab", [1, T + 1], INT32)
        work = sb("work", [128, 6400])
        pring = work[0:P, 6072:6072 + 2 * HR * H].rearrange("p (a n) -> p a n", a=2)

        def wk(a, n):
            return work[:, a:a + n]

        x_in = [wk(1024 * b, 1024).rearrange("p (j n) -> p j n", j=2) for b in range(2)]
        xn = [wk(2048 + 1024 * b, 1024).rearrange("p (j n) -> p j n", j=2) for b in range(2)]
        elr_sb = [wk(a_, 32).rearrange("p (j n) -> p j n", j=2) for a_ in (4096, 6200)]
        st6 = wk(4128, 12).rearrange("p (j n) -> p j n", j=2)
        mv = wk(4140, 4).rearrange("p (j n) -> p j n", j=2)
        std = wk(4144, 2)
        rstd = wk(4146, 2)
        xT1 = [wk(4200 + 1000 * b, 1000) for b in range(2)]
        xT13 = [a_.rearrange("p (k n) -> p k n", k=KC) for a_ in xT1]
        xT = [wk(1000 * b, 1000).rearrange("p (k n) -> p k n", k=KC) for b in range(2)]
        ts = wk(2000, 1000)
        ts3 = ts.rearrange("p (k n) -> p k n", k=KC)
        ts2 = wk(3000, 1000)
        ts23 = ts2.rearrange("p (k n) -> p k n", k=KC)
        phi = wk(4000, 1024).rearrange("p (j n) -> p j n", j=2)
        vext = wk(5024, 1032).rearrange("p (j c n) -> p j c n", j=2, c=C)
        nk = wk(6056, 16).rearrange("p (j n) -> p j n", j=2)
        vout = R2[0:P, 14592:15616].rearrange("p (j n) -> p j n", j=2)
        rq = wk(2000, 1000)
        attnT = wk(3000, 1000)
        attnT3 = attnT.rearrange("p (k n) -> p k n", k=KC)
        xm = wk(0, 1024).rearrange("p (j n) -> p j n", j=2)
        cand = wk(0, 64).rearrange("p (k c) -> p k c", k=NCH)
        candv = wk(64, 32)
        ends = wk(96, 4)
        cfl = wk(100, 2)
        onehot = [wk(2112 + 128 * s, P) for s in range(2)]
        absd = [wk(2368 + 128 * s, P) for s in range(2)]
        iota_f = wk(2624, P)
        one125 = wk(2750, 1)
        zrow = wk(2752, D)
        thr = wk(3266, 1)
        cmp = wk(3272, ET // 2)
        cnt = wk(3674, 2)
        xmb = wk(0, 4 * D).rearrange("p (j n) -> p j n", j=4)
        xn2b = wk(5500, D)
        mvs = wk(6020, 4).rearrange("p (j n) -> p j n", j=2)
        stds = wk(6024, 2)
        den = wk(4150, H)
        xT6 = wk(4200, 500)
        xT63 = xT6.rearrange("p (k n) -> p k n", k=KC)
        gK, gA, gB, sel, win, pre, cnt_t, keep = [work[0:P, a_:a_ + T * X]
                                                  for a_ in (5100, 2600, 2200, 3000, 3400, 4000, 4400, 5500)]
        slot_s = sb("slot_s", [P, T], INT32)
        slot_g = sb("slot_g", [P, T], INT32)
        rcnt = sb("rcnt", [P, T])
        noff = sb("noff", [P, T])
        tb = [sb(f"tb{i}", [P, T]) for i in range(3)]
        sm = sb("sm", [P, 8, X])
        smi = sb("smi", [P, 4, X], INT32)
        xs = [work[0:SLOT, D * s:D * (s + 1)] for s in range(2)]
        xsT = [work[:, 1024 + 448 * s:1472 + 448 * s] for s in range(2)]
        ys = [work[0:SLOT, 2048 + D * s:2560 + D * s] for s in range(2)]
        yg = [R2[0:P, D * s:D * (s + 1)] for s in range(NF)]
        x1_all = acc

        ps = ctx.enter_context(nc.psum_tensor("ps", [128, 8, 512], FP32))

        def two(b, rows=128):
            return ps[0:rows, b:b + 2, 0:500]

        def chunk(b, k, lo, n, rows=128):
            return ps[0:rows, b + k // 2, (k % 2) * GT + lo:(k % 2) * GT + lo + n]

        names = """elr_params omega_params xn_ready xnT_ready elr_ready idx_loaded val_params proj_params consts_ready
            row_ready er_back elr_psum v_psum vg_read lq_psum wo_loaded er_started ert_loaded xm_ready wo_psum
            attn_ready dst_loaded ends_ready ends_written segmax_ready sp_passed xm_back x1_ready x1_kept
            xn2_kept block_summed experts_loaded scattered y_ready xs_transposed x1_back out_ready out_done
            pool_step pool_passed tops_loaded node_ready looked_up starts_moved chunk_er logits_kept iota_ready
            zero_written weights_kept tile_free vals_ready slots_ready onehot_free acc_free welr_ready
            xn_transposed v_ones fq_read kt_psum lq_read vg_psum v_copied fk_read fk_psum kt_copied qt_psum
            phi_ready kv_added kv_psum qt_copied fq_psum kvb_ready phiq_ready qkv_psum seg_t_psum negdst_ready
            f_psum cmp_ready hi_psum weights_ready weights_psum hi_ready msg_ready onehot_ready xT6_ready
            gate_read gate_psum xn2_ready xn2_transposed col_ready col_psum cnt_ready cnt_psum pre_ready
            pre_psum xsT_copied y_psum act_step var_ready std_ready kexp_done qexp_done el_t_copied dst_read
            er_t_copied shifted dve_step dve_passed dve_misc""".split()
        S = {n: sem(n) for n in names}
        x_loaded = [sem(f"x_loaded{b}") for b in range(2)]
        elr_written = [sem(f"elr_written{b}") for b in range(2)]
        xT_kept = [sem(f"xT_kept{b}") for b in range(2)]
        xT_loaded = [sem(f"xT_loaded{b}") for b in range(2)]
        val_written = [sem(f"val_written{j}") for j in range(2)]
        xm_in = [sem(f"xm_in{j}") for j in range(2)]
        xm_out = [sem(f"xm_out{j}") for j in range(2)]
        logits_in = [sem(f"logits_in{h_}") for h_ in range(2)]
        gathered = [sem(f"gathered{q}") for q in range(4)]
        xs_loaded = [sem(f"xs_loaded{s}") for s in range(2)]
        y_out = [sem(f"y_out{s}") for s in range(2)]
        yg_loaded = [sem(f"yg_loaded{s}") for s in range(NF // 2)]

        def rows(tab, t):
            return tab[bass.ds(t * P, P), :]

        block = ctx.enter_context(nc.Block())

        @block.sync
        def _(sp_):
            eng = sp_
            wv4 = "(k p) n -> p k n"
            eng.dma_start(s_wsrc, W_src.rearrange(wv4, p=128)).then_inc(S["elr_params"], 16)
            eng.dma_start(s_wdst, W_dst.rearrange(wv4, p=128)).then_inc(S["elr_params"], 16)
            for d_, a_ in ((s_al, attn_l.rearrange("h f -> (h f)")), (s_ar, attn_r.rearrange("h f -> (h f)")),
                           (s_bs, b_src), (s_bd, b_dst)):
                eng.dma_start(d_, a_.partition_broadcast(128)).then_inc(S["elr_params"], 16)
            with nc.allow_non_contiguous_dma(reason="small"):
                eng.dma_start(gw[:, :, :], gate_w.rearrange("o (k p) e -> p (o k) e", p=128)).then_inc(S["omega_params"], 16)
            def load_x(g, b, used):
                if used is not None:
                    eng.wait_ge(S["xn_ready"], used)
                for j in range(2):
                    eng.dma_start(x_in[b][0:P, j, :], rows(x, 2 * g + j)).then_inc(x_loaded[b], 16)

            def keep_xT(g, b):
                eng.wait_ge(S["xnT_ready"], g + 1)
                eng.dma_start(xnT_all[:, :, bass.ds(g * GT, GT)], xT13[b]).then_inc(xT_kept[b], 16)

            el_v = el_tab.rearrange("(t p) h -> p t h", p=P)
            er_v = er_tab.rearrange("(t p) h -> p t h", p=P)

            def store_logits(g, b):
                eng.wait_ge(S["elr_ready"], g + 1)
                eng.dma_start(el_v[:, bass.ds(2 * g, 2), :], elr_sb[b][0:P, :, 0:H]).then_inc(elr_written[b], 16)
                eng.dma_start(er_v[:, bass.ds(2 * g, 2), :], elr_sb[b][0:P, :, H:2 * H]).then_inc(elr_written[b], 16)

            load_x(0, 0, None)

            def trip(i):
                load_x(2 * i + 1, 1, 4 * i)
                keep_xT(2 * i, 0)
                if not isinstance(i, int):
                    store_logits(2 * i - 2, 0)
                load_x(2 * i + 2, 0, 4 * i + 2)
                keep_xT(2 * i + 1, 1)
                if not isinstance(i, int):
                    store_logits(2 * i - 1, 1)

            trip(0)
            eng.dma_start(src_i[:, :], srcT).then_inc(S["idx_loaded"], 16)
            eng.dma_start(dst_i[:, :], dstT).then_inc(S["idx_loaded"], 16)
            eng.dma_start(bval[:, :], b_val.partition_broadcast(P)).then_inc(S["val_params"], 16)
            eng.dma_start(w_vg, W_val.rearrange(wv4, p=128)).then_inc(S["val_params"], 16)
            for w_, m_ in ((w_k, Wk), (w_v, Wv), (w_q, Wq)):
                eng.dma_start(w_, m_.rearrange(wv4, p=128)).then_inc(S["proj_params"], 16)
            eng.wait_ge(S["consts_ready"], 1)
            for o_, m_ in ((omk, omega_k), (omq, omega_q)):
                for r in range(2):
                    eng.dma_start(o_[F * r:F * r + F, F * r:F * r + F], m_).then_inc(S["omega_params"], 16)
            with nc.allow_non_contiguous_dma(reason="32-byte rows"):
                with eng.Fori(1, G // 2) as i:
                    trip(i)
                keep_xT(G - 1, 0)
                for g in range(G - 3, G):
                    store_logits(g, g % 2)
                for b in range(2):
                    eng.wait_ge(elr_written[b], 32 * (G // 2 + 1 - b))
                eng.wait_ge(S["row_ready"], 4)
                eng.dma_start(look[:, 0:T * H].rearrange("p (t h) -> p t h", h=H), er_v).then_inc(S["er_back"], 16)
                eng.dma_start(smi[0:NCH, 0, 0:1], dst.rearrange("(c r) -> c r", c=NCH)[:, 0:1]).then_inc(S["er_back"], 16)
            for b in range(2):
                eng.wait_ge(xT_kept[b], 16 * (G // 2 + 1 - b))
            eng.wait_ge(S["elr_psum"], G)
            for b in range(2):
                eng.wait_ge(elr_written[b], 32 * (G // 2 + 1 - b))

            def load_xT(g, b, used):
                if used is not None:
                    eng.wait_ge(S["v_psum"], used)
                eng.dma_start(xT[b], xnT_all[:, :, bass.ds(g * GT, GT)]).then_inc(xT_loaded[b], 16)

            def store_val(g, b):
                for j in range(2):
                    eng.wait_ge(S["vg_read"], 2 * g + j + 1)
                    eng.dma_start(rows(val_tab, 2 * g + j), vout[:, j, :]).then_inc(val_written[j], 16)

            load_xT(0, 0, None)
            def trip(i):
                load_xT(2 * i + 1, 1, 4 * i)
                store_val(2 * i, 0)
                load_xT(2 * i + 2, 0, 4 * i + 2)
                store_val(2 * i + 1, 1)

            trips(eng, G // 2, trip)
            store_val(G - 1, 0)
            eng.wait_ge(S["lq_psum"], G)
            eng.dma_start(w_o, Wo.rearrange(wv4, p=128)).then_inc(S["wo_loaded"], 16)
            for j in range(2):
                eng.wait_ge(val_written[j], 16 * G)
            eng.wait_ge(S["er_started"], 16 * (T + 1))
            eng.dma_start(R2[0:P, 8448:8448 + ET * H], er_starts.rearrange("(p r) h -> p (r h)", p=P)).then_inc(S["ert_loaded"], 16)
            def trip(g):
                for j in range(2):
                    eng.wait_ge(xm_out[j], 16 * g)
                    eng.dma_start(xm[0:P, j, :], rows(x, 2 * g + j)).then_inc(xm_in[j], 16)
                for j in range(2):
                    eng.wait_ge(S["xm_ready"], 2 * g + j + 1)
                    eng.dma_start(rows(xm_tab, 2 * g + j), xm[0:P, j, :]).then_inc(xm_out[j], 16)

            trips(eng, G, trip)
            for j in range(2):
                eng.wait_ge(xm_out[j], 16 * G)
            eng.wait_ge(S["wo_psum"], 2 * G)
            eng.wait_ge(S["attn_ready"], G)
            for c in range(NCH):
                eng.dma_start(scan_m[H * c:H * c + H, :].bitcast(INT32), dst[c * CL:(c + 1) * CL].partition_broadcast(H)).then_inc(S["dst_loaded"], 16)
            eng.wait_ge(S["ends_ready"], 1)
            eng.dma_start(ends_tab, ends).then_inc(S["ends_written"], 16)
            eng.wait_ge(S["ends_written"], 16)
            with nc.allow_non_contiguous_dma(reason="ends of chunks"):
                for c in range(NCH):
                    eng.dma_start(cand[H * c:H * c + H, :, :], ends_tab.rearrange("(k h) c -> h k c", h=H)).then_inc(S["ends_written"], 16)
            eng.wait_ge(S["segmax_ready"], 1)

            def hold(sem_, value):
                eng.wait_ge(sem_, value)
                eng.sem_inc(S["sp_passed"], 1)

            def load_xm(t):
                hold(S["xm_back"], 16 * t)
                eng.dma_start(xmb[0:P, bass.ds(t % 4, 1), :].rearrange("p a n -> p (a n)"), rows(xm_tab, t)).then_inc(S["xm_back"], 16)

            def store_x1(t):
                hold(S["x1_ready"], t + 1)
                hold(S["x1_kept"], 16 * t)
                eng.dma_start(rows(x1_tab, t), xmb[0:P, bass.ds(t % 4, 1), :].rearrange("p a n -> p (a n)")).then_inc(S["x1_kept"], 16)

            for t in range(4):
                load_xm(t)
            for t in range(3):
                store_x1(t)
            with eng.Fori(4, T) as t:
                hold(S["x1_kept"], 16 * (t - 3))
                hold(S["xn2_kept"], t - 3)
                load_xm(t)
                store_x1(t - 1)
            store_x1(T - 1)
            eng.wait_ge(S["block_summed"], T)
            for e_ in range(X):
                eng.dma_start(exp_w[:, e_, :, :], experts[e_].rearrange(wv4, p=128)).then_inc(S["experts_loaded"], 16)
            eng.wait_ge(S["scattered"], 16 * T)
            eng.wait_ge(S["x1_kept"], 16 * T)

            def load_xs(n, s):
                eng.dma_start(xs[s], xs_tab[bass.ds(n * SLOT, SLOT), :]).then_inc(xs_loaded[s], 16)

            def store_y(n, s):
                eng.wait_ge(S["y_ready"], n + 1)
                eng.dma_start(y_tab[bass.ds(n * SLOT, SLOT), :], ys[s]).then_inc(y_out[s], 16)

            NT = X * XT
            for s in range(2):
                load_xs(s, s)

            def trip(i, back=True):
                for s in range(2):
                    n = 2 * i + s
                    eng.wait_ge(S["xs_transposed"], n + 1)
                    load_xs(n + 2, s)
                    if back:
                        eng.dma_start(x1_all[:, bass.ds(n, 1), :].rearrange("p a n -> p (a n)"), rows(x1_tab, n)).then_inc(S["x1_back"], 16)
                    store_y(n, s)

            trips(eng, T // 2, trip)
            with eng.Fori(T // 2, NT // 2 - 1) as i:
                trip(i, False)
            for s in range(2):
                store_y(NT - 2 + s, s)
            def trip(t):
                eng.wait_ge(S["out_ready"], t + 1)
                eng.dma_start(rows(out, t), x1_all[:, bass.ds(t, 1), :].rearrange("p a n -> p (a n)")).then_inc(S["out_done"], 16)

            trips(eng, T, trip)
            eng.wait_ge(S["out_done"], 16 * T)

        @block.gpsimd
        def _(eng):
            st = Steps(eng, S["pool_step"], S["pool_passed"])
            for t_ in (omk, omq):
                st.done(eng.memset(t_[:, :], 0.0))
            eng.sem_inc(S["consts_ready"], 1)
            for t_ in (ident, halves, half2, before):
                st.done(eng.memset(t_[:, :], 0.0))
            for t_ in (kvb, kob, kvacc):
                st.done(eng.memset(t_[:, :, :], 0.0))
            st.done(eng.memset(eps[:, :], EPS_LN))
            st.done(eng.memset(ones[:, :], 1.0))
            st.done(eng.affine_select(out=ident[:, :], in_=ident[:, :], compare_op=ALU.not_equal, fill=1.0, base=0,
                                      pattern=[[-1, 128]], channel_multiplier=1))
            st.done(eng.affine_select(out=before[:, :], in_=before[:, :], compare_op=ALU.is_ge, fill=1.0, base=0,
                                      pattern=[[-1, 128]], channel_multiplier=1))
            for r in range(2):
                st.done(eng.memset(halves[F * r:F * r + F, F * r:F * r + F], 1.0))
                st.done(eng.memset(half2[F * r:F * r + F, r:r + 1], 1.0))
            eng.sem_inc(S["consts_ready"], 1)
            node, start, nxt = noff[:, :], tb[0][:, :], tb[1][:, :]
            eng.dma_start(tops, dstT[0, :].partition_broadcast(P)).then_inc(S["tops_loaded"], 16)
            st.done(eng.memset(look, 0.0))
            eng.dma_start(er_starts.rearrange("(p r) h -> p (r h)", p=P), look).then_inc(S["tops_loaded"], 16)
            st.done(eng.iota(node, pattern=[[P, T]], base=0, channel_multiplier=1, allow_small_or_imprecise_dtypes=True))
            st.done(eng.memset(nxt, float(E)))
            st.done(eng.iota(cthr, pattern=[[CL, NCH - 1]], base=CL, channel_multiplier=0, allow_small_or_imprecise_dtypes=True))
            eng.sem_inc(S["node_ready"], 1)
            for n, tab_ in enumerate((dstT[0:1, :].rearrange("o (a b) -> (o a) b", b=MIDS), dst.rearrange("(a b) -> a b", b=P))):
                w_ = tab_.shape[1]
                eng.wait_ge(S["row_ready"], n + 1)
                for t in range(T):
                    eng.indirect_dma_start(out=look[:, w_ * t:w_ * t + w_].bitcast(INT32), out_offset=None, in_=tab_,
                                           in_offset=bass.IndirectOffsetOnAxis(ap=slot_g[:, t:t + 1], axis=0)).then_inc(S["looked_up"], 16)
            eng.wait_ge(S["row_ready"], 3)
            eng.dma_start(start_tab, start).then_inc(S["starts_moved"], 16)
            eng.wait_ge(S["starts_moved"], 16)
            eng.dma_start(nxt[0:P - 1, :], start_tab[1:P, :]).then_inc(S["starts_moved"], 16)
            eng.dma_start(nxt[P - 1:P, 0:T - 1], start_tab[0:1, 1:T]).then_inc(S["starts_moved"], 16)
            eng.wait_ge(S["row_ready"], 4)
            eng.wait_ge(S["er_back"], 32)
            eng.indirect_dma_start(out=sm[0:NCH, 0, :], out_offset=None, in_=er_tab[:, :],
                                   in_offset=bass.IndirectOffsetOnAxis(ap=smi[0:NCH, 0, 0:1], axis=0)).then_inc(S["chunk_er"], 16)
            for t in range(T):
                eng.indirect_dma_start(out=er_starts[:, :], out_offset=bass.IndirectOffsetOnAxis(ap=slot_s[:, t:t + 1], axis=0),
                                       in_=look[:, t * H:t * H + H], in_offset=None,
                                       bounds_check=E - 1, oob_is_err=False).then_inc(S["er_started"], 16)
            eng.wait_ge(S["chunk_er"], 16)
            eng.wait_ge(S["er_started"], 16 * T)
            eng.dma_start(er_starts[0:NCH, :], sm[0:NCH, 0, :]).then_inc(S["er_started"], 16)
            eng.wait_ge(S["idx_loaded"], 32)
            for b in range(2):
                eng.wait_ge(xT_kept[b], 16 * (G // 2 + 1 - b))
            BC = CT // HR

            def gather_logits(i, b):
                h_ = b % 2
                st.done(eng.tensor_copy(pidx[:, h_, :], src_i[:, bass.ds((2 * BC * i + b) * HR, HR)]), apart=True)
                for q in range(HR):
                    eng.indirect_dma_start(out=pring[:, h_, q * H:q * H + H], out_offset=None, in_=el_tab[:, :],
                                           in_offset=bass.IndirectOffsetOnAxis(ap=pidx[:, h_, q:q + 1], axis=0))\
                        .then_inc(logits_in[h_], 16)

            def keep_logits(i, b):
                g0 = (b % BC) * HR
                st.done(eng.tensor_copy(ELP[:, g0:g0 + HR, bass.ds(2 * i + b // BC, 1), :].rearrange("p g c h -> p g (c h)"),
                                        pring[:, b % 2, :].rearrange("p (g h) -> p g h", h=H)))

            def trip(i):
                for b in range(2 * BC):
                    if b >= 2 or not isinstance(i, int):
                        eng.wait_ge(logits_in[b % 2], 16 * HR * (BC * i + b // 2))
                        keep_logits(i, b - 2)
                    gather_logits(i, b)

            trip(0)
            st.n -= 4 * BC
            with eng.Fori(1, NCH // 2) as i:
                st.loop(i, 4 * BC)
                trip(i)
            st.end(NCH // 2)
            for b in range(2):
                eng.wait_ge(logits_in[b], 16 * HR * BC * NCH // 2)
                keep_logits(NCH // 2, b - 2)
            eng.sem_inc(S["logits_kept"], 1)
            eng.wait_ge(S["xm_ready"], 2 * G)
            eng.wait_ge(S["wo_psum"], 2 * G)
            st.done(eng.iota(iota_f[0:P, :], pattern=[[1, P]], base=0, channel_multiplier=0, allow_small_or_imprecise_dtypes=True))
            st.done(eng.memset(one125[:, :], float(P)))
            st.done(eng.memset(zrow[:, :], 0.0))
            st.done(eng.iota(thr[:, :], pattern=[[0, 1]], base=P, channel_multiplier=P, allow_small_or_imprecise_dtypes=True))
            st.done(eng.iota(sm[:, 4, :], pattern=[[XR, X]], base=0, channel_multiplier=0, allow_small_or_imprecise_dtypes=True))
            st.done(eng.iota(noff[:, :], pattern=[[P, T]], base=ROWS, channel_multiplier=1, allow_small_or_imprecise_dtypes=True))
            eng.sem_inc(S["iota_ready"], 1)
            zb = zrow[0:P, :]
            eng.dma_start(xs_tab[N:ROWS, :], zb[0:ROWS - N, :]).then_inc(S["zero_written"], 16)
            eng.dma_start(y_tab[ROWS:ROWS + 1, :], zb[0:1, :]).then_inc(S["zero_written"], 16)
            for j in range(2):
                eng.wait_ge(val_written[j], 16 * G)
            def quarter(i, q):
                eng.wait_ge(S["tile_free"], RING * i + 4 * q + 4)
                st.done(eng.tensor_copy(vidx[:, 4 * q:4 * q + 4], src_i[:, bass.ds(RING * i + 4 * q, 4)]), apart=True)
                for s in range(4 * q, 4 * q + 4):
                    eng.indirect_dma_start(out=ring[:, s, :], out_offset=None, in_=val_tab[:, :],
                                           in_offset=bass.IndirectOffsetOnAxis(ap=vidx[:, s:s + 1], axis=0))\
                        .then_inc(gathered[q], 16)

            def report(q, n):
                eng.wait_ge(gathered[q], 64 * n)
                eng.sem_inc(S["vals_ready"], 4)

            def trip(i):
                eng.dma_start(rows(xs_tab, i), zb).then_inc(S["zero_written"], 16)
                st.loop(i, 4)
                for q in range(4):
                    quarter(i, q)
                    if isinstance(i, int) and q == 0:
                        eng.wait_ge(S["weights_kept"], NB)
                        report(0, 1)
                    elif isinstance(i, int) and q == 1:
                        pass
                    elif q >= 1:
                        report(q - 1, i + 1)
                    elif not isinstance(i, int):
                        report(3, i)

            assert ET // RING == T
            trips(eng, T, trip)
            st.end(T)
            report(3, ET // RING)
            eng.wait_ge(S["zero_written"], 16 * (T + 2))
            eng.wait_ge(S["slots_ready"], 1)
            eng.wait_ge(S["xn2_kept"], T)
            for t in range(T):
                eng.indirect_dma_start(out=xs_tab[:, :], out_offset=bass.IndirectOffsetOnAxis(ap=slot_s[:, t:t + 1], axis=0),
                                       in_=acc[:, t, :], in_offset=None,
                                       bounds_check=ROWS - 1, oob_is_err=False).then_inc(S["scattered"], 16)
            NT = X * XT
            for s in range(2):
                eng.wait_ge(y_out[s], 16 * (NT // 2))
            for t in range(T):
                if t >= NF:
                    eng.wait_ge(S["out_ready"], t - NF + 1)
                eng.indirect_dma_start(out=yg[t % NF], out_offset=None, in_=y_tab[:, :],
                                       in_offset=bass.IndirectOffsetOnAxis(ap=slot_g[:, t:t + 1], axis=0))\
                    .then_inc(yg_loaded[t % NF // 2], 16)

        @block.tensor
        def _(pe):
            pe.sem_inc(S["tile_free"], RING)
            pe.sem_inc(S["onehot_free"], 2)
            pe.sem_inc(S["acc_free"], 2)

            def mm(o, l, r, start=True, stop=True):
                return pe.matmul(o, l, r, start=start, stop=stop)

            pe.wait_ge(S["consts_ready"], 2)
            pe.wait_ge(S["welr_ready"], 1)
            def logits(g, b):
                pe.wait_ge(S["xnT_ready"], g + 1)
                pe.wait_ge(S["elr_ready"], g)
                for j in range(2):
                    for k in range(KC):
                        last = mm(ps[0:P, 4, 16 * j:16 * j + 16], xT13[b][:, k, j * P:j * P + P], welr[:, k, :], k == 0, k == KC - 1)
                last.then_inc(S["elr_psum"], 1)

            def turn(g, b, copied):
                if copied is not None:
                    pe.wait_ge(S["xnT_ready"], copied)
                for j in range(2):
                    pe.wait_ge(S["xn_ready"], 2 * g + j + 1)
                    for k in range(KC):
                        last = pe.transpose(chunk(2 * b, k, j * P, P), xn[b][0:P, j, 128 * k:128 * k + 128], ident[0:P, 0:P])
                    last.then_inc(S["xn_transposed"], 1)

            turn(0, 0, None)
            turn(1, 1, None)
            logits(0, 0)

            def trip(i):
                turn(2 * i, 0, 2 * i - 1)
                logits(2 * i - 1, 1)
                turn(2 * i + 1, 1, 2 * i)
                logits(2 * i, 0)

            with pe.Fori(1, G // 2) as i:
                trip(i)
            turn(G - 1, 0, G - 2)
            logits(G - 2, 1)
            logits(G - 1, 0)
            pe.wait_ge(S["val_params"], 32)
            pe.wait_ge(S["proj_params"], 48)
            pe.wait_ge(S["omega_params"], 80)
            pe.wait_ge(S["elr_ready"], G)
            pe.wait_ge(S["v_ones"], 1)

            def group(g, b, u):
                pe.wait_ge(xT_loaded[b], 16 * (u + 1))
                pe.wait_ge(S["fq_read"], g)
                for c in range(C):
                    for k in range(KC):
                        last = mm(chunk(0, c, 0, GT), w_k[:, k, 128 * c:128 * c + 128], xT[b][:, k, :], k == 0, k == KC - 1)
                last.then_inc(S["kt_psum"], 1)
                pe.wait_ge(S["lq_read"], g)

                def values(j):
                    pe.wait_ge(S["vg_read"], 2 * g + j)
                    for k in range(KC):
                        last = mm(ps[0:P, 2, :], xT[b][:, k, j * P:j * P + P], w_vg[:, k, :], k == 0, k == KC - 1)
                    last.then_inc(S["vg_psum"], 1)
                    pe.wait_ge(S["v_copied"], 2 * g + j)
                    for k in range(KC):
                        last = mm(ps[0:P, 3, :], xT[b][:, k, j * P:j * P + P], w_v[:, k, :], k == 0, k == KC - 1)
                    last.then_inc(S["v_psum"], 1)

                def scores_k(j):
                    pe.wait_ge(S["fk_read"], 4 * g + 2 * j)
                    for c in range(C):
                        mm(ps[0:P, 4, 128 * c:128 * c + 128], ts3[:, c, j * P:j * P + P], omk[:, :])
                        last = mm(ps[0:P, 7, 2 * c:2 * c + 2], ts23[:, c, j * P:j * P + P], half2[:, :])
                    last.then_inc(S["fk_psum"], 1)

                values(0)
                pe.wait_ge(S["kt_copied"], 2 * g + 2)
                scores_k(0)
                scores_k(1)
                for c in range(C):
                    for k in range(KC):
                        last = mm(chunk(0, c, 0, GT), w_q[:, k, 128 * c:128 * c + 128], xT[b][:, k, :], k == 0, k == KC - 1)
                last.then_inc(S["qt_psum"], 1)
                values(1)
                pe.wait_ge(S["phi_ready"], 2 * g + 2)
                pe.wait_ge(S["v_copied"], 2 * g + 2)
                pe.wait_ge(S["kv_added"], g)
                for c in range(C):
                    for j in range(2):
                        last = mm(ps[:, 5 + c // 2, 129 * (c % 2):129 * (c % 2) + 129], phi[0:P, j, 128 * c:128 * c + 128],
                                  vext[0:P, j, c, :], j == 0, j == 1)
                last.then_inc(S["kv_psum"], 1)
                pe.wait_ge(S["qt_copied"], 2 * g + 2)
                for c in range(C):
                    last = mm(chunk(0, c, 0, GT), omq[:, :], ts3[:, c, :])
                last.then_inc(S["fq_psum"], 1)
                pe.wait_ge(S["vg_read"], 2 * g + 2)
                for c in range(C):
                    last = mm(chunk(2, c, 0, GT), halves[:, :], ts23[:, c, :])
                last.then_inc(S["lq_psum"], 1)
                

            def trip(i):
                group(2 * i, 0, i)
                group(2 * i + 1, 1, i)

            trips(pe, G // 2, trip)
            group(G - 1, 0, G // 2)
            pe.wait_ge(S["kvb_ready"], 8)
            pe.wait_ge(S["phiq_ready"], G)
            pe.wait_ge(S["wo_loaded"], 16)
            def attention(g):
                pe.wait_ge(S["attn_ready"], g)
                for c in range(C):
                    mm(chunk(0, c, 0, GT), kvb[:, c, :], xnT_all[:, c, bass.ds(g * GT, GT)])
                for c in range(C):
                    last = mm(chunk(2, c, 0, GT), kob[:, c, :], xnT_all[:, c, bass.ds(g * GT, GT)])
                last.then_inc(S["qkv_psum"], 1)

            def output(g):
                pe.wait_ge(S["attn_ready"], g + 1)
                pe.wait_ge(S["xm_ready"], 2 * g)
                for j in range(2):
                    for c in range(C):
                        last = mm(ps[0:P, 4 + j, :], attnT3[:, c, j * P:j * P + P], w_o[:, c, :], c == 0, c == C - 1)
                    last.then_inc(S["wo_psum"], 1)

            attention(0)
            attention(1)
            output(0)
            with pe.Fori(2, G) as g:
                attention(g)
                output(g - 1)
            output(G - 1)
            pe.wait_ge(S["logits_kept"], 1)
            pe.wait_ge(S["ert_loaded"], 16)
            for first, tab_, b0, copied in ((0, ELP, 0, "el_t_copied"), (NB, ert, 2, "er_t_copied")):
                for k in range(NB):
                    if k >= 2:
                        pe.wait_ge(S[copied], k - 1)
                    for g in range(TB * k, min(TB * k + TB, CT)):
                        last = pe.transpose(ps[:, b0 + k % 2, (g % TB) * P:(g % TB) * P + P], tab_[:, g, :, :].rearrange("p c h -> p (c h)"),
                                            ident[0:P, 0:P])
                    last.then_inc(S["seg_t_psum"], 1)
            pe.wait_ge(S["negdst_ready"], 1)
            pe.wait_ge(S["iota_ready"], 1)
            mm(ps[0:T, 4, 0:ET // 2], ones[0:1, 0:T], negdst[0:1, :].rearrange("p (u s) -> p u s", s=2)[:, :, 0]).then_inc(S["f_psum"], 1)
            pe.wait_ge(S["cmp_ready"], 1)
            mm(ps[0:1, 5, 0:T], cnt[0:T, 1:2], ident[0:T, 0:T]).then_inc(S["hi_psum"], 1)
            for k in range(NB):
                pe.wait_ge(S["weights_ready"], k + 1)
                if k >= 2:
                    pe.wait_ge(S["weights_kept"], k - 1)
                for g in range(TB * k, min(TB * k + TB, CT)):
                    last = pe.transpose(ps[0:P, 6 + k % 2, (g % TB) * 128:(g % TB) * 128 + 128], scan_x[:, g * P:g * P + P], ident[:, :])
                last.then_inc(S["weights_psum"], 1)
            pe.wait_ge(S["hi_ready"], 1)
            pe.wait_ge(S["weights_kept"], NB)
            zb16 = zrow.bitcast(BF16)

            def block_sums(c):
                lo = pe.value_load(hi_tab[0:1, bass.ds(c, 1)], min_val=0, max_val=ET // 2 - 1)
                hi = pe.value_load(hi_tab[0:1, bass.ds(c + 1, 1)], min_val=0, max_val=ET // 2 - 1)
                a = c % 2
                pe.wait_ge(S["acc_free"], c + 1)
                o512 = ps[0:P, bass.ds(2 * a, 1), :].rearrange("p a n -> p (a n)")
                o8 = ps[0:P, bass.ds(2 * a + 1, 1), 0:H].rearrange("p a n -> p (a n)")
                mm(o512, zb16[0:1, 0:P], zb16[0:1, 0:D], True, False)
                mm(o8, zb16[0:1, 0:P], zb16[0:1, 0:H], True, False)

                def tiles(u, lastone):
                    for s in range(2):
                        pe.wait_ge(S["msg_ready"], 2 * u + s + 1)
                        pe.wait_ge(S["onehot_ready"], 2 * (u + c) + s + 1)
                        stop = lastone and s == 1
                        m = mm(o512, onehot[s][0:P, :], ring[:, bass.ds((2 * u + s) % RING, 1), :].rearrange("p a n -> p (a n)"), False, stop)
                        if not lastone:
                            m.then_inc(S["tile_free"], 1)
                        mm(o8, onehot[s][0:P, :], EW[:, bass.ds(2 * u + s, 1), :].rearrange("p a n -> p (a n)"), False, stop)\
                            .then_inc(S["onehot_free"], 1)

                with pe.If(lo < hi):
                    with pe.Fori(lo, hi) as u:
                        tiles(u, False)
                tiles(hi, True)

            def gates(t):
                pe.wait_ge(S["xT6_ready"], t + 1)
                pe.wait_ge(S["gate_read"], t)
                for k in range(KC):
                    last = mm(ps[0:P, 6, 0:X], xT63[:, k, :], gw[:, k, :], k == 0, k == KC - 1)
                last.then_inc(S["gate_psum"], 1)

            def turn_xn2(t):
                pe.wait_ge(S["xn2_ready"], t + 1)
                pe.wait_ge(S["xT6_ready"], t)
                for k in range(KC):
                    last = pe.transpose(ps[:, 4, k * P:k * P + P], xn2b[0:P, 128 * k:128 * k + 128], ident[0:P, 0:P])
                last.then_inc(S["xn2_transposed"], 1)

            staggered(pe, ((0, block_sums), (4, gates), (3, turn_xn2)))
            def trip(i):
                pe.wait_ge(S["col_ready"], i + 1)
                mm(ps[0:P, 0, 0:X], ones[0:P, 0:P], sm[:, 0, :]).then_inc(S["col_psum"], 1)

            trips(pe, SINK, trip)
            def trip(i):
                pe.wait_ge(S["cnt_ready"], i + 1)
                mm(ps[0:P, 1, 0:X], ones[0:P, 0:P], sm[:, 1, :]).then_inc(S["cnt_psum"], 1)

            trips(pe, BITS + 1, trip)
            for r in range(2):
                pe.wait_ge(S["pre_ready"], r + 1)
                mm(ps[0:P, 2, 0:T * X], before[0:P, 0:P], win)
                mm(ps[0:P, 3, 0:T * X], ones[0:P, 0:P], win).then_inc(S["pre_psum"], 1)
            pe.wait_ge(S["experts_loaded"], 16 * X)

            def turn_xs(n, s):
                pe.wait_ge(xs_loaded[s], 16 * (n // 2 + 1))
                pe.wait_ge(S["xsT_copied"], max(n - 1, 0) if isinstance(n, int) else n - 1)
                for k in range(KC):
                    last = pe.transpose(ps[:, 4 + s, k * SLOT:k * SLOT + SLOT], xs[s][:, 128 * k:128 * k + 128], ident[0:SLOT, 0:SLOT])
                last.then_inc(S["xs_transposed"], 1)

            def product(n, s, e_):
                pe.wait_ge(S["xsT_copied"], n + 1)
                pe.wait_ge(S["y_ready"], max(n - 1, 0) if isinstance(n, int) else n - 1)
                for k in range(KC):
                    last = mm(ps[0:SLOT, 6 + s, :], xsT[s][:, k * SLOT:k * SLOT + SLOT],
                              exp_w[:, bass.ds(e_, 1), k, :].rearrange("p a n -> p (a n)"), k == 0, k == KC - 1)
                last.then_inc(S["y_psum"], 1)

            def trip(i, final=False):
                for m in range(2 * XT):
                    if not (final and m == 2 * XT - 1):
                        turn_xs(i * 2 * XT + m + 1, (m + 1) % 2)
                    product(i * 2 * XT + m, m % 2, 2 * i + m // XT)

            turn_xs(0, 0)
            trip(0)
            with pe.Fori(1, X // 2 - 1) as i:
                trip(i)
            trip(X // 2 - 1, True)

        @block.scalar
        def _(act):
            st = Steps(act, S["act_step"])
            fn = act.activation
            act.wait_ge(S["consts_ready"], 2)

            def deviation(g):
                for j in range(2):
                    act.wait_ge(S["var_ready"], 2 * g + j + 1)
                    fn(std[0:P, j:j + 1], mv[0:P, j, 1:2], ACT.Sqrt, bias=eps[0:P, :]).then_inc(S["std_ready"], 1)

            def copy_xT(g, b, kept):
                act.wait_ge(S["xn_transposed"], 2 * g + 2)
                if kept is not None:
                    act.wait_ge(xT_kept[b], 16 * kept)
                    act.wait_ge(S["elr_psum"], 2 * kept - 1 + b)
                fn(xT1[b], two(2 * b), ACT.Copy).then_inc(S["xnT_ready"], 1)

            deviation(0)
            copy_xT(0, 0, None)
            deviation(1)
            copy_xT(1, 1, None)
            deviation(2)
            with act.Fori(1, G // 2) as i:
                copy_xT(2 * i, 0, i)
                deviation(2 * i + 1)
                copy_xT(2 * i + 1, 1, i)
                deviation(2 * i + 2)
            copy_xT(G - 1, 0, G // 2)
            for b in range(2):
                act.wait_ge(elr_written[b], 32 * (G // 2 + 1 - b))
            for b in range(2):
                act.wait_ge(xT_kept[b], 16 * (G // 2 + 1 - b))

            def group(g):
                act.wait_ge(S["kt_psum"], g + 1)
                act.wait_ge(S["phiq_ready"], g)
                fn(ts, two(0), ACT.Copy, scale=SCALE).then_inc(S["kt_copied"], 1)
                fn(ts2, two(0), ACT.Square, scale=SCALE).then_inc(S["kt_copied"], 1)

                def v_copy(j):
                    act.wait_ge(S["v_psum"], 2 * g + j + 1)
                    act.wait_ge(S["kv_psum"], g)
                    fn(vext[0:P, j, :, 0:128], ps[0:P, 3, :].rearrange("p (c n) -> p c n", c=C), ACT.Copy).then_inc(S["v_copied"], 1)

                v_copy(0)
                for j in range(2):
                    act.wait_ge(S["fk_read"], 4 * g + 2 * j + 2)
                    fn(phi[0:P, j, :], phi[0:P, j, :], ACT.Exp).then_inc(S["kexp_done"], 1)
                    fn(nk[0:P, j, :], nk[0:P, j, :], ACT.Exp, scale=-0.5).then_inc(S["kexp_done"], 1)
                act.wait_ge(S["qt_psum"], g + 1)
                act.wait_ge(S["fk_psum"], 2 * g + 2)
                fn(ts, two(0), ACT.Copy, scale=SCALE).then_inc(S["qt_copied"], 1)
                fn(ts2, two(0), ACT.Square, scale=SCALE).then_inc(S["qt_copied"], 1)
                v_copy(1)
                act.wait_ge(S["fq_read"], g + 1)
                fn(ts, ts, ACT.Exp).then_inc(S["qexp_done"], 1)
                act.wait_ge(S["lq_read"], g + 1)
                fn(ts2, ts2, ACT.Exp, scale=-0.5).then_inc(S["qexp_done"], 1)

            def trip(g):
                group(g)

            trips(act, G, trip)
            for k in range(NB):
                act.wait_ge(S["seg_t_psum"], k + 1)
                n = min(TB, CT - TB * k) * P
                fn(scan_e[:, TB * k * P:TB * k * P + n], ps[:, k % 2, 0:n], ACT.Copy).then_inc(S["el_t_copied"], 1)
            act.wait_ge(S["dst_read"], 1)
            m3 = scan_m.rearrange("q (p g) -> q g p", g=CT)
            for k in range(NB):
                act.wait_ge(S["seg_t_psum"], NB + k + 1)
                n = min(TB, CT - TB * k)
                fn(m3[:, TB * k:TB * k + n, :], ps[:, 2 + k % 2, 0:n * P].rearrange("q (g p) -> q g p", g=n), ACT.Copy).then_inc(S["er_t_copied"], 1)
            for k in range(NB):
                act.wait_ge(S["shifted"], k + 1)
                x_ = scan_x[:, TB * k * P:min(TB * k * P + TB * P, CL)]
                fn(x_, x_, ACT.Exp).then_inc(S["weights_ready"], 1)
            act.wait_ge(S["iota_ready"], 1)
            act.wait_ge(S["hi_ready"], 1)

            def onehots(u, c):
                for s in range(2):
                    k2 = 2 * (u + c) + s
                    fn(absd[s][0:P, :], iota_f[0:P, :], ACT.Abs, bias=negdst[:, bass.ds(2 * u + s, 1)]).then_inc(S["act_step"], 1)
                    act.wait_ge(S["act_step"], k2 + c + 1)
                    act.wait_ge(S["onehot_free"], k2 + 1)
                    fn(onehot[s][0:P, :], absd[s][0:P, :], ACT.Relu, scale=-1.0, bias=1.0).then_inc(S["onehot_ready"], 1)

            def copy_xn2(t):
                act.wait_ge(S["xn2_transposed"], t + 1)
                act.wait_ge(S["gate_psum"], t)
                fn(xT6, ps[:, 4, 0:500], ACT.Copy).then_inc(S["xT6_ready"], 1)

            def block_onehots(c):
                lo = act.value_load(hi_tab[0:1, bass.ds(c, 1)], min_val=0, max_val=ET // 2 - 1)
                hi = act.value_load(hi_tab[0:1, bass.ds(c + 1, 1)], min_val=0, max_val=ET // 2 - 1)
                with act.If(lo < hi):
                    with act.Fori(lo, hi) as u:
                        onehots(u + 1, c)
                if not isinstance(c, int) or c >= 4:
                    copy_xn2(c - 4)
                fn(iota_f[0:P, :], iota_f[0:P, :], ACT.Identity, bias=one125[0:P, :]).then_inc(S["act_step"], 1)
                act.wait_ge(S["act_step"], 2 * (hi + c) + 2 + c + 1)
                if not isinstance(c, int) or c < T - 1:
                    onehots(hi, c + 1)
                return hi

            def copy_sums(c, hi):
                act.wait_ge(S["onehot_free"], 2 * (hi + c) + 2 + 2)
                a = c % 2
                fn(acc[:, bass.ds(c, 1), :].rearrange("p a n -> p (a n)"), ps[0:P, bass.ds(2 * a, 1), :].rearrange("p a n -> p (a n)"), ACT.Copy)\
                    .then_inc(S["block_summed"], 1)
                fn(accd[:, bass.ds(c, 1), :].rearrange("p a n -> p (a n)"), ps[0:P, bass.ds(2 * a + 1, 1), 0:H].rearrange("p a n -> p (a n)"), ACT.Copy)\
                    .then_inc(S["acc_free"], 1)

            def deviation2(t):
                act.wait_ge(S["var_ready"], T + t + 1)
                fn(stds[0:P, bass.ds(t % 2, 1)], mvs[0:P, bass.ds(t % 2, 1), 1:2].rearrange("p a n -> p (a n)"), ACT.Sqrt, bias=eps[0:P, :])\
                    .then_inc(S["std_ready"], 1)

            onehots(0, 0)
            def last_xn2(c):
                if isinstance(c, int) and c >= T - 4:
                    copy_xn2(c)

            staggered(act, ((0, lambda c: copy_sums(c, block_onehots(c))), (2, deviation2), (4, last_xn2)))
            def trip(i):
                for s in range(2):
                    n = 2 * i + s
                    act.wait_ge(S["xs_transposed"], n + 1)
                    act.wait_ge(S["y_psum"], max(n - 1, 0) if isinstance(n, int) else n - 1)
                    fn(xsT[s], ps[:, 4 + s, 0:KC * SLOT], ACT.Copy).then_inc(S["xsT_copied"], 1)

            trips(act, X * XT // 2, trip)

        @block.vector
        def _(v):
            st = Steps(v, S["dve_step"], S["dve_passed"])
            v.wait_ge(S["elr_params"], 96)
            for w_, a_, o_ in ((s_wsrc, s_al, 0), (s_wdst, s_ar, H)):
                st.done(v.tensor_tensor(out=s_prod, in0=w_, in1=a_.unsqueeze(1).to_broadcast([128, KC, D]), op=ALU.mult))
                st.done(v.tensor_reduce(out=welr[:, :, o_:o_ + H], in_=s_prod.rearrange("p k (h f) -> p k h f", h=H), axis=AX.X, op=ALU.add))
            for b_, a_, o_ in ((s_bs, s_al, 0), (s_bd, s_ar, H)):
                st.done(v.tensor_tensor(out=b_, in0=b_, in1=a_, op=ALU.mult))
                st.done(v.tensor_reduce(out=belr[:, o_:o_ + H], in_=b_[0:P, :].rearrange("p (h f) -> p h f", h=H), axis=AX.X, op=ALU.add))
            v.sem_inc(S["welr_ready"], 1)
            def norm(g, b, u):
                v.wait_ge(x_loaded[b], 32 * (u + 1))
                for j in range(2):
                    st.done(v.bn_stats(out=st6[0:P, j, :], in_=x_in[b][0:P, j, :]), apart=True)
                    v.bn_aggr(out=mv[0:P, j, :], in_=st6[0:P, j, :]).then_inc(S["var_ready"], 1)
                for j in range(2):
                    v.wait_ge(S["std_ready"], 2 * g + j + 1)
                    st.done(v.reciprocal(rstd[0:P, j:j + 1], std[0:P, j:j + 1]))
                    v.tensor_scalar(xn[b][0:P, j, :], x_in[b][0:P, j, :], mv[0:P, j, 0:1], rstd[0:P, j:j + 1], ALU.subtract, ALU.mult)\
                        .then_inc(S["xn_ready"], 1)

            def add_bias(g, b, u):
                v.wait_ge(S["elr_psum"], g + 1)
                v.wait_ge(elr_written[b], 32 * u)
                v.tensor_tensor(out=elr_sb[b][0:P, :, :], in0=ps[0:P, 4, 0:32].rearrange("p (j n) -> p j n", j=2),
                                in1=belr[:, :].unsqueeze(1).to_broadcast([P, 2, 2 * H]), op=ALU.add).then_inc(S["elr_ready"], 1)

            def trip(i):
                st.loop(i, 8)
                for b in range(2):
                    v.wait_ge(S["xn_transposed"], 4 * i)
                    norm(2 * i + b, b, i)
                    if not isinstance(i, int) or i > 0:
                        add_bias(2 * i + b - 2, b, i - 1)

            node, start, nxt, tmp = noff[:, :], tb[0][:, :], tb[1][:, :], tb[2][:, :]

            def below(row, n, out_):
                l3 = look[:, 0:T * n].rearrange("p (t n) -> p t n", n=n)
                st.done(v.tensor_tensor(out=l3, in0=row, in1=node.unsqueeze(2).to_broadcast([P, T, n]), op=ALU.is_lt))
                st.done(v.tensor_reduce(out=out_, in_=l3, axis=AX.X, op=ALU.add))

            def look_at(n):
                return look[:, 0:T * n].bitcast(INT32).rearrange("p (t n) -> p t n", n=n)

            def first_top():
                v.wait_ge(S["node_ready"], 1)
                v.wait_ge(S["tops_loaded"], 32)
                top_row = tops.rearrange("p (a b) -> p a b", b=MIDS)[:, :, 0]
                below(top_row.unsqueeze(1).to_broadcast([P, T, TOPS]), TOPS, start)
                st.done(v.tensor_scalar(start, start, -1.0, 0.0, ALU.add, ALU.max))
                st.done(v.tensor_copy(slot_g[:, :], start))
                v.sem_inc(S["row_ready"], 1)

            def first_tile():
                v.wait_ge(S["looked_up"], 16 * T)
                below(look_at(MIDS), MIDS, tmp)
                st.done(v.scalar_tensor_tensor(out=start, in0=start, scalar=float(MIDS), in1=tmp, op0=ALU.mult, op1=ALU.add))
                st.done(v.tensor_scalar(start, start, -1.0, 0.0, ALU.add, ALU.max))
                st.done(v.tensor_copy(slot_g[:, :], start))
                v.sem_inc(S["row_ready"], 1)

            def first_edge():
                v.wait_ge(S["looked_up"], 32 * T)
                below(look_at(P), P, tmp)
                st.done(v.scalar_tensor_tensor(out=start, in0=start, scalar=float(P), in1=tmp, op0=ALU.mult, op1=ALU.add))
                v.sem_inc(S["row_ready"], 1)

            def first_row():
                c3 = look[:, 0:T * (NCH - 1)].rearrange("p (t n) -> p t n", n=NCH - 1)
                st.done(v.tensor_tensor(out=c3, in0=start.unsqueeze(2).to_broadcast([P, T, NCH - 1]),
                                        in1=cthr.unsqueeze(1).to_broadcast([P, T, NCH - 1]), op=ALU.is_ge))
                st.done(v.tensor_reduce(out=tmp, in_=c3, axis=AX.X, op=ALU.add))
                v.wait_ge(S["starts_moved"], 48)
                st.done(v.tensor_tensor(out=nxt, in0=start, in1=nxt, op=ALU.is_lt))
                st.done(v.tensor_scalar(start, start, float(NCH), float(-E), ALU.mult, ALU.add))
                st.done(v.scalar_tensor_tensor(out=start, in0=tmp, scalar=float(1 - NCH * CL), in1=start, op0=ALU.mult, op1=ALU.add))
                st.done(v.tensor_tensor(out=start, in0=start, in1=nxt, op=ALU.mult))
                st.done(v.tensor_scalar(slot_s[:, :], start, float(E), None, ALU.add))
                v.sem_inc(S["row_ready"], 1)

            trip(0)
            st.end(1)
            first_top()
            st.n -= 8
            trip(1)
            st.end(2)
            for step_, lo_, hi_ in ((first_tile, 2, 6), (first_edge, 6, 11), (first_row, 11, G // 2)):
                st.n -= 8 * lo_
                with v.Fori(lo_, hi_) as i:
                    trip(i)
                st.end(hi_)
                step_()
            v.wait_ge(S["xn_transposed"], 2 * G - 2)
            norm(G - 1, 0, G // 2)
            for g in range(G - 3, G):
                add_bias(g, g % 2, g // 2)
            for b in range(2):
                v.wait_ge(elr_written[b], 32 * (G // 2 + 1 - b))
            v.wait_ge(S["elr_psum"], G)
            for b in range(2):
                v.wait_ge(xT_kept[b], 16 * (G // 2 + 1 - b))
            v.memset(vext[:, :, :, 128:129], 1.0).then_inc(S["v_ones"], 1)
            v.wait_ge(S["val_params"], 32)
            v.wait_ge(S["consts_ready"], 2)

            def trip(g):
                st.loop(g, 3)

                def values(j):
                    v.wait_ge(S["vg_psum"], 2 * g + j + 1)
                    v.wait_ge(val_written[j], 16 * g)
                    v.tensor_tensor(out=vout[:, j, :], in0=ps[0:P, 2, :], in1=bval[:, :], op=ALU.add).then_inc(S["vg_read"], 1)

                values(0)
                for j in range(2):
                    v.wait_ge(S["fk_psum"], 2 * g + j + 1)
                    v.wait_ge(S["kv_psum"], g)
                    v.tensor_scalar(phi[0:P, j, :], ps[0:P, 4, :], FCLAMP, None, ALU.min).then_inc(S["fk_read"], 1)
                    v.tensor_scalar(nk[0:P, j, :], ps[0:P, 7, 0:H], EPS_PHI * EPS_PHI, None, ALU.max).then_inc(S["fk_read"], 1)
                for j in range(2):
                    v.wait_ge(S["kexp_done"], 4 * g + 2 * j + 2)
                    st.done(v.tensor_scalar(nk[0:P, j, :], nk[0:P, j, :], EPS_PHI, None, ALU.max))
                    p3 = phi[0:P, j, :].rearrange("p (h m) -> p h m", h=H)
                    v.tensor_tensor(out=p3, in0=p3, in1=nk[0:P, j, :].unsqueeze(2).to_broadcast([P, H, F]), op=ALU.mult)\
                        .then_inc(S["phi_ready"], 1)
                values(1)
                v.wait_ge(S["kv_psum"], g + 1)
                v.wait_ge(S["kv_added"], g)
                v.tensor_tensor(out=kvacc[:, :, :], in0=kvacc[:, :, :], in1=ps[:, 5:7, 0:258], op=ALU.add).then_inc(S["kv_added"], 1)
                v.wait_ge(S["fq_psum"], g + 1)
                v.tensor_scalar(ts, two(0), FCLAMP, None, ALU.min).then_inc(S["fq_read"], 1)
                v.wait_ge(S["lq_psum"], g + 1)
                v.tensor_scalar(ts2, two(2), EPS_PHI * EPS_PHI, None, ALU.max).then_inc(S["lq_read"], 1)
                v.wait_ge(S["qexp_done"], 2 * g + 2)
                st.done(v.tensor_scalar(ts2, ts2, EPS_PHI, None, ALU.max))
                v.tensor_tensor(out=xnT_all[:, :, bass.ds(g * GT, GT)], in0=ts3, in1=ts23, op=ALU.mult).then_inc(S["phiq_ready"], 1)

            trips(v, G, trip)
            st.end(G)
            v.wait_ge(S["kv_added"], G)
            kv4 = kvacc[:, :, :].rearrange("p b (q n) -> p (b q) n", n=129)
            for r in range(2):
                h_ = slice(F * r, F * r + F)
                for c in range(C):
                    v.tensor_copy(kob[h_, c, h_], kv4[h_, c, 128:129].to_broadcast([F, F])).then_inc(S["dve_misc"], 1)
                v.tensor_copy(kvb[h_, :, h_], kv4[h_, :, h_]).then_inc(S["kvb_ready"], 4)
            v.wait_ge(S["dve_misc"], 2 * C)
            def divide(g):
                v.wait_ge(S["qkv_psum"], g + 1)
                st.done(v.reciprocal(rq.rearrange("p (b n) -> p b n", b=2), two(2)))
                v.wait_ge(S["wo_psum"], 2 * g)
                v.tensor_tensor(out=attnT.rearrange("p (b n) -> p b n", b=2), in0=two(0), in1=rq.rearrange("p (b n) -> p b n", b=2), op=ALU.mult)\
                    .then_inc(S["attn_ready"], 1)

            def add_x(g):
                for j in range(2):
                    v.wait_ge(S["wo_psum"], 2 * g + j + 1)
                    v.wait_ge(xm_in[j], 16 * (g + 1))
                    v.tensor_tensor(out=xm[0:P, j, :], in0=xm[0:P, j, :], in1=ps[0:P, 4 + j, :], op=ALU.add).then_inc(S["xm_ready"], 1)

            divide(0)
            st.n -= 1
            with v.Fori(1, G) as g:
                st.loop(g, 1)
                divide(g)
                add_x(g - 1)
            st.end(G)
            add_x(G - 1)
            v.wait_ge(S["idx_loaded"], 32)
            st.done(v.tensor_scalar(negdst[:, :], dst_i[:, :], -1.0, None, ALU.mult))
            v.sem_inc(S["negdst_ready"], 1)
            v.wait_ge(S["dst_loaded"], 16 * NCH)
            st.done(v.tensor_copy(scan_d, scan_m.bitcast(INT32)))
            v.sem_inc(S["dst_read"], 1)
            st.done(v.tensor_tensor(out=scan_p[:, 1:CL], in0=scan_d[:, 1:CL], in1=scan_d[:, 0:CL - 1], op=ALU.is_equal))
            st.done(v.memset(scan_p[:, 0:1], 0.0))
            v.wait_ge(S["er_t_copied"], NB)
            st.done(v.tensor_tensor_scan(out=scan_x, data0=scan_p[:, 0:CL], data1=scan_m, initial=0.0, op0=ALU.mult, op1=ALU.add))
            v.wait_ge(S["el_t_copied"], NB)
            st.done(v.tensor_tensor(out=scan_x, in0=scan_x, in1=scan_e, op=ALU.add))
            st.done(v.scalar_tensor_tensor(out=scan_x, in0=scan_x, scalar=0.2, in1=scan_x, op0=ALU.mult, op1=ALU.max))
            st.done(v.tensor_scalar(scan_p[:, 0:CL], scan_p[:, 0:CL], -1.0, -FAR, ALU.add, ALU.mult))
            st.done(v.memset(scan_p[:, CL:CL + 1], FAR))
            st.done(v.tensor_tensor_scan(out=scan_m, data0=scan_p[:, 0:CL], data1=scan_x, initial=FAR, op0=ALU.add, op1=ALU.max))
            st.done(v.tensor_tensor_scan(out=rev(scan_e), data0=rev(scan_p[:, 1:CL + 1]), data1=rev(scan_m), initial=FAR, op0=ALU.add, op1=ALU.max))
            for c_, s_ in ((0, scan_d[:, 0:1]), (1, scan_e[:, 0:1]), (2, scan_d[:, CL - 1:CL]), (3, scan_m[:, CL - 1:CL])):
                st.done(v.tensor_copy(ends[:, c_:c_ + 1], s_))
            v.sem_inc(S["ends_ready"], 1)
            v.wait_ge(S["f_psum"], 1)
            v.wait_ge(S["iota_ready"], 1)
            st.done(v.tensor_scalar(cmp[0:T, :], ps[0:T, 4, 0:ET // 2], thr[0:T, :], 0.0, ALU.add, ALU.is_gt))
            st.done(v.tensor_reduce(out=cnt[0:T, 0:1], in_=cmp[0:T, :], axis=AX.X, op=ALU.add))
            st.done(v.tensor_scalar(cnt[0:T, 1:2], cnt[0:T, 0:1], -1.0, 0.0, ALU.add, ALU.max))
            v.sem_inc(S["cmp_ready"], 1)
            v.wait_ge(S["hi_psum"], 1)
            st.done(v.memset(hi_tab[0:1, 0:1], 0))
            st.done(v.tensor_copy(hi_tab[0:1, 1:T + 1], ps[0:1, 5, 0:T]))
            v.sem_inc(S["hi_ready"], 1)
            v.wait_ge(S["ends_written"], 16 * (NCH + 1))
            cd = cand.rearrange("p k (a b) -> p (k a) b", b=2)
            for side, edge in ((0, scan_d[:, 0:1]), (1, scan_d[:, CL - 1:CL])):
                st.done(v.tensor_scalar(candv, cd[:, :, 0], edge, FAR, ALU.not_equal, ALU.mult))
                st.done(v.tensor_tensor(out=candv, in0=candv, in1=cd[:, :, 1], op=ALU.add))
                st.done(v.tensor_reduce(out=cfl[:, side:side + 1], in_=candv, axis=AX.X, op=ALU.max))
                st.done(v.tensor_scalar(scan_m, scan_d, edge, FAR, ALU.not_equal, ALU.mult))
                st.done(v.scalar_tensor_tensor(out=scan_e, in0=scan_m, scalar=cfl[:, side:side + 1], in1=scan_e, op0=ALU.add, op1=ALU.max))
            v.sem_inc(S["segmax_ready"], 1)
            for k in range(NB):
                lo_, hi_ = TB * k * P, min(TB * k * P + TB * P, CL)
                v.tensor_tensor(out=scan_x[:, lo_:hi_], in0=scan_x[:, lo_:hi_], in1=scan_e[:, lo_:hi_], op=ALU.subtract)\
                    .then_inc(S["shifted"], 1)
            ew_v = EW.rearrange("p (c g) h -> p g c h", c=NCH)
            for k in range(NB):
                v.wait_ge(S["weights_psum"], k + 1)
                n = min(TB, CT - TB * k)
                v.tensor_copy(ew_v[:, TB * k:TB * k + n, :, :], ps[0:P, 6 + k % 2, 0:n * 128].rearrange("p (g c h) -> p g c h", g=n, c=NCH))\
                    .then_inc(S["weights_kept"], 1)
            v.wait_ge(S["weights_kept"], NB)

            def messages(u):
                for s in range(2):
                    v.wait_ge(S["vals_ready"], 2 * u + s + 1)
                    r3 = ring[:, bass.ds((2 * u + s) % RING, 1), :].rearrange("p a (h f) -> p (a h) f", h=H)
                    w_ = EW[:, bass.ds(2 * u + s, 1), :].rearrange("p a h -> p (a h)").unsqueeze(2).to_broadcast([P, H, F])
                    v.tensor_tensor(out=r3, in0=r3, in1=w_, op=ALU.mult).then_inc(S["msg_ready"], 1)

            def block_messages(c):
                lo = v.value_load(hi_tab[0:1, bass.ds(c, 1)], min_val=0, max_val=ET // 2 - 1)
                hi = v.value_load(hi_tab[0:1, bass.ds(c + 1, 1)], min_val=0, max_val=ET // 2 - 1)
                with v.If(lo < hi):
                    with v.Fori(lo, hi) as u:
                        messages(u + 1)

            def read_gates(t):
                v.wait_ge(S["gate_psum"], t + 1)
                v.tensor_scalar(gK[:, bass.ds(t * X, X)], ps[0:P, 6, 0:X], 1e-10, None, ALU.max).then_inc(S["gate_read"], 1)

            def slot_of(t):
                return xmb[0:P, bass.ds(t % 4, 1), :].rearrange("p a n -> p (a n)")

            def norm_x1(t):
                v.wait_ge(S["xn2_kept"], t)
                v.wait_ge(S["std_ready"], T + t + 1)
                st.done(v.reciprocal(rstd[0:P, 0:1], stds[0:P, bass.ds(t % 2, 1)]))
                v.wait_ge(S["xn2_transposed"], t)
                mean = mvs[0:P, bass.ds(t % 2, 1), 0:1].rearrange("p a n -> p (a n)")
                v.tensor_scalar(xn2b[0:P, :], slot_of(t), mean, rstd[0:P, 0:1], ALU.subtract, ALU.mult).then_inc(S["xn2_ready"], 1)
                v.tensor_scalar(acc[:, bass.ds(t, 1), :].rearrange("p a n -> p (a n)"), slot_of(t), mean, rstd[0:P, 0:1],
                                ALU.subtract, ALU.mult).then_inc(S["xn2_kept"], 1)

            def make_x1(t):
                v.wait_ge(S["acc_free"], t + 3)
                a1 = acc[:, bass.ds(t, 1), :].rearrange("p a n -> p (a n)")
                st.done(v.tensor_scalar(den[0:P, :], accd[:, bass.ds(t, 1), :].rearrange("p a n -> p (a n)"), 1e-16, None, ALU.max))
                st.done(v.reciprocal(den[0:P, :], den[0:P, :]))
                v.wait_ge(S["block_summed"], t + 1)
                a3 = a1.rearrange("p (h f) -> p h f", h=H)
                st.done(v.tensor_tensor(out=a3, in0=a3, in1=den[0:P, :].unsqueeze(2).to_broadcast([P, H, F]), op=ALU.mult))
                v.wait_ge(S["xm_back"], 16 * (t + 1))
                v.tensor_tensor(out=slot_of(t), in0=slot_of(t), in1=a1, op=ALU.add).then_inc(S["x1_ready"], 1)
                v.wait_ge(S["x1_ready"], t + 1)
                v.sem_inc(S["dve_passed"], 1)
                st.done(v.bn_stats(out=st6[0:P, 0, :], in_=slot_of(t)), apart=True)
                st.done(v.bn_aggr(out=mv[0:P, 0, :], in_=st6[0:P, 0, :]))
                v.tensor_copy(mvs[0:P, bass.ds(t % 2, 1), :].rearrange("p a n -> p (a n)"), mv[0:P, 0, :]).then_inc(S["var_ready"], 1)

            messages(0)
            staggered(v, ((0, block_messages), (3, norm_x1), (1, make_x1), (5, read_gates)), st, 6)
            def te(a_):
                return a_.rearrange("p (t e) -> p t e", e=X)

            def et(a_):
                return a_.rearrange("p (t e) -> p e t", e=X)

            def over_t(a_):
                return a_.unsqueeze(1).to_broadcast([P, T, X])

            def over_e(a_):
                return a_.unsqueeze(2).to_broadcast([P, T, X])

            sa, sr, lose = tb[0], tb[1], tb[2]
            v.wait_ge(S["gate_read"], T)
            st.done(v.memset(sa[:, :], 1.0))
            def trip(i):
                st.loop(i, 6)
                st.done(v.tensor_tensor(out=te(gB), in0=te(gK), in1=over_e(sa[:, :]), op=ALU.mult))
                st.done(v.tensor_reduce(out=sm[:, 0, :], in_=et(gB), axis=AX.X, op=ALU.add))
                v.sem_inc(S["col_ready"], 1)
                v.wait_ge(S["col_psum"], i + 1)
                st.done(v.reciprocal(sm[:, 2, :], ps[0:P, 0, 0:X]))
                st.done(v.tensor_tensor(out=te(gB), in0=te(gK), in1=over_t(sm[:, 2, :]), op=ALU.mult))
                st.done(v.tensor_reduce(out=sr[:, :], in_=te(gB), axis=AX.X, op=ALU.add))
                st.done(v.reciprocal(sa[:, :], sr[:, :]))

            trips(v, SINK, trip)
            st.end(SINK)
            st.done(v.tensor_tensor(out=te(gA), in0=te(gB), in1=over_e(sa[:, :]), op=ALU.mult))
            cur, bit, trial, hit = [smi[:, q, :] for q in range(4)]
            st.done(v.memset(cur, 0))
            st.done(v.memset(bit, 1 << (BITS - 1)))
            def trip(i):
                st.loop(i, 6)
                st.done(v.tensor_tensor(out=trial, in0=cur, in1=bit, op=ALU.bitwise_or))
                st.done(v.tensor_tensor(out=te(sel), in0=te(gA), in1=over_t(trial.bitcast(FP32)), op=ALU.is_ge))
                st.done(v.tensor_reduce(out=sm[:, 1, :], in_=et(sel), axis=AX.X, op=ALU.add))
                v.sem_inc(S["cnt_ready"], 1)
                v.wait_ge(S["cnt_psum"], i + 1)
                st.done(v.scalar_tensor_tensor(out=hit, in0=ps[0:P, 1, 0:X], scalar=float(CAP), in1=bit, op0=ALU.is_ge, op1=ALU.mult))
                st.done(v.tensor_tensor(out=cur, in0=cur, in1=hit, op=ALU.bitwise_or))
                st.done(v.tensor_scalar(bit, bit, 0.5, None, ALU.mult))

            trips(v, BITS, trip)
            st.end(BITS)
            cf = over_t(cur.bitcast(FP32))
            st.done(v.tensor_tensor(out=te(sel), in0=te(gA), in1=cf, op=ALU.is_gt))
            st.done(v.tensor_tensor(out=te(win), in0=te(gA), in1=cf, op=ALU.is_equal))
            st.done(v.tensor_reduce(out=sm[:, 1, :], in_=et(sel), axis=AX.X, op=ALU.add))
            v.sem_inc(S["cnt_ready"], 1)
            v.wait_ge(S["cnt_psum"], BITS + 1)
            st.done(v.tensor_scalar(sm[:, 3, :], ps[0:P, 1, 0:X], -1.0, float(CAP), ALU.mult, ALU.add))
            keep3 = keep.rearrange("p (e t) -> p e t", e=X)
            st.done(v.memset(keep, 1.0))
            st.done(v.memset(keep3[:, :, 0:1], 0.0))

            def rank(r):
                v.sem_inc(S["pre_ready"], 1)
                v.wait_ge(S["pre_psum"], r + 1)
                ct3 = cnt_t.rearrange("p (e t) -> p e t", e=X)
                st.done(v.tensor_copy(ct3, et(ps[0:P, 3, 0:T * X])))
                st.done(v.tensor_tensor_scan(out=gB, data0=keep, data1=cnt_t, initial=0.0, op0=ALU.mult, op1=ALU.add))
                st.done(v.tensor_tensor(out=gB, in0=gB, in1=cnt_t, op=ALU.subtract))
                st.done(v.tensor_tensor(out=te(pre), in0=te(ps[0:P, 2, 0:T * X]), in1=gB.rearrange("p (e t) -> p t e", e=X), op=ALU.add))

            rank(0)
            st.done(v.tensor_tensor(out=te(pre), in0=te(pre), in1=over_t(sm[:, 3, :]), op=ALU.is_lt))
            st.done(v.tensor_tensor(out=pre, in0=pre, in1=win, op=ALU.mult))
            st.done(v.tensor_tensor(out=sel, in0=sel, in1=pre, op=ALU.add))
            st.done(v.tensor_reduce(out=rcnt[:, :], in_=te(sel), axis=AX.X, op=ALU.add))
            st.done(v.tensor_scalar(rcnt[:, :], rcnt[:, :], 1.0, None, ALU.add))
            st.done(v.reciprocal(rcnt[:, :], rcnt[:, :]))
            st.done(v.scalar_tensor_tensor(out=win, in0=gA, scalar=0.5, in1=sel, op0=ALU.is_gt, op1=ALU.mult))
            st.done(v.tensor_reduce(out=sr[:, :], in_=te(win), axis=AX.X, op=ALU.add))
            st.done(v.tensor_scalar(sa[:, :], sr[:, :], 1.5, None, ALU.is_lt))
            st.done(v.tensor_tensor(out=te(win), in0=te(win), in1=over_e(sa[:, :]), op=ALU.mult))
            st.done(v.tensor_tensor(out=sr[:, :], in0=sr[:, :], in1=sa[:, :], op=ALU.mult))
            st.done(v.tensor_scalar(lose[:, :], sr[:, :], -1.0, 1.0, ALU.mult, ALU.add))
            rank(1)
            st.done(v.tensor_tensor(out=te(pre), in0=te(pre), in1=over_t(sm[:, 4, :]), op=ALU.add))
            st.done(v.tensor_tensor(out=pre, in0=pre, in1=win, op=ALU.mult))
            st.done(v.tensor_reduce(out=sr[:, :], in_=te(pre), axis=AX.X, op=ALU.add))
            st.done(v.tensor_tensor(out=noff[:, :], in0=noff[:, :], in1=lose[:, :], op=ALU.mult))
            st.done(v.tensor_tensor(out=slot_s[:, :], in0=noff[:, :], in1=sr[:, :], op=ALU.add))
            st.done(v.scalar_tensor_tensor(out=slot_g[:, :], in0=lose[:, :], scalar=float(ROWS), in1=sr[:, :], op0=ALU.mult, op1=ALU.add))
            v.sem_inc(S["slots_ready"], 1)
            def trip(i):
                for s in range(2):
                    n = 2 * i + s
                    v.wait_ge(S["y_psum"], n + 1)
                    v.wait_ge(y_out[s], 16 * i)
                    v.tensor_copy(ys[s], ps[0:SLOT, 6 + s, :]).then_inc(S["y_ready"], 1)

            trips(v, X * XT // 2, trip)
            v.wait_ge(S["x1_back"], 16 * T)

            def trip(i):
                for s in range(NF):
                    v.wait_ge(yg_loaded[s // 2], 32 * (i + 1))
                    x_ = x1_all[:, bass.ds(NF * i + s, 1), :].rearrange("p a n -> p (a n)")
                    v.scalar_tensor_tensor(out=x_, in0=yg[s], scalar=rcnt[:, bass.ds(NF * i + s, 1)], in1=x_, op0=ALU.mult, op1=ALU.add)\
                        .then_inc(S["out_ready"], 1)

            trips(v, T // NF, trip)


_INS = ["x", "srcT", "dstT", "dst", "L0_gnn_W_src", "L0_gnn_b_src", "L0_gnn_W_dst", "L0_gnn_b_dst", "L0_gnn_W_val", "L0_gnn_b_val",
        "L0_gnn_attn_l", "L0_gnn_attn_r", "L0_mix_Wq", "L0_mix_Wk", "L0_mix_Wv", "L0_mix_Wo", "L0_mix_omega_q", "L0_mix_omega_k",
        "L0_ffn_gate_w", "L0_ffn_experts"]


def kernel(**inputs):
    import numpy as _np
    import concourse.bacc as _bacc
    from concourse import mybir as _mybir
    from concourse.bass_utils import run_bass_kernel_spmd as _run

    nc = _bacc.Bacc("TRN2", target_bir_lowering=False, num_devices=1)
    arrays, args = {}, []
    laid = dict(inputs)
    for name in ("src", "dst"):
        laid[name + "T"] = _np.ascontiguousarray(_np.asarray(inputs[name]).reshape(ET, P).T)
    for name in _INS:
        a = _np.ascontiguousarray(laid[name])
        arrays[f"in_{name}_dram"] = a
        args.append(nc.dram_tensor(f"in_{name}_dram", a.shape, _mybir.dt.from_np(a.dtype), kind="ExternalInput").ap())
    args.append(nc.dram_tensor("out_0_dram", (N, D), _mybir.dt.float32, kind="ExternalOutput").ap())
    gps_layer(nc, *args)
    r = _run(nc, [arrays], core_ids=[0])
    return r.results[0]["out_0_dram"]
```
